# Optimizing a Trainium2 kernel written in Bass

```python
import numpy as np
import jax
import jax.numpy as jnp

def _softmax(x, axis=-1):
    return jax.nn.softmax(x, axis=axis)

def _gelu(x):
    return jax.nn.gelu(x, approximate=True)

def _silu(x):
    return jax.nn.silu(x)

def _sigmoid(x):
    return jax.nn.sigmoid(x)

def _layernorm(x, axis=-1, eps=1e-05):
    m = jnp.mean(x, axis=axis, keepdims=True)
    v = jnp.var(x, axis=axis, keepdims=True)
    return (x - m) / jnp.sqrt(v + eps)

def _scatter_add(tgt, idx, src, axis=0):
    return tgt.at[idx].add(src)

def _segment_sum(src, seg, n):
    return jax.ops.segment_sum(src, seg, n)
kernel_name = 'mk_flamingo_gated_d2_seqx_r8_99fe43'

def setup_inputs(seed: int=0):
    np.random.seed(seed)
    _w = jnp.asarray

    def _rec_inputs():
        import jax
        import jax.numpy as jnp
        _rk = jax.random.key(seed)
        x = -0.0005207 + 1.001 * jax.random.normal(jax.random.fold_in(_rk, 1), (4, 512, 128), jnp.float32)
        _lenS = 512 - jax.random.randint(jax.random.fold_in(_rk, 7), (4,), 0, max(1, 512 // 4) + 1, jnp.int32)
        _lenS2 = 77 - jax.random.randint(jax.random.fold_in(_rk, 8), (4,), 0, max(1, 77 // 4) + 1, jnp.int32)
        _ctx_1024P = jax.random.normal(jax.random.fold_in(_rk, 11), (4, 16, 128), jnp.float32)
        _ctx_1024c = jax.random.dirichlet(jax.random.fold_in(_rk, 511), 0.3 * jnp.ones((16,), jnp.float32), (4, 77))
        _ctx_1024t = jnp.einsum('bsk,bkd->bsd', _ctx_1024c, _ctx_1024P)
        _ctx_1024t = _ctx_1024t * jax.lax.rsqrt(jnp.mean(jnp.square(_ctx_1024t)) + 1e-12) * 0.953939
        ctx_1024 = 4.13588e-05 + 0.999923 * (_ctx_1024t + 0.3 * jax.random.normal(jax.random.fold_in(_rk, 611), (4, 77, 128), jnp.float32))
        _g = jax.random.normal(jax.random.fold_in(_rk, 9001), (2, 2), jnp.float32)
        _g = jnp.sign(_g) * jnp.maximum(jnp.abs(_g), 1.0) + (_g == 0) * 1.0
        g_xattn = _g[0]
        g_ffn = _g[1]
        return (x, ctx_1024, g_xattn, g_ffn)
    x, ctx_1024, g_xattn, g_ffn = _rec_inputs()

    def _L0_xattn_setup():
        import jax, jax.numpy as jnp
        import numpy as np
        WIDTH = 128
        DATA_WIDTH = 128
        HEADS = 16
        INIT_SCALE = 0.02
        key = jax.random.key(seed)
        ks = jax.random.split(key, 8)
        x = jax.random.normal(ks[0], (2, 128, WIDTH), dtype=jnp.float32)
        data = jax.random.normal(ks[1], (2, 512, DATA_WIDTH), dtype=jnp.float32)
        Wq = jax.random.normal(ks[2], (WIDTH, WIDTH), dtype=jnp.float32) * INIT_SCALE
        bq = jnp.zeros((WIDTH,), dtype=jnp.float32)
        Wkv = jax.random.normal(ks[3], (DATA_WIDTH, 2 * WIDTH), dtype=jnp.float32) * INIT_SCALE
        bkv = jnp.zeros((2 * WIDTH,), dtype=jnp.float32)
        Wp = jax.random.normal(ks[4], (WIDTH, WIDTH), dtype=jnp.float32) * INIT_SCALE
        bp = jnp.zeros((WIDTH,), dtype=jnp.float32)
        return {'x': x, 'data': data, 'Wq': Wq, 'bq': bq, 'Wkv': Wkv, 'bkv': bkv, 'Wp': Wp, 'bp': bp}
    _L0_xattn_all = _L0_xattn_setup()
    _L0_xattn_in = {k: v for k, v in _L0_xattn_all.items() if k in ('Wq', 'bq', 'Wkv', 'bkv', 'Wp', 'bp')}
    del _L0_xattn_all

    def _L0_ffn_setup():
        import jax, jax.numpy as jnp
        import numpy as np
        B, S, H, E, K = (2, 256, 128, 8, 2)
        FF = 4 * H
        EPS = 1e-05
        key = jax.random.key(seed)
        ks = jax.random.split(key, 5)
        rn = lambda k, shape, scale: jax.random.normal(k, shape, dtype=jnp.float32) * scale
        return {'x': rn(ks[0], (B, S, H), 1.0), 'router_W': rn(ks[1], (H, E), H ** (-0.5)), 'router_b': jnp.zeros((E,), jnp.float32), 'ln_g': jnp.ones((E, H), jnp.float32), 'ln_b': jnp.zeros((E, H), jnp.float32), 'W1': rn(ks[2], (E, H, FF), H ** (-0.5)), 'b1': jnp.zeros((E, FF), jnp.float32), 'W2': rn(ks[3], (E, FF, H), FF ** (-0.5)), 'b2': jnp.zeros((E, H), jnp.float32)}
    _L0_ffn_all = _L0_ffn_setup()
    _L0_ffn_in = {k: v for k, v in _L0_ffn_all.items() if k in ('router_W', 'router_b', 'ln_g', 'ln_b', 'W1', 'b1', 'W2', 'b2')}
    del _L0_ffn_all

    def _L1_xattn_setup():
        import jax, jax.numpy as jnp
        import numpy as np
        EMBED_DIM = 128
        NUM_HEADS = 16
        HEAD_DIM = EMBED_DIM // NUM_HEADS
        N, S = (4, 256)
        key = jax.random.key(seed)
        ks = jax.random.split(key, 11)
        s = 1.0 / np.sqrt(EMBED_DIM)
        inp = {'query': jax.random.normal(ks[0], (N, S, EMBED_DIM), jnp.float32), 'key': jax.random.normal(ks[1], (N, S, EMBED_DIM), jnp.float32), 'value': jax.random.normal(ks[2], (N, S, EMBED_DIM), jnp.float32), 'wq': jax.random.normal(ks[3], (EMBED_DIM, EMBED_DIM), jnp.float32) * s, 'bq': jnp.zeros((EMBED_DIM,), jnp.float32), 'wk': jax.random.normal(ks[4], (EMBED_DIM, EMBED_DIM), jnp.float32) * s, 'bk': jnp.zeros((EMBED_DIM,), jnp.float32), 'wv': jax.random.normal(ks[5], (EMBED_DIM, EMBED_DIM), jnp.float32) * s, 'bv': jnp.zeros((EMBED_DIM,), jnp.float32), 'wo': jax.random.normal(ks[6], (EMBED_DIM, EMBED_DIM), jnp.float32) * s, 'bo': jnp.zeros((EMBED_DIM,), jnp.float32)}
        return inp
    _L1_xattn_all = _L1_xattn_setup()
    _L1_xattn_in = {k: v for k, v in _L1_xattn_all.items() if k in ('wq', 'bq', 'wk', 'bk', 'wv', 'bv', 'wo', 'bo')}
    del _L1_xattn_all

    def _L1_ffn_setup():
        import jax, jax.numpy as jnp
        import numpy as np
        E, H, I = (8, 128, 64)
        NG, TKG, TOPK = (4, 2, 4)
        SCALE = 2.5

        def _mlp(x, wg, wu, wd):
            return jax.nn.silu(x @ wg) * (x @ wu) @ wd
        key = jax.random.key(seed)
        ks = jax.random.split(key, 8)
        s = 0.02
        return {'hidden_states': jax.random.normal(ks[0], (32, 32, H), jnp.float32), 'gate_w': jax.random.normal(ks[1], (E, H), jnp.float32) * np.float32(np.sqrt(2.0 / H)), 'correction_bias': jnp.zeros((E,), jnp.float32), 'Wg': jax.random.normal(ks[2], (E, H, I), jnp.float32) * s, 'Wu': jax.random.normal(ks[3], (E, H, I), jnp.float32) * s, 'Wd': jax.random.normal(ks[4], (E, I, H), jnp.float32) * s, 'Wg_s': jax.random.normal(ks[5], (H, I), jnp.float32) * s, 'Wu_s': jax.random.normal(ks[6], (H, I), jnp.float32) * s, 'Wd_s': jax.random.normal(ks[7], (I, H), jnp.float32) * s}
    _L1_ffn_all = _L1_ffn_setup()
    _L1_ffn_in = {k: v for k, v in _L1_ffn_all.items() if k in ('gate_w', 'correction_bias', 'Wg', 'Wu', 'Wd', 'Wg_s', 'Wu_s', 'Wd_s')}
    del _L1_ffn_all
    return {'x': x, 'ctx_1024': ctx_1024, 'g_xattn': g_xattn, 'g_ffn': g_ffn, 'L0_xattn_Wq': _L0_xattn_in['Wq'], 'L0_xattn_bq': _L0_xattn_in['bq'], 'L0_xattn_Wkv': _L0_xattn_in['Wkv'], 'L0_xattn_bkv': _L0_xattn_in['bkv'], 'L0_xattn_Wp': _L0_xattn_in['Wp'], 'L0_xattn_bp': _L0_xattn_in['bp'], 'L0_ffn_router_W': _L0_ffn_in['router_W'], 'L0_ffn_router_b': _L0_ffn_in['router_b'], 'L0_ffn_ln_g': _L0_ffn_in['ln_g'], 'L0_ffn_ln_b': _L0_ffn_in['ln_b'], 'L0_ffn_W1': _L0_ffn_in['W1'], 'L0_ffn_b1': _L0_ffn_in['b1'], 'L0_ffn_W2': _L0_ffn_in['W2'], 'L0_ffn_b2': _L0_ffn_in['b2'], 'L1_xattn_wq': _L1_xattn_in['wq'], 'L1_xattn_bq': _L1_xattn_in['bq'], 'L1_xattn_wk': _L1_xattn_in['wk'], 'L1_xattn_bk': _L1_xattn_in['bk'], 'L1_xattn_wv': _L1_xattn_in['wv'], 'L1_xattn_bv': _L1_xattn_in['bv'], 'L1_xattn_wo': _L1_xattn_in['wo'], 'L1_xattn_bo': _L1_xattn_in['bo'], 'L1_ffn_gate_w': _L1_ffn_in['gate_w'], 'L1_ffn_correction_bias': _L1_ffn_in['correction_bias'], 'L1_ffn_Wg': _L1_ffn_in['Wg'], 'L1_ffn_Wu': _L1_ffn_in['Wu'], 'L1_ffn_Wd': _L1_ffn_in['Wd'], 'L1_ffn_Wg_s': _L1_ffn_in['Wg_s'], 'L1_ffn_Wu_s': _L1_ffn_in['Wu_s'], 'L1_ffn_Wd_s': _L1_ffn_in['Wd_s']}

def reference(x, ctx_1024, g_xattn, g_ffn, L0_xattn_Wq, L0_xattn_bq, L0_xattn_Wkv, L0_xattn_bkv, L0_xattn_Wp, L0_xattn_bp, L0_ffn_router_W, L0_ffn_router_b, L0_ffn_ln_g, L0_ffn_ln_b, L0_ffn_W1, L0_ffn_b1, L0_ffn_W2, L0_ffn_b2, L1_xattn_wq, L1_xattn_bq, L1_xattn_wk, L1_xattn_bk, L1_xattn_wv, L1_xattn_bv, L1_xattn_wo, L1_xattn_bo, L1_ffn_gate_w, L1_ffn_correction_bias, L1_ffn_Wg, L1_ffn_Wu, L1_ffn_Wd, L1_ffn_Wg_s, L1_ffn_Wu_s, L1_ffn_Wd_s):
    import jax
    import jax.numpy as jnp

    def _L0_xattn_ref(x, data, Wq, bq, Wkv, bkv, Wp, bp):
        import jax, jax.numpy as jnp
        import numpy as np
        WIDTH = 128
        DATA_WIDTH = 128
        HEADS = 16
        INIT_SCALE = 0.02
        bs, n_ctx, _ = x.shape
        _, n_data, _ = data.shape
        d = WIDTH // HEADS
        q = (x @ Wq + bq).reshape(bs, n_ctx, HEADS, d)
        kv = (data @ Wkv + bkv).reshape(bs, n_data, HEADS, 2 * d)
        k, v = (kv[..., :d], kv[..., d:])
        scale = 1.0 / np.sqrt(d).astype(np.float32)
        scores = jnp.einsum('bqhd,bkhd->bhqk', q, k) * scale
        attn = jax.nn.softmax(scores, axis=-1)
        out = jnp.einsum('bhqk,bkhd->bqhd', attn, v).reshape(bs, n_ctx, WIDTH)
        return out @ Wp + bp

    def _L0_ffn_ref(x, router_W, router_b, ln_g, ln_b, W1, b1, W2, b2):
        import jax, jax.numpy as jnp
        import numpy as np
        B, S, H, E, K = (2, 256, 128, 8, 2)
        FF = 4 * H
        EPS = 1e-05
        logits = x @ router_W + router_b
        w, idx = jax.lax.top_k(logits, K)
        w = jax.nn.softmax(w, axis=-1)
        gates = jnp.einsum('bske,bsk->bse', jax.nn.one_hot(idx, E, dtype=x.dtype), w)
        mu = jnp.mean(x, axis=-1, keepdims=True)
        var = jnp.mean(jnp.square(x - mu), axis=-1, keepdims=True)
        xhat = (x - mu) * jax.lax.rsqrt(var + EPS)
        h = xhat[:, :, None, :] * ln_g + ln_b
        a = jax.nn.gelu(jnp.einsum('bseh,ehf->bsef', h, W1) + b1, approximate=False)
        y = jnp.einsum('bsef,efh->bseh', a, W2) + b2
        y = y + x[:, :, None, :]
        out = jnp.einsum('bseh,bse->bsh', y, gates)
        return out

    def _L1_xattn_ref(query, key, value, wq, bq, wk, bk, wv, bv, wo, bo):
        import jax, jax.numpy as jnp
        import numpy as np
        EMBED_DIM = 128
        NUM_HEADS = 16
        HEAD_DIM = EMBED_DIM // NUM_HEADS
        N, S = (4, 256)
        n = query.shape[0]
        Q = query @ wq.T + bq
        K = key @ wk.T + bk
        V = value @ wv.T + bv
        Q = Q.reshape(n, -1, NUM_HEADS, HEAD_DIM).transpose(0, 2, 1, 3)
        K = K.reshape(n, -1, NUM_HEADS, HEAD_DIM).transpose(0, 2, 1, 3)
        V = V.reshape(n, -1, NUM_HEADS, HEAD_DIM).transpose(0, 2, 1, 3)
        energy = jnp.einsum('nhqd,nhkd->nhqk', Q, K)
        attn = jax.nn.softmax(energy / jnp.sqrt(jnp.float32(HEAD_DIM)), axis=-1)
        out = jnp.einsum('nhqk,nhkd->nhqd', attn, V)
        out = out.transpose(0, 2, 1, 3).reshape(n, -1, NUM_HEADS * HEAD_DIM)
        return out @ wo.T + bo

    def _L1_ffn_ref(hidden_states, gate_w, correction_bias, Wg, Wu, Wd, Wg_s, Wu_s, Wd_s):
        import jax, jax.numpy as jnp
        import numpy as np
        E, H, I = (8, 128, 64)
        NG, TKG, TOPK = (4, 2, 4)
        SCALE = 2.5

        def _mlp(x, wg, wu, wd):
            return jax.nn.silu(x @ wg) * (x @ wu) @ wd
        B, T, _ = hidden_states.shape
        x = hidden_states.reshape(-1, H)
        N = x.shape[0]
        logits = x @ gate_w.T
        scores = jax.nn.sigmoid(logits)
        scores_c = scores + correction_bias
        grp = scores_c.reshape(N, NG, E // NG)
        group_scores = jnp.sum(jax.lax.top_k(grp, 2)[0], axis=-1)
        grp_idx = jax.lax.top_k(group_scores, TKG)[1]
        group_mask = jnp.zeros_like(group_scores).at[jnp.arange(N)[:, None], grp_idx].set(1.0)
        score_mask = jnp.repeat(group_mask, E // NG, axis=-1) > 0.5
        scores_for_choice = jnp.where(score_mask, scores_c, 0.0)
        topk_idx = jax.lax.top_k(scores_for_choice, TOPK)[1]
        topk_w = jnp.take_along_axis(scores, topk_idx, axis=-1)
        topk_w = topk_w / (jnp.sum(topk_w, axis=-1, keepdims=True) + 1e-20)
        topk_w = topk_w * SCALE
        cw = jnp.sum(jax.nn.one_hot(topk_idx, E, dtype=topk_w.dtype) * topk_w[..., None], axis=1)
        g = jnp.einsum('nh,ehi->eni', x, Wg)
        u = jnp.einsum('nh,ehi->eni', x, Wu)
        y = jnp.einsum('eni,eih->enh', jax.nn.silu(g) * u, Wd)
        routed = jnp.einsum('enh,ne->nh', y, cw)
        out = routed + _mlp(x, Wg_s, Wu_s, Wd_s)
        return out.reshape(B, T, H)
    x = x + jnp.tanh(g_xattn[0]) * _L0_xattn_ref(_layernorm(x, axis=-1), ctx_1024, L0_xattn_Wq, L0_xattn_bq, L0_xattn_Wkv, L0_xattn_bkv, L0_xattn_Wp, L0_xattn_bp)
    x = x + jnp.tanh(g_ffn[0]) * _L0_ffn_ref(_layernorm(x, axis=-1), L0_ffn_router_W, L0_ffn_router_b, L0_ffn_ln_g, L0_ffn_ln_b, L0_ffn_W1, L0_ffn_b1, L0_ffn_W2, L0_ffn_b2)
    x = x + jnp.tanh(g_xattn[1]) * _L1_xattn_ref(_layernorm(x, axis=-1), ctx_1024, ctx_1024, L1_xattn_wq, L1_xattn_bq, L1_xattn_wk, L1_xattn_bk, L1_xattn_wv, L1_xattn_bv, L1_xattn_wo, L1_xattn_bo)
    x = x + jnp.tanh(g_ffn[1]) * _L1_ffn_ref(_layernorm(x, axis=-1), L1_ffn_gate_w, L1_ffn_correction_bias, L1_ffn_Wg, L1_ffn_Wu, L1_ffn_Wd, L1_ffn_Wg_s, L1_ffn_Wu_s, L1_ffn_Wd_s)
    return x

_drawn_inputs = setup_inputs


def setup_inputs(seed=0):
    import zlib

    import numpy as np

    out = dict(_drawn_inputs(seed))
    spreads = {'g_ffn': (-1.0, 0.6),
     'L0_xattn_bq': (0.0, 0.8),
     'L0_xattn_bkv': (0.0, 0.1),
     'L0_xattn_bp': (0.0, 0.1),
     'L0_ffn_router_b': (0.0, 0.1),
     'L0_ffn_ln_g': (1.0, 0.2),
     'L0_ffn_ln_b': (0.0, 0.1),
     'L0_ffn_b1': (0.0, 0.1),
     'L0_ffn_b2': (0.0, 0.1),
     'L1_xattn_bq': (0.0, 0.1),
     'L1_xattn_bk': (0.0, 0.8),
     'L1_xattn_bv': (0.0, 0.1),
     'L1_xattn_bo': (0.0, 0.1),
     'L1_ffn_correction_bias': (0.0, 0.8)}
    factors = {'L0_xattn_Wq': 6.744,
     'L1_ffn_gate_w': 8.0,
     'L1_ffn_Wg': 8.0,
     'L1_ffn_Wu': 8.0,
     'L1_ffn_Wd': 8.0,
     'L1_ffn_Wg_s': 8.0,
     'L1_ffn_Wu_s': 8.0,
     'L1_ffn_Wd_s': 8.0}
    for name, (base, spread) in spreads.items():
        noise = np.random.default_rng([zlib.crc32(name.encode()), seed]).standard_normal(out[name].shape)
        drawn = base * np.exp(spread * noise) if base else spread * noise
        out[name] = jnp.asarray(drawn.astype(out[name].dtype))
    for name, factor in factors.items():
        out[name] = (out[name] * factor).astype(out[name].dtype)
    return out
```

```python
import concourse.bass as bass
from concourse import mybir
from contextlib import ExitStack

F32 = mybir.dt.float32
F32R = mybir.dt.float32r
I32 = mybir.dt.int32
ALU = mybir.AluOpType
ACT = mybir.ActivationFunctionType
AX = mybir.AxisListType

P = 128
B = 4
T = 4
Q = T * P
L = 2
S = 77
HD = 8
G = 4
HG = 4
H = G * HG
GW = HG * HD
KG = HG * S
C = -(-KG // P)
E = 8
FF = 512
FC = FF // P
I1 = 64
PAIRS = E // 2
EPS = 1e-5
SCALE = 1.0 / float(HD) ** 0.5
ROUTED_SCALE = 2.5
RSQRT_GUESS = 0x5F3759DF

R_BK, R_BQ, R_BV, R_B1, R_LNG, R_LNB, R_GW = 0, 8, 16, 18, 50, 58, 66
ROWS = 74
CH = [(c * P) % S for c in range(C)]


def build(nc, I, out):
    ctx = ExitStack()
    with ctx:
        def sb(name, shape, dt=F32):
            return ctx.enter_context(nc.sbuf_tensor(name, shape, dt))

        def sem(name):
            return ctx.enter_context(nc.semaphore(name))

        X = sb("X", [P, B * T, P])
        xn = sb("xn", [P, B * T, P])
        ctx_sb = sb("ctx_sb", [S, B, P])
        rows = sb("rows", [ROWS, P])
        cols = sb("cols", [P, ROWS])
        wq0 = sb("wq0", [P, P])
        wkv0 = sb("wkv0", [P, 2 * P])
        wnat = sb("wnat", [P, 4, P])
        wT = sb("wT", [P, 4, P])
        wv = sb("wv", [P, L, P])
        wp = sb("wp", [P, L, P])
        wpx = sb("wpx", [P, L, P])
        wkS = sb("wkS", [P, L, G, P])
        wqS = sb("wqS", [P, L, G, P])
        gains = sb("gains", [P, 4])
        tg = sb("tg", [P, 4])
        bpb = sb("bpb", [P, L, P])
        bpx = sb("bpx", [P, L, P])
        bvb = sb("bvb", [P, L, P])
        rb = sb("rb", [P, E])
        cb = sb("cb", [P, E])
        rw = sb("rw", [P, E])
        b2p = sb("b2p", [P, P])
        w1raw = sb("w1raw", [P, 2, FF])
        w1h = sb("w1h", [P, E, FF], F32R)
        w1l = sb("w1l", [P, E, FF], F32R)
        w2 = sb("w2", [P, E, FC, P])
        b1p = sb("b1p", [P, E * FC])
        wg1 = sb("wg1", [P, PAIRS + 1, P])
        wu1 = sb("wu1", [P, PAIRS + 1, P])
        wd1 = sb("wd1", [P, PAIRS + 1, P])
        ident = sb("ident", [P, P])
        maskK = sb("maskK", [P, G, HG])
        maskV = sb("maskV", [P, C, P])
        tri = sb("tri", [P, E, E])
        pick = sb("pick", [P, PAIRS, P])
        pickr = sb("pickr", [P, PAIRS, P], F32R)
        ctxT = sb("ctxT", [P, B, 3, S])
        kst = sb("kst", [P, L, G, B * S])
        K4 = sb("K4", [P, 2, G, C * P], F32R)
        V4 = sb("V4", [P, 2, C, P])
        Z = sb("Z", [P, 2, G, Q], F32R)
        qhi = sb("qhi", [P, G, Q], F32R)
        khi = qhi[:, :, 0:B * S]
        xT = sb("xT", [P, Q])
        mpad = sb("mpad", [P, T, P])
        Pr = sb("Pr", [P, 2, G, Q])
        rden = sb("rden", [P, Q])
        oT = sb("oT", [P, Q])
        st6 = sb("st6", [P, T, 6])
        mv = sb("mv", [P, T, 2])
        ve = sb("ve", [P, T])
        rs = sb("rs", [P, T])
        rt = sb("rt", [P, T])
        xa = sb("xa", [P, T, P])
        xh = sb("xh", [P, T, P])
        xhTh = sb("xhTh", [P, B * Q], F32R)
        xhTl = sb("xhTl", [P, B * Q], F32R)
        lg = sb("lg", [P, T, E])
        lw = sb("lw", [P, T, E])
        cmpa = sb("cmpa", [P, T, E, E])
        cmpb = sb("cmpb", [P, T, E, E])
        rank = sb("rank", [P, T, E])
        gsc = sb("gsc", [P, T, E // 2])
        t4 = sb("t4", [P, T])
        ex = sb("ex", [P, T, E])
        gate = sb("gate", [P, B, T, E])
        gcur = sb("gcur", [P, T, E])
        gpad = sb("gpad", [P, T, P])
        gT = oT
        cwT = xhTl[:, :].rearrange("p (b q) -> p b q", b=B)
        acc = rden[:, :].rearrange("p (t n) -> p t n", t=T)
        act = Pr
        x3T = act[:, :, :, :].rearrange("p a c q -> p (a c) q")
        w2flat = w2[:, :, :, :].rearrange("p e c n -> p (e c n)")
        hT = w2flat[:, 0:(PAIRS + 1) * Q].rearrange("p (a q) -> p a q", q=Q)
        sg = w2flat[:, (PAIRS + 1) * Q:(PAIRS + 3) * Q].rearrange("p (a q) -> p a q", q=Q)

        ps = ctx.enter_context(nc.psum_tensor("ps", [P, 8, 512], F32))
        S0, O, D, F = 0, 2, 3, 4
        HB, YB = 0, 4

        x_in = [sem(f"x_in{b}") for b in range(B)]
        ctx_in, rows_in, attw_in, small_in, w2_in, m1w_in = (sem(n) for n in (
            "ctx_in", "rows_in", "attw_in", "small_in", "w2_in", "m1w_in"))
        w1_in = [sem(f"w1_in{i}") for i in range(2)]
        w1_used = sem("w1_used")
        zeroed = sem("zeroed")
        consts = sem("consts")
        setup_ps, setup_sb, setup_act = sem("setup_ps"), sem("setup_sb"), sem("setup_act")
        dstep, astep, pstep = sem("dstep"), sem("astep"), sem("pstep")
        dloop = sem("dloop")
        xn_ready, xt_ps, xt_sb, v_ps, v_sb, q_ps, qh_sb, z_sb = (sem(n) for n in (
            "xn_ready", "xt_ps", "xt_sb", "v_ps", "v_sb", "q_ps", "qh_sb", "z_sb"))
        k4_ready, mx_ps, mx_done, mt_ps, mz_sb = (sem(n) for n in (
            "k4_ready", "mx_ps", "mx_done", "mt_ps", "mz_sb"))
        s_ps, p_sb, pv_done, o_read, ot_sb, proj_ps, res_done = (sem(n) for n in (
            "s_ps", "p_sb", "pv_done", "o_read", "ot_sb", "proj_ps", "res_done"))
        w1h_done, b1_ps, b1_sb = (sem(n) for n in ("w1h_done", "b1_ps", "b1_sb"))
        xa_ready, xh_ready, xa_ps, xa_sb, lg_ps, xh_ps, xhh_sb, xhl_sb = (sem(n) for n in (
            "xa_ready", "xh_ready", "xa_ps", "xa_sb", "lg_ps", "xh_ps", "xhh_sb", "xhl_sb"))
        lg_sb, dif_sb, ex_sb, gp_sb, gt_ps, gt_sb, b2_ps, b2_sb = (sem(n) for n in (
            "lg_sb", "dif_sb", "ex_sb", "gp_sb", "gt_ps", "gt_sb", "b2_ps", "b2_sb"))
        h_ps, a_sb, y_ps, y_used, x_final = (sem(n) for n in ("h_ps", "a_sb", "y_ps", "y_used", "x_final"))
        n3_ready, t3_ps, t3_sb, l3_ps, l3_sb, e3_sb, c3_sb, c3_ps, c3h_sb, c3l_sb = (sem(n) for n in (
            "n3_ready", "t3_ps", "t3_sb", "l3_ps", "l3_sb", "e3_sb", "c3_sb", "c3_ps", "c3h_sb", "c3l_sb"))
        gu_ps, sg_sb, h3_sb, y3_ps, x_out = (sem(n) for n in ("gu_ps", "sg_sb", "h3_sb", "y3_ps", "x_out"))
        stored = sem("stored")

        LN = L * B
        block = ctx.enter_context(nc.Block())

        @block.sync
        def _(sp):
            for b in range(B):
                sp.dma_start(X[:, T * b:T * (b + 1), :],
                             I["x"][b].rearrange("(t p) d -> p t d", p=P)).then_inc(x_in[b], 16)
            sp.dma_start(ctx_sb[:, :, :], I["ctx_1024"].rearrange("b k d -> k b d")).then_inc(ctx_in, 16)
            for e in range(E):
                if e >= 2:
                    sp.wait_ge(w1_used, e - 1)
                    sp.wait_ge(b1_ps, e // 2)
                sp.dma_start(w1raw[:, e % 2, :], I["L0_ffn_W1"][e]).then_inc(w1_in[e % 2], 16)
            sp.dma_start(w2[:, :, :, :], I["L0_ffn_W2"].rearrange("e (c p) n -> p e c n", p=P)).then_inc(w2_in, 16)
            sp.wait_ge(zeroed, 4)
            for w, name in ((wg1, "L1_ffn_Wg"), (wu1, "L1_ffn_Wu")):
                sp.dma_start(w[:, 0:PAIRS, :].rearrange("p a (e i) -> p (a e) i", e=2),
                             I[name].rearrange("e d i -> d e i")).then_inc(m1w_in, 16)
                sp.dma_start(w[:, PAIRS, 0:I1], I[name + "_s"]).then_inc(m1w_in, 16)
            for two in range(2):
                sp.dma_start(wd1[I1 * two:I1 * (two + 1), 0:PAIRS, :],
                             I["L1_ffn_Wd"].rearrange("(a e) i n -> e i a n", e=2)[two]).then_inc(m1w_in, 16)
            sp.dma_start(wd1[0:I1, PAIRS, :], I["L1_ffn_Wd_s"]).then_inc(m1w_in, 16)
            for b in range(B):
                sp.wait_ge(x_out, b + 1)
                sp.dma_start(out[b].rearrange("(t p) d -> p t d", p=P),
                             X[:, T * b:T * (b + 1), :]).then_inc(stored, 16)
            sp.wait_ge(stored, 16 * B)

        M1W = 16 * 7

        @block.gpsimd
        def _(pool):
            n = [0]

            def link(ins):
                n[0] += 1
                ins.then_inc(pstep, 1)
                pool.wait_ge(pstep, n[0])

            pool.memset(rows[:, :], 0.0).then_inc(zeroed, 1)
            pool.wait_ge(zeroed, 1)
            pool.memset(rows[0:8, 3 * GW:P], -1.0).then_inc(zeroed, 1)
            link(pool.memset(ident[:, :], 0.0))
            link(pool.affine_select(out=ident[:, :], in_=ident[:, :], compare_op=ALU.not_equal, fill=1.0,
                                    base=0, pattern=[[-1, P]], channel_multiplier=1))
            link(pool.memset(wg1[:, PAIRS, I1:P], 0.0))
            link(pool.memset(wu1[:, PAIRS, I1:P], 0.0))
            pool.memset(wd1[I1:P, PAIRS, :], 0.0).then_inc(zeroed, 2)
            pool.wait_ge(zeroed, 4)
            link(pool.memset(maskK[:, :, :], 1.0))
            for r in range(3):
                m = maskK[GW * r:GW * (r + 1), :, :]
                link(pool.affine_select(out=m, in_=m, compare_op=ALU.is_ge, fill=0.0, base=0,
                                        pattern=[[0, G], [-HD, HG]], channel_multiplier=1))
                link(pool.affine_select(out=m, in_=m, compare_op=ALU.is_ge, fill=0.0, base=HD - 1,
                                        pattern=[[0, G], [HD, HG]], channel_multiplier=-1))
            m = maskK[3 * GW:P, :, :]
            link(pool.affine_select(out=m, in_=m, compare_op=ALU.is_equal, fill=0.0, base=0,
                                    pattern=[[-HG, G], [-1, HG]], channel_multiplier=1))
            link(pool.memset(maskV[:, :, :], 1.0))
            for c in range(C):
                m = maskV[:, c, :].rearrange("p (g h d) -> p g h d", g=G, h=HG)
                link(pool.affine_select(out=m, in_=m, compare_op=ALU.is_ge, fill=0.0, base=P * c,
                                        pattern=[[0, G], [-S, HG], [0, HD]], channel_multiplier=1))
                link(pool.affine_select(out=m, in_=m, compare_op=ALU.is_ge, fill=0.0, base=S - 1 - P * c,
                                        pattern=[[0, G], [S, HG], [0, HD]], channel_multiplier=-1))
            link(pool.memset(tri[:, :, :], 1.0))
            link(pool.affine_select(out=tri[:, :, :], in_=tri[:, :, :], compare_op=ALU.is_gt, fill=0.0, base=0,
                                    pattern=[[1, E], [-1, E]], channel_multiplier=0))
            link(pool.memset(pick[:, :, :], 0.0))
            for r in (0, 32):
                m = pick[r:r + E, :, :].rearrange("p a (e i) -> p a e i", e=2)
                link(pool.affine_select(out=m, in_=m, compare_op=ALU.not_equal, fill=1.0, base=0,
                                        pattern=[[-2, PAIRS], [-1, 2], [0, I1]], channel_multiplier=1))
            link(pool.memset(mpad[:, :, :], 0.0))
            link(pool.memset(gpad[:, :, :], 0.0))
            pool.tensor_copy(pickr[:, :, :], pick[:, :, :]).then_inc(consts, 1)
            for s in range(LN):
                l, b = divmod(s, B)
                pool.wait_ge(setup_sb, 3 + l)
                if s >= 2:
                    pool.wait_ge(s_ps, G * C * (s - 1))
                for g in range(G):
                    o = K4[:, s % 2, g, 0:KG].rearrange("p (h k) -> p h k", h=HG)
                    k = kst[:, l, g, S * b:S * (b + 1)]
                    pool.tensor_tensor(o, k.unsqueeze(1).broadcast_to([P, HG, S]),
                                       maskK[:, g, :].unsqueeze(2).broadcast_to([P, HG, S]),
                                       ALU.mult).then_inc(k4_ready, 1)

        @block.scalar
        def _(eng):
            eng.wait_ge(zeroed, 2)
            bkv = I["L0_xattn_bkv"].rearrange("(g h x) -> g h x", g=G, h=HG)
            for r in range(3):
                dst = slice(GW * r, GW * (r + 1))
                eng.dma_start(rows[R_BK:R_BK + G, dst].rearrange("g (h d) -> g h d", h=HG),
                              bkv[:, :, 0:HD]).then_inc(rows_in, 16)
                eng.dma_start(rows[R_BK + G:R_BK + 2 * G, dst], I["L1_xattn_bk"].rearrange("(g x) -> g x", g=G)).then_inc(rows_in, 16)
                eng.dma_start(rows[R_BQ:R_BQ + G, dst], I["L0_xattn_bq"].rearrange("(g x) -> g x", g=G)).then_inc(rows_in, 16)
                eng.dma_start(rows[R_BQ + G:R_BQ + 2 * G, dst], I["L1_xattn_bq"].rearrange("(g x) -> g x", g=G)).then_inc(rows_in, 16)
            eng.dma_start(rows[R_BV:R_BV + 1, :].rearrange("o (h d) -> o h d", h=H),
                          I["L0_xattn_bkv"].rearrange("(o h x) -> o h x", o=1, h=H)[:, :, HD:2 * HD]).then_inc(rows_in, 16)
            eng.dma_start(rows[R_BV + 1:R_BV + 2, :], I["L1_xattn_bv"].rearrange("(o n) -> o n", o=1)).then_inc(rows_in, 16)
            eng.dma_start(rows[R_B1:R_B1 + E * FC, :], I["L0_ffn_b1"].rearrange("e (c p) -> (e c) p", p=P)).then_inc(rows_in, 16)
            eng.dma_start(rows[R_LNG:R_LNG + E, :], I["L0_ffn_ln_g"]).then_inc(rows_in, 16)
            eng.dma_start(rows[R_LNB:R_LNB + E, :], I["L0_ffn_ln_b"]).then_inc(rows_in, 16)
            eng.dma_start(rows[R_GW:R_GW + E, :], I["L1_ffn_gate_w"]).then_inc(rows_in, 16)
            eng.dma_start(wq0[:, :], I["L0_xattn_Wq"]).then_inc(attw_in, 16)
            eng.dma_start(wkv0[:, :], I["L0_xattn_Wkv"]).then_inc(attw_in, 16)
            eng.dma_start(wp[:, 0, :], I["L0_xattn_Wp"]).then_inc(attw_in, 16)
            for i, n in enumerate(("wq", "wk", "wv", "wo")):
                eng.dma_start(wnat[:, i, :], I["L1_xattn_" + n]).then_inc(attw_in, 16)
            for i, (n, j) in enumerate((("g_xattn", 0), ("g_ffn", 2))):
                eng.dma_start(gains[:, j:j + 2], I[n].rearrange("(o n) -> o n", o=1).broadcast_to([P, 2])).then_inc(small_in, 16)
            eng.dma_start(bpb[:, 0, :], I["L0_xattn_bp"].rearrange("(o n) -> o n", o=1).broadcast_to([P, P])).then_inc(small_in, 16)
            eng.dma_start(bpb[:, 1, :], I["L1_xattn_bo"].rearrange("(o n) -> o n", o=1).broadcast_to([P, P])).then_inc(small_in, 16)
            eng.dma_start(rb[:, :], I["L0_ffn_router_b"].rearrange("(o n) -> o n", o=1).broadcast_to([P, E])).then_inc(small_in, 16)
            eng.dma_start(cb[:, :], I["L1_ffn_correction_bias"].rearrange("(o n) -> o n", o=1).broadcast_to([P, E])).then_inc(small_in, 16)
            eng.dma_start(rw[:, :], I["L0_ffn_router_W"]).then_inc(small_in, 16)
            eng.wait_ge(setup_sb, 1)
            eng.dma_start(b2p[0:E, :], I["L0_ffn_b2"]).then_inc(small_in, 16)
            eng.wait_ge(small_in, 16 * 8)
            eng.activation(tg[:, :], gains[:, :], ACT.Tanh).then_inc(setup_act, 1)
            for l in range(L):
                eng.wait_ge(setup_ps, 4 + l)
                for g in range(G):
                    ins = eng.activation(khi[2 * GW:3 * GW, g, :], ps[2 * GW:3 * GW, F + g, 0:B * S], ACT.Identity,
                                         bias=cols[2 * GW:3 * GW, R_BK + G * l + g:R_BK + G * l + g + 1])
                ins.then_inc(setup_act, 1)
                if l == 0:
                    eng.wait_ge(setup_sb, 3)

            def x_copy(s):
                eng.wait_ge(xt_ps, s + 1)
                eng.activation(xT[:, :], ps[:, F, :], ACT.Copy).then_inc(xt_sb, 1)

            def q_upper(s, g):
                l = s // B
                eng.wait_ge(q_ps, G * s + g + 1)
                if s >= 1:
                    eng.wait_ge(z_sb, G * (s - 1) + g + 1)
                eng.activation(qhi[GW:2 * GW, g, :], ps[GW:2 * GW, F + g, :], ACT.Identity,
                               bias=cols[GW:2 * GW, R_BQ + G * l + g:R_BQ + G * l + g + 1]).then_inc(qh_sb, 1)

            def m_rows(s):
                eng.wait_ge(mt_ps, s + 1)
                if s >= 2:
                    eng.wait_ge(s_ps, G * C * (s - 1))
                eng.activation(Z[3 * GW:3 * GW + H, s % 2, :, :],
                               ps[3 * GW:3 * GW + H, F, :].unsqueeze(1).broadcast_to([H, G, Q]),
                               ACT.Copy).then_inc(mz_sb, 1)

            def exps(s, c, g):
                i = G * C * s + G * c + g
                n = C * s + c
                eng.wait_ge(s_ps, i + 1)
                if n >= 2 and g == 0:
                    eng.wait_ge(pv_done, n - 1)
                eng.activation(Pr[:, n % 2, g, :], ps[:, S0 + i % 2, :], ACT.Exp, scale=SCALE).then_inc(p_sb, 1)

            def w1_upper(e):
                eng.wait_ge(w1_in[e % 2], 16 * (e // 2 + 1))
                eng.activation(w1h[:, e, :], w1raw[:, e % 2, :], ACT.Copy,
                               scale=cols[:, R_LNG + e:R_LNG + e + 1]).then_inc(w1h_done, 1)

            def attention(l):
                s0 = l * B
                x_copy(s0)
                for g in range(G):
                    q_upper(s0, g)
                m_rows(s0)
                for s in range(s0, s0 + B):
                    more = s + 1 < s0 + B
                    for i in range(G * C):
                        exps(s, i // G, i % G)
                        if more and i == 0:
                            x_copy(s + 1)
                        if more and i in (5, 6, 7):
                            q_upper(s + 1, i - 5)
                        if more and i == 7:
                            q_upper(s + 1, 3)
                        if l == 0 and i in (9, 10):
                            w1_upper(2 * s + i - 9)
                    if more:
                        m_rows(s + 1)

            attention(0)
            for b in range(B):
                eng.wait_ge(xa_ps, b + 1)
                eng.activation(xT[:, :], ps[:, F, :], ACT.Copy).then_inc(xa_sb, 1)
                eng.wait_ge(xh_ps, b + 1)
                eng.activation(xhTh[:, Q * b:Q * (b + 1)], ps[:, F + 1, :], ACT.Copy).then_inc(xhh_sb, 1)
                eng.wait_ge(dif_sb, b + 1)
                eng.activation(ex[:, :, :], lw[:, :, :], ACT.Exp).then_inc(ex_sb, 1)
                eng.wait_ge(gt_ps, b + 1)
                ins = eng.activation(gT[:, :], ps[:, F + 3, :], ACT.Copy).then_inc(gt_sb, 1)
            eng.wait_ge(gt_sb, B)
            eng.activation(ex[:, :, :], lw[:, :, :], ACT.Copy).then_inc(a_sb, FC)
            with eng.Fori(0, B) as b:
                for e in range(E):
                    eng.wait_ge(y_ps, b * E + (e + 1))
                    for c in range(FC):
                        eng.wait_ge(h_ps, b * (E * FC) + (FC * e + c + 1))
                        eng.activation(act[:, e % 2, c, :], ps[:, HB + c, :], ACT.Gelu,
                                       bias=b1p[:, FC * e + c:FC * e + c + 1]).then_inc(a_sb, 1)
            attention(1)
            for b in range(B):
                eng.wait_ge(t3_ps, b + 1)
                eng.activation(x3T[:, b, :], ps[:, F, :], ACT.Copy).then_inc(t3_sb, 1)
                eng.wait_ge(l3_sb, b + 1)
                eng.activation(ex[:, :, :], lw[:, :, :], ACT.Exp).then_inc(e3_sb, 1)
                eng.wait_ge(c3_ps, b + 1)
                eng.activation(cwT[0:E, b, :], ps[0:E, F + 2, :], ACT.Copy).then_inc(c3h_sb, 1)
            for i in range(B * (PAIRS + 1)):
                eng.wait_ge(gu_ps, i + 1)
                if i >= 2:
                    eng.wait_ge(h3_sb, i - 1)
                eng.activation(sg[:, i % 2, :], ps[:, 3 * (i % 2), :], ACT.Silu).then_inc(sg_sb, 1)

        @block.tensor
        def _(pe):
            def mm(o, w, x, start=True, stop=True):
                return nc.tensor.matmul(o, w, x, start=start, stop=stop)

            pe.wait_ge(pstep, 2)
            pe.wait_ge(rows_in, 16 * 18)
            nc.tensor.transpose(ps[:, F, 0:ROWS], rows[:, :], ident[0:ROWS, 0:ROWS]).then_inc(setup_ps, 1)
            pe.wait_ge(ctx_in, 16)
            for b in range(B):
                ins = nc.tensor.transpose(ps[:, F + 1, S * b:S * (b + 1)], ctx_sb[:, b, :], ident[0:S, 0:S])
            ins.then_inc(setup_ps, 1)
            pe.wait_ge(attw_in, 16 * 7)
            for i in range(4):
                ins = nc.tensor.transpose(ps[:, F + 2, P * i:P * (i + 1)], wnat[:, i, :], ident[:, :])
            ins.then_inc(setup_ps, 1)
            for l in range(L):
                pe.wait_ge(setup_sb, 2 + l)
                for g in range(G):
                    ins = mm(ps[:, F + g, 0:B * S], wkS[:, l, g, :],
                             ctxT[:, :, 0, :])
                ins.then_inc(setup_ps, 1)
            pe.wait_ge(setup_sb, 4)
            for l in range(L):
                ins = mm(ps[:, F, P * l:P * (l + 1)], bvb[:, l, :], wp[:, l, :])
            ins.then_inc(setup_ps, 1)
            pe.wait_ge(setup_sb, 5)

            def front_x(s):
                pe.wait_ge(xn_ready, s + 1)
                if s % B:
                    pe.wait_ge(mz_sb, s)
                for t in range(T):
                    ins = nc.tensor.transpose(ps[:, F, P * t:P * (t + 1)], xn[:, T * (s % B) + t, :], ident[:, :])
                ins.then_inc(xt_ps, 1)

            def front_v(s):
                l, b = divmod(s, B)
                if s % B >= 2:
                    pe.wait_ge(res_done, s - 1)
                rep = ctxT[:, b, :, :].rearrange("p r k -> p (r k)")
                for c in range(C):
                    ins = mm(ps[:, F + 1, P * c:P * (c + 1)], rep[:, CH[c]:CH[c] + P], wv[:, l, :])
                ins.then_inc(v_ps, 1)

            def front_q(s, g):
                l = s // B
                if g == 0:
                    pe.wait_ge(xt_sb, s + 1)
                if g == 1:
                    pe.wait_ge(v_sb, s + 1)
                if g == 2 and 2 <= s < B:
                    pe.wait_ge(b1_sb, s - 1)
                mm(ps[:, F + g, :], wqS[:, l, g, :], xT[:, :]).then_inc(q_ps, 1)

            def front_mx(s, t, half):
                if t == 0:
                    pe.wait_ge(z_sb, G * s + 2 * half + 2)
                    pe.wait_ge(k4_ready, G * s + 2 * half + 2)
                else:
                    pe.wait_ge(mx_done, 2 * T * s + 2 * (t - 1) + half + 1)
                for g in (2 * half, 2 * half + 1):
                    ins = mm(ps[:, F + g, 0:KG], Z[0:3 * GW, s % 2, g, P * t:P * (t + 1)],
                             K4[0:3 * GW, s % 2, g, 0:KG])
                ins.then_inc(mx_ps, 1)

            def front_m(s):
                pe.wait_ge(mx_done, 2 * T * (s + 1))
                for t in range(T):
                    ins = mm(ps[:, F, P * t:P * (t + 1)], mpad[:, t, :], ident[:, :])
                ins.then_inc(mt_ps, 1)

            def scores(s, c, g):
                i = G * C * s + G * c + g
                if c == 0 and g == 0:
                    pe.wait_ge(mz_sb, s + 1)
                if i >= 2:
                    pe.wait_ge(p_sb, i - 1)
                mm(ps[:, S0 + i % 2, :], K4[:, s % 2, g, P * c:P * (c + 1)], Z[:, s % 2, g, :]).then_inc(s_ps, 1)

            def pv(s, c):
                n = C * s + c
                pe.wait_ge(p_sb, G * (n + 1))
                if c == 0:
                    pe.wait_ge(v_sb, s + 1)
                    if s:
                        pe.wait_ge(o_read, s)
                for bank, w in ((O, V4[:, s % 2, c, :]), (D, maskV[:, c, :])):
                    for g in range(G):
                        cols_g = slice(GW * g, GW * (g + 1))
                        ins = nc.tensor.matmul(ps[cols_g, bank, :], w[:, cols_g], Pr[:, n % 2, g, :],
                                               start=c == 0, stop=c == C - 1, tile_position=(0, GW * g))
                ins.then_inc(pv_done, 1)

            def w1_bias(s):
                pe.wait_ge(mx_done, 2 * T * min(s + 2, B))
                for e in (2 * s, 2 * s + 1):
                    pe.wait_ge(w1_in[e % 2], 16 * (e // 2 + 1))
                    for c in range(FC):
                        i = FC * (e % 2) + c
                        ins = mm(ps[:, F + 2, i:i + 1], w1raw[:, e % 2, P * c:P * (c + 1)], cols[:, R_LNB + e:R_LNB + e + 1])
                ins.then_inc(b1_ps, 1)

            def project(s):
                pe.wait_ge(ot_sb, s + 1)
                for t in range(T):
                    ins = mm(ps[:, F + 1, P * t:P * (t + 1)], oT[:, P * t:P * (t + 1)], wpx[:, s // B, :])
                ins.then_inc(proj_ps, 1)

            def attention(l):
                s0 = l * B
                front_x(s0)
                front_v(s0)
                for g in range(G):
                    front_q(s0, g)
                for i in range(2 * T):
                    front_mx(s0, i // 2, i % 2)
                front_m(s0)
                for s in range(s0, s0 + B):
                    n = s + 1 if s + 1 < s0 + B else None
                    sc = iter([(s, i // G, i % G) for i in range(G * C)])
                    step = lambda k=1: [scores(*next(sc)) for _ in range(k)]
                    front = lambda f, *a: n is not None and f(n, *a)
                    step()
                    front(front_x)
                    step(2)
                    front(front_v)
                    step(2)
                    front(front_q, 0)
                    step()
                    front(front_q, 1)
                    step()
                    front(front_q, 2)
                    step()
                    front(front_q, 3)
                    pv(s, 0)
                    front(front_mx, 0, 0)
                    step()
                    front(front_mx, 0, 1)
                    step()
                    pv(s, 1)
                    front(front_mx, 1, 0)
                    front(front_mx, 1, 1)
                    step()
                    front(front_mx, 2, 0)
                    front(front_mx, 2, 1)
                    step()
                    pv(s, 2)
                    front(front_mx, 3, 0)
                    front(front_mx, 3, 1)
                    front(front_m)
                    if l == 0:
                        w1_bias(s)
                    project(s)

            attention(0)
            for b in range(B):
                pe.wait_ge(xa_ready, b + 1)
                if b:
                    pe.wait_ge(b2_sb, b)
                for t in range(T):
                    ins = nc.tensor.transpose(ps[:, F, P * t:P * (t + 1)], xa[:, t, :], ident[:, :])
                ins.then_inc(xa_ps, 1)
                pe.wait_ge(xh_ready, b + 1)
                if b:
                    pe.wait_ge(xhl_sb, b)
                else:
                    pe.wait_ge(res_done, B)
                for t in range(T):
                    ins = nc.tensor.transpose(ps[:, F + 1, P * t:P * (t + 1)], xh[:, t, :], ident[:, :])
                ins.then_inc(xh_ps, 1)
                pe.wait_ge(xa_sb, b + 1)
                for t in range(T):
                    ins = mm(ps[:, F + 2, E * t:E * (t + 1)], xT[:, P * t:P * (t + 1)], rw[:, :])
                ins.then_inc(lg_ps, 1)
                pe.wait_ge(gp_sb, b + 1)
                for t in range(T):
                    ins = nc.tensor.transpose(ps[:, F + 3, P * t:P * (t + 1)], gpad[:, t, :], ident[:, :])
                ins.then_inc(gt_ps, 1)
                pe.wait_ge(gt_sb, b + 1)
                for t in range(T):
                    ins = mm(ps[:, F, P * t:P * (t + 1)], gT[:, P * t:P * (t + 1)], b2p[:, :])
                ins.then_inc(b2_ps, 1)
            pe.wait_ge(w1_used, E)
            pe.wait_ge(b1_sb, B)
            pe.wait_ge(b2_sb, B)
            pe.wait_ge(xhl_sb, B)
            pe.wait_ge(w2_in, 16)
            pe.wait_ge(dloop, 1)
            mm(ps[:, YB, 0:P], ident[:, :], ident[:, :]).then_inc(y_ps, 2)

            def hidden(b, e):
                for c in range(FC):
                    pe.wait_ge(a_sb, b * (E * FC) + (FC * e + c + 1))
                    xh_b, xl_b = (x[:, bass.ds(b * Q, Q)] for x in (xhTh, xhTl))
                    col = slice(P * c, P * (c + 1))
                    mm(ps[:, HB + c, :], w1h[:, e, col], xh_b, True, False)
                    mm(ps[:, HB + c, :], w1h[:, e, col], xl_b, False, False)
                    mm(ps[:, HB + c, :], w1l[:, e, col], xh_b, False, True).then_inc(h_ps, 1)

            def output(b, e):
                pe.wait_ge(a_sb, b * (E * FC) + (FC * (e + 2)))
                pe.wait_ge(y_used, b * E + (e + 1))
                for t in range(T):
                    for c in range(FC):
                        ins = mm(ps[:, YB + e % 2, P * t:P * (t + 1)], act[:, e % 2, c, P * t:P * (t + 1)],
                                 w2[:, e, c, :], c == 0, c == FC - 1)
                ins.then_inc(y_ps, 1)

            with pe.Fori(0, B) as b:
                hidden(b, 0)
                for e in range(E):
                    if e + 1 < E:
                        hidden(b, e + 1)
                    output(b, e)
            pe.wait_ge(y_used, 2 + B * E)
            attention(1)
            for b in range(B):
                pe.wait_ge(n3_ready, b + 1)
                if b:
                    pe.wait_ge(t3_sb, b)
                for t in range(T):
                    ins = nc.tensor.transpose(ps[:, F, P * t:P * (t + 1)], xn[:, T * b + t, :], ident[:, :])
                ins.then_inc(t3_ps, 1)
                pe.wait_ge(t3_sb, b + 1)
                if b == 0:
                    pe.wait_ge(res_done, 2 * B)
                for t in range(T):
                    ins = mm(ps[:, F + 1, E * t:E * (t + 1)], x3T[:, b, P * t:P * (t + 1)], cols[:, R_GW:R_GW + E])
                ins.then_inc(l3_ps, 1)
                pe.wait_ge(c3_sb, b + 1)
                if b:
                    pe.wait_ge(c3l_sb, b)
                for t in range(T):
                    ins = nc.tensor.transpose(ps[:, F + 2, P * t:P * (t + 1)], gpad[:, t, :], ident[:, :])
                ins.then_inc(c3_ps, 1)
            pe.wait_ge(c3l_sb, B)
            pe.wait_ge(m1w_in, M1W)

            def gate_up(b, a):
                i = b * (PAIRS + 1) + a
                g0 = 3 * (i % 2)
                if i >= 2:
                    pe.wait_ge(h3_sb, i - 1)
                mm(ps[:, g0, :], wg1[:, a, :], x3T[:, b, :])
                ins = mm(ps[:, g0 + 1, :], wu1[:, a, :], x3T[:, b, :])
                if a < PAIRS:
                    ins = mm(ps[:, g0 + 2, :], pickr[:, a, :], cwT[:, b, :])
                ins.then_inc(gu_ps, 1)

            def down(b):
                pe.wait_ge(h3_sb, (b + 1) * (PAIRS + 1))
                if b >= 2:
                    pe.wait_ge(x_out, b - 1)
                for t in range(T):
                    for a in range(PAIRS + 1):
                        ins = mm(ps[:, 6 + b % 2, P * t:P * (t + 1)], hT[:, a, P * t:P * (t + 1)], wd1[:, a, :],
                                 a == 0, a == PAIRS)
                ins.then_inc(y3_ps, 1)

            for b in range(B):
                for a in range(PAIRS + 1):
                    gate_up(b, a)
                down(b)

        @block.vector
        def _(dve):
            n = [0]

            def link(ins):
                n[0] += 1
                ins.then_inc(dstep, 1)
                dve.wait_ge(dstep, n[0])

            def rsqrt(link, eps):
                link(dve.tensor_scalar(ve[:, :], mv[:, :, 1], eps, None, ALU.add))
                link(dve.tensor_scalar(rs[:, :].bitcast(I32), ve[:, :].bitcast(I32), -0.5, float(RSQRT_GUESS),
                                       ALU.mult, ALU.add))
                for _ in range(3):
                    link(dve.tensor_tensor(rt[:, :], rs[:, :], rs[:, :], ALU.mult))
                    link(dve.tensor_tensor(rt[:, :], rt[:, :], ve[:, :], ALU.mult))
                    link(dve.tensor_scalar(rt[:, :], rt[:, :], -0.5, 1.5, ALU.mult, ALU.add))
                    link(dve.tensor_tensor(rs[:, :], rs[:, :], rt[:, :], ALU.mult))

            def norm(link, dst, src, between=None):
                for t in range(T):
                    ins = dve.bn_stats(st6[:, t, :], src(t))
                link(ins)
                if between:
                    between()
                for t in range(T):
                    ins = dve.bn_aggr(mv[:, t, :], st6[:, t, :])
                link(ins)
                rsqrt(link, EPS)
                for t in range(T):
                    ins = dve.tensor_scalar(dst(t), src(t), mv[:, t, 0:1], rs[:, t:t + 1], ALU.subtract, ALU.mult)
                return ins

            def ranks(x, m, into):
                k = [P, T, m, m]
                a, c = cmpa[:, :, 0:m, 0:m], cmpb[:, :, 0:m, 0:m]
                xi = x.unsqueeze(3).broadcast_to(k)
                xj = x.unsqueeze(2).broadcast_to(k)
                dve.tensor_tensor(a, xj, xi, ALU.is_gt)
                link(dve.tensor_tensor(c, xj, xi, ALU.is_equal))
                link(dve.tensor_tensor(c, c, tri[:, 0:m, 0:m].unsqueeze(1).broadcast_to(k), ALU.mult))
                link(dve.tensor_tensor(a, a, c, ALU.add))
                link(dve.tensor_reduce(into, a, AX.X, ALU.add))

            dve.memset(b2p[:, :], 0.0)
            dve.memset(wkS[:, :, :, 3 * GW:P], 0.0)
            dve.memset(wqS[:, :, :, 3 * GW:P], 0.0)
            dve.memset(Z[:, :, :, :].bitcast(F32), 0.0)
            dve.memset(qhi[:, :, :].bitcast(F32), 0.0)
            dve.memset(K4[:, :, :, :].bitcast(F32), 0.0)
            dve.wait_ge(zeroed, 1)
            dve.memset(rt[:, :], 0.0).then_inc(setup_sb, 1)
            def norm_slot(s):
                b = s % B
                dve.wait_ge(x_in[b], 16)
                norm(link, lambda t: xn[:, T * b + t, :], lambda t: X[:, T * b + t, :]).then_inc(xn_ready, 1)

            norm_slot(0)
            dve.wait_ge(setup_ps, 1)
            link(dve.tensor_copy(cols[:, :], ps[:, F, 0:ROWS]))
            dve.wait_ge(setup_ps, 2)
            dve.tensor_copy(ctxT[:, :, :, :], ps[:, F + 1, 0:B * S].rearrange("p (b k) -> p b k", b=B)
                            .unsqueeze(2).broadcast_to([P, B, 3, S]))
            dve.wait_ge(setup_ps, 3)
            link(dve.tensor_copy(wT[:, :, :], ps[:, F + 2, :].rearrange("p (i n) -> p i n", i=4)))
            kv0 = wkv0[:, :].rearrange("p (g h x) -> p g h x", g=G, h=HG)
            for g in range(G):
                rep = [P, 3, HG, HD]
                for dst, src in ((wkS[:, 0], kv0[:, g, :, 0:HD]),
                                 (wqS[:, 0], wq0[:, GW * g:GW * (g + 1)].rearrange("p (h d) -> p h d", h=HG)),
                                 (wkS[:, 1], wT[:, 1, GW * g:GW * (g + 1)].rearrange("p (h d) -> p h d", h=HG)),
                                 (wqS[:, 1], wT[:, 0, GW * g:GW * (g + 1)].rearrange("p (h d) -> p h d", h=HG))):
                    dve.tensor_copy(dst[:, g, 0:3 * GW].rearrange("p (r h d) -> p r h d", r=3, h=HG),
                                    src.unsqueeze(1).broadcast_to(rep))
            dve.tensor_copy(wv[:, 0, :].rearrange("p (g h d) -> p g h d", g=G, h=HG), kv0[:, :, :, HD:2 * HD])
            dve.tensor_copy(wv[:, 1, :], wT[:, 2, :])
            dve.tensor_copy(wp[:, 1, :], wT[:, 3, :])
            for l in range(L):
                ins = dve.tensor_copy(bvb[:, l, :], cols[:, R_BV + l:R_BV + l + 1].broadcast_to([P, P]))
            ins.then_inc(setup_sb, 1)
            for l in range(L):
                dve.wait_ge(setup_ps, 4 + l)
                dve.wait_ge(setup_act, 2 + l)
                for g in range(G):
                    ins = dve.scalar_tensor_tensor(out=kst[:, l, g, :], in0=ps[:, F + g, 0:B * S],
                                                   scalar=cols[:, R_BK + G * l + g:R_BK + G * l + g + 1],
                                                   in1=khi[:, g, :].bitcast(F32), op0=ALU.add, op1=ALU.subtract)
                ins.then_inc(setup_sb, 1)
            dve.wait_ge(setup_ps, 6)
            dve.wait_ge(setup_act, 1)
            for l in range(L):
                dve.tensor_scalar(wpx[:, l, :], wp[:, l, :], tg[:, l:l + 1], None, ALU.mult)
            link(dve.tensor_tensor(bpb[:, :, :], ps[:, F, 0:L * P].rearrange("p (l n) -> p l n", l=L), bpb[:, :, :], ALU.add))
            for l in range(L):
                ins = dve.tensor_scalar(bpx[:, l, :], bpb[:, l, :], tg[:, l:l + 1], None, ALU.mult)
            ins.then_inc(setup_sb, 1)
            dve.wait_ge(setup_sb, 5)
            link(dve.memset(qhi[2 * GW:3 * GW, :, :].bitcast(F32), 0.0))
            dve.wait_ge(consts, 1)

            def v_mask(s):
                dve.wait_ge(v_ps, s + 1)
                if s >= 2:
                    dve.wait_ge(pv_done, C * (s - 1))
                dve.tensor_tensor(V4[:, s % 2, :, :], ps[:, F + 1, 0:C * P].rearrange("p (c n) -> p c n", c=C),
                                  maskV[:, :, :], ALU.mult).then_inc(v_sb, 1)

            def z_rows(s, g):
                l = s // B
                dve.wait_ge(qh_sb, G * s + g + 1)
                if s >= 2:
                    dve.wait_ge(s_ps, G * C * (s - 1))
                dve.scalar_tensor_tensor(out=Z[0:3 * GW, s % 2, g, :], in0=ps[0:3 * GW, F + g, :],
                                         scalar=cols[0:3 * GW, R_BQ + G * l + g:R_BQ + G * l + g + 1],
                                         in1=qhi[0:3 * GW, g, :].bitcast(F32),
                                         op0=ALU.add, op1=ALU.subtract).then_inc(z_sb, 1)

            def maxima(s, t, half):
                dve.wait_ge(mx_ps, 2 * T * s + 2 * t + half + 1)
                src = ps[:, F + 2 * half:F + 2 * half + 2, 0:KG].rearrange("p g (h k) -> p g h k", h=HG)
                o = mpad[:, t, 3 * GW + 2 * HG * half:3 * GW + 2 * HG * (half + 1)].rearrange("p (g h) -> p g h", g=2)
                dve.tensor_reduce(o, src, AX.X, ALU.max).then_inc(mx_done, 1)

            def normalise(s):
                dve.wait_ge(pv_done, C * (s + 1))
                link(dve.reciprocal(rden[:, :], ps[:, D, :]))
                if s:
                    dve.wait_ge(proj_ps, s)
                dve.tensor_tensor(oT[:, :], ps[:, O, :], rden[:, :], ALU.mult).then_inc(ot_sb, 1)
                dve.wait_ge(ot_sb, s + 1)
                dve.tensor_copy(rt[:, :], rs[:, :]).then_inc(o_read, 1)

            def residual(s):
                l, b = divmod(s, B)
                xb = X[:, T * b:T * (b + 1), :]
                link(dve.tensor_tensor(xb, xb, bpx[:, l, :].unsqueeze(1).broadcast_to([P, T, P]), ALU.add))
                dve.wait_ge(proj_ps, s + 1)
                ins = dve.tensor_tensor(xb, xb, ps[:, F + 1, :].rearrange("p (t n) -> p t n", t=T), ALU.add)
                ins.then_inc(res_done, 1)

            def w1_lower(e):
                dve.wait_ge(w1h_done, e + 1)
                dve.scalar_tensor_tensor(out=w1l[:, e, :], in0=w1raw[:, e % 2, :], scalar=cols[:, R_LNG + e:R_LNG + e + 1],
                                         in1=w1h[:, e, :].bitcast(F32), op0=ALU.mult, op1=ALU.subtract).then_inc(w1_used, 1)

            def attention(l):
                s0 = l * B
                v_mask(s0)
                for g in range(G):
                    z_rows(s0, g)
                if l == 0:
                    norm_slot(1)
                for i in range(2 * T):
                    maxima(s0, i // 2, i % 2)
                for s in range(s0, s0 + B):
                    more = s + 1 < s0 + B
                    if l == 0 and s + 2 < B:
                        norm_slot(s + 2)
                    if more:
                        v_mask(s + 1)
                        for g in range(G):
                            z_rows(s + 1, g)
                        for i in range(6):
                            maxima(s + 1, i // 2, i % 2)
                    normalise(s)
                    if more:
                        maxima(s + 1, 3, 0)
                        maxima(s + 1, 3, 1)
                    residual(s)
                    if l == 0:
                        dve.wait_ge(b1_ps, s + 1)
                        j = 2 * FC * s
                        dve.tensor_tensor(b1p[:, j:j + 2 * FC], ps[:, F + 2, 0:2 * FC],
                                          cols[:, R_B1 + j:R_B1 + j + 2 * FC], ALU.add).then_inc(b1_sb, 1)
                        w1_lower(2 * s)
                        w1_lower(2 * s + 1)

            attention(0)

            for b in range(B):
                dve.wait_ge(res_done, b + 1)
                if b:
                    dve.wait_ge(xh_ps, b)
                    dve.wait_ge(b2_sb, b)
                norm(link, lambda t: xa[:, t, :], lambda t: X[:, T * b + t, :]).then_inc(xa_ready, 1)
                dve.wait_ge(xa_ready, b + 1)
                norm(link, lambda t: xh[:, t, :], lambda t: xa[:, t, :]).then_inc(xh_ready, 1)
                dve.wait_ge(xhh_sb, b + 1)
                dve.tensor_tensor(xhTl[:, Q * b:Q * (b + 1)], ps[:, F + 1, :], xhTh[:, Q * b:Q * (b + 1)].bitcast(F32),
                                  ALU.subtract).then_inc(xhl_sb, 1)
                dve.wait_ge(lg_ps, b + 1)
                link(dve.tensor_tensor(lg[:, :, :], ps[:, F + 2, 0:T * E].rearrange("p (t e) -> p t e", t=T),
                                       rb[:, :].unsqueeze(1).broadcast_to([P, T, E]), ALU.add))
                link(dve.tensor_reduce(t4[:, :], lg[:, :, :], AX.X, ALU.max))
                dve.tensor_tensor(lw[:, :, :], lg[:, :, :], t4[:, :].unsqueeze(2).broadcast_to([P, T, E]),
                                  ALU.subtract).then_inc(dif_sb, 1)
                ranks(lg[:, :, :], E, rank[:, :, :])
                link(dve.tensor_scalar(rank[:, :, :], rank[:, :, :], 2.0, None, ALU.is_lt))
                dve.wait_ge(ex_sb, b + 1)
                link(dve.tensor_tensor(ex[:, :, :], ex[:, :, :], rank[:, :, :], ALU.mult))
                link(dve.tensor_reduce(t4[:, :], ex[:, :, :], AX.X, ALU.add))
                link(dve.reciprocal(t4[:, :], t4[:, :]))
                link(dve.tensor_scalar(t4[:, :], t4[:, :], tg[:, 2:3], None, ALU.mult))
                link(dve.tensor_tensor(gate[:, b, :, :], ex[:, :, :], t4[:, :].unsqueeze(2).broadcast_to([P, T, E]), ALU.mult))
                if b:
                    dve.wait_ge(gt_ps, b)
                dve.tensor_copy(gpad[:, :, 0:E], gate[:, b, :, :]).then_inc(gp_sb, 1)
                link(dve.tensor_reduce(t4[:, :], gate[:, b, :, :], AX.X, ALU.add))
                for t in range(T):
                    x = X[:, T * b + t, :]
                    ins = dve.scalar_tensor_tensor(out=x, in0=xa[:, t, :], scalar=t4[:, t:t + 1], in1=x,
                                                   op0=ALU.mult, op1=ALU.add)
                link(ins)
                dve.wait_ge(b2_ps, b + 1)
                xb = X[:, T * b:T * (b + 1), :]
                dve.tensor_tensor(xb, xb, ps[:, F, :].rearrange("p (t n) -> p t n", t=T), ALU.add).then_inc(b2_sb, 1)
            dve.wait_ge(b2_sb, B)
            dve.memset(rt[:, :], 0.0).then_inc(dloop, 1)
            dve.wait_ge(dloop, 1)
            n_loop = [0]
            STEPS = 22
            dve.tensor_copy(rt[:, :], rs[:, :]).then_inc(y_used, 2)
            with dve.Fori(0, B) as b:
                n_loop[0] = 0

                def loop_link(ins):
                    n_loop[0] += 1
                    ins.then_inc(dloop, 1)
                    dve.wait_ge(dloop, b * STEPS + (n_loop[0] + 1))

                xb = X[:, bass.ds(b * T, T), :]
                dve.tensor_copy(gcur[:, :, :], gate[:, bass.ds(b, 1), :, :].rearrange("p o t e -> p (o t) e"))
                loop_link(dve.tensor_copy(acc[:, :, :], xb))
                for e in range(E):
                    dve.wait_ge(y_ps, b * E + (e + 3))
                    for t in range(T):
                        ins = dve.scalar_tensor_tensor(out=acc[:, t, :], in0=ps[:, YB + e % 2, P * t:P * (t + 1)],
                                                       scalar=gcur[:, t, e:e + 1], in1=acc[:, t, :],
                                                       op0=ALU.mult, op1=ALU.add)
                    ins.then_inc(y_used, 1)
                    if e + 1 < E:
                        dve.wait_ge(y_used, b * E + (e + 3))
                dve.wait_ge(y_used, b * E + (E + 2))
                dve.tensor_scalar(xb, acc[:, :, :], 1.0, None, ALU.mult)
                norm(loop_link, lambda t: xa[:, t, :], lambda t: acc[:, t, :],
                     lambda: dve.tensor_copy(rt[:, :], rs[:, :]))
                loop_link(dve.tensor_copy(rt[:, :], rs[:, :]))
                ins = dve.tensor_scalar(xn[:, bass.ds(b * T, T), :], xa[:, :, :], 1.0, None, ALU.mult)
                ins.then_inc(xn_ready, 1)
                loop_link(dve.tensor_copy(rt[:, :], rs[:, :]))
                while n_loop[0] < STEPS:
                    loop_link(dve.tensor_copy(rt[:, :], rs[:, :]))
                assert n_loop[0] == STEPS
            attention(1)
            dve.memset(cwT[:, :, :].bitcast(F32), 0.0)
            for b in range(B):
                dve.wait_ge(res_done, B + b + 1)
                norm(link, lambda t: xn[:, T * b + t, :], lambda t: X[:, T * b + t, :]).then_inc(n3_ready, 1)
                dve.wait_ge(l3_ps, b + 1)
                dve.tensor_scalar(lw[:, :, :], ps[:, F + 1, 0:T * E].rearrange("p (t e) -> p t e", t=T),
                                  -1.0, 88.0, ALU.mult, ALU.min).then_inc(l3_sb, 1)
                dve.wait_ge(e3_sb, b + 1)
                link(dve.tensor_scalar(ex[:, :, :], ex[:, :, :], 1.0, None, ALU.add))
                link(dve.reciprocal(ex[:, :, :], ex[:, :, :]))
                link(dve.tensor_tensor(lg[:, :, :], ex[:, :, :], cb[:, :].unsqueeze(1).broadcast_to([P, T, E]), ALU.add))
                two = lg[:, :, :].rearrange("p t (g e) -> p t g e", e=2)
                link(dve.tensor_tensor(gsc[:, :, :], two[:, :, :, 0], two[:, :, :, 1], ALU.add))
                ranks(gsc[:, :, :], E // 2, rank[:, :, 0:E // 2])
                link(dve.tensor_scalar(gsc[:, :, :], rank[:, :, 0:E // 2], 2.0, None, ALU.is_lt))
                link(dve.tensor_tensor(two, two, gsc[:, :, :].unsqueeze(3).broadcast_to([P, T, E // 2, 2]), ALU.mult))
                ranks(lg[:, :, :], E, rank[:, :, :])
                link(dve.tensor_scalar(rank[:, :, :], rank[:, :, :], 4.0, None, ALU.is_lt))
                link(dve.tensor_tensor(ex[:, :, :], ex[:, :, :], rank[:, :, :], ALU.mult))
                link(dve.tensor_reduce(t4[:, :], ex[:, :, :], AX.X, ALU.add))
                link(dve.tensor_scalar(t4[:, :], t4[:, :], 1e-20, None, ALU.add))
                link(dve.reciprocal(t4[:, :], t4[:, :]))
                link(dve.tensor_scalar(t4[:, :], t4[:, :], ROUTED_SCALE, None, ALU.mult))
                if b:
                    dve.wait_ge(c3_ps, b)
                dve.tensor_tensor(gpad[:, :, 0:E], ex[:, :, :], t4[:, :].unsqueeze(2).broadcast_to([P, T, E]),
                                  ALU.mult).then_inc(c3_sb, 1)
                dve.wait_ge(c3h_sb, b + 1)
                dve.tensor_tensor(cwT[32:32 + E, b, :], ps[0:E, F + 2, :], cwT[0:E, b, :].bitcast(F32),
                                  ALU.subtract).then_inc(c3l_sb, 1)
            for b in range(B):
                for a in range(PAIRS + 1):
                    i = b * (PAIRS + 1) + a
                    g0 = 3 * (i % 2)
                    dve.wait_ge(sg_sb, i + 1)
                    if b:
                        dve.wait_ge(y3_ps, b)
                    ins = dve.tensor_tensor(hT[:, a, :], sg[:, i % 2, :], ps[:, g0 + 1, :], ALU.mult)
                    if a < PAIRS:
                        link(ins)
                        ins = dve.tensor_tensor(hT[:, a, :], hT[:, a, :], ps[:, g0 + 2, :], ALU.mult)
                    ins.then_inc(h3_sb, 1)
                dve.wait_ge(y3_ps, b + 1)
                xb = X[:, T * b:T * (b + 1), :]
                dve.scalar_tensor_tensor(out=xb, in0=ps[:, 6 + b % 2, :].rearrange("p (t n) -> p t n", t=T),
                                         scalar=tg[:, 3:4], in1=xb, op0=ALU.mult, op1=ALU.add).then_inc(x_out, 1)


_INS = ["x", "ctx_1024", "g_xattn", "g_ffn", "L0_xattn_Wq", "L0_xattn_bq", "L0_xattn_Wkv", "L0_xattn_bkv",
        "L0_xattn_Wp", "L0_xattn_bp", "L0_ffn_router_W", "L0_ffn_router_b", "L0_ffn_ln_g", "L0_ffn_ln_b",
        "L0_ffn_W1", "L0_ffn_b1", "L0_ffn_W2", "L0_ffn_b2", "L1_xattn_wq", "L1_xattn_bq", "L1_xattn_wk",
        "L1_xattn_bk", "L1_xattn_wv", "L1_xattn_bv", "L1_xattn_wo", "L1_xattn_bo", "L1_ffn_gate_w",
        "L1_ffn_correction_bias", "L1_ffn_Wg", "L1_ffn_Wu", "L1_ffn_Wd", "L1_ffn_Wg_s", "L1_ffn_Wu_s",
        "L1_ffn_Wd_s"]


def kernel(**inputs):
    import numpy as np
    import concourse.bacc as bacc
    from concourse.bass_utils import run_bass_kernel_spmd

    nc = bacc.Bacc("TRN2", target_bir_lowering=False, num_devices=1)
    arrays, aps = {}, {}
    for name in _INS:
        a = np.ascontiguousarray(inputs[name])
        arrays[f"in_{name}"] = a
        aps[name] = nc.dram_tensor(f"in_{name}", a.shape, mybir.dt.from_np(a.dtype), kind="ExternalInput").ap()
    out = nc.dram_tensor("out", inputs["x"].shape, F32, kind="ExternalOutput").ap()
    build(nc, aps, out)
    r = run_bass_kernel_spmd(nc, [arrays], core_ids=[0])
    return r.results[0]["out"]
```

```python
import concourse.bass as bass
from concourse import mybir
from contextlib import ExitStack

F32 = mybir.dt.float32
F32R = mybir.dt.float32r
I32 = mybir.dt.int32
ALU = mybir.AluOpType
ACT = mybir.ActivationFunctionType
AX = mybir.AxisListType

HP = 64
P = 128
B = 4
T = 4
Q = T * P
L = 2
S = 77
HD = 8
G = 4
HG = 4
H = G * HG
GW = HG * HD
KG = HG * S
C = -(-KG // P)
E = 8
FF = 512
FC = FF // P
I1 = 64
PAIRS = E // 2
EPS = 1e-5
SCALE = 1.0 / float(HD) ** 0.5
ROUTED_SCALE = 2.5
RSQRT_GUESS = 0x5F3759DF
N = B * Q
R = N + P
NT = (2 * N + E * (P - 1)) // P
W1_AT, W2_AT, B1_AT, B2_AT = 0, FF, 2 * FF, 2 * FF + FC
WW = B2_AT + P

R_BK, R_BQ, R_BV, R_B1, R_LNG, R_LNB, R_GW = 0, 8, 16, 18, 50, 58, 66
ROWS = 74
CH = [(c * P) % S for c in range(C)]


def build(nc, I, out):
    ctx = ExitStack()
    with ctx:
        def sb(name, shape, dt=F32):
            return ctx.enter_context(nc.sbuf_tensor(name, shape, dt))

        def sem(name):
            return ctx.enter_context(nc.semaphore(name))

        X = sb("X", [P, B * T, P])
        xn = sb("xn", [P, B * T, P])
        ctx_sb = sb("ctx_sb", [S, B, P])
        rows = sb("rows", [ROWS, P])
        cols = sb("cols", [P, ROWS])
        wq0 = sb("wq0", [P, P])
        wkv0 = sb("wkv0", [P, 2 * P])
        wnat = sb("wnat", [P, 4, P])
        wT = sb("wT", [P, 4, P])
        wv = sb("wv", [P, L, P])
        wp = sb("wp", [P, L, P])
        wpx = sb("wpx", [P, L, P])
        wkS = sb("wkS", [P, L, G, P])
        wqS = sb("wqS", [P, L, G, P])
        gains = sb("gains", [P, 4])
        tg = sb("tg", [P, 4])
        bpb = sb("bpb", [P, L, P])
        bpx = sb("bpx", [P, L, P])
        bvb = sb("bvb", [P, L, P])
        rb = sb("rb", [P, E])
        cb = sb("cb", [P, E])
        rw = sb("rw", [P, E])
        w12 = sb("w12", [P, E, WW])
        wcur = sb("wcur", [P, 4, WW])
        wg1 = sb("wg1", [P, PAIRS + 1, P])
        wu1 = sb("wu1", [P, PAIRS + 1, P])
        wd1 = sb("wd1", [P, PAIRS + 1, P])
        ident = sb("ident", [P, P])
        maskK = sb("maskK", [P, G, HG])
        maskV = sb("maskV", [P, C, P])
        tri = {m: sb(f"tri{m}", [P, T, m, m]) for m in (E, E // 2)}
        pick = sb("pick", [P, PAIRS, P])
        pickr = sb("pickr", [P, PAIRS, P], F32R)
        ctxT = sb("ctxT", [P, B, 3, S])
        kst = sb("kst", [P, L, G, B * S])
        K4 = sb("K4", [P, 2, G, C * P], F32R)
        V4 = sb("V4", [P, 2, C, P])
        Z = sb("Z", [P, 2, G, Q], F32R)
        khi = Z[:, 1, :, 0:B * S]
        qf = sb("qf", [P, G, Q])
        xT = sb("xT", [P, Q])
        mpad = sb("mpad", [P, T, P])
        Pr = sb("Pr", [P, 2, G, Q])
        rden = sb("rden", [P, Q])
        oT = sb("oT", [P, Q])
        st6w = sb("st6w", [P, 3 * T, 6])
        mv = sb("mv", [P, 3 * T, 2])
        ve = sb("ve", [P, 3 * T])
        rs = sb("rs", [P, 3 * T])
        rt = sb("rt", [P, 3 * T])
        xa = sb("xa", [P, T, P])
        xh = sb("xh", [P, 2, T, P])
        xaT = sb("xaT", [P, Q])
        lg = sb("lg", [P, T, E])
        lw = sb("lw", [P, T, E])
        cmpa = sb("cmpa", [P, T * E * E])
        cmpb = sb("cmpb", [P, T * E * E])
        rank = sb("rank", [P, T, E])
        gsc = sb("gsc", [P, T, E // 2])
        l1 = sb("l1", [P, T])
        t4 = sb("t4", [P, T])
        e2 = sb("e2", [P, T])
        ex = sb("ex", [P, T, E])
        first = sb("first", [P, B, T, E])
        second = sb("second", [P, B, T, E])
        both = sb("both", [P, T, E])
        before = sb("before", [P, T + 1, E])
        place = sb("place", [P, B, T, E])
        w_first = sb("w_first", [P, B, T])
        w_second = sb("w_second", [P, B, T])
        rowF = sb("rowF", [P, 2, T])
        rowI = sb("rowI", [P, 2, B, T], I32)
        getF = sb("getF", [P, 2, B * T])
        getI = sb("getI", [P, 2, B * T], I32)
        wide = sb("wide", [P, B, T, E])
        earlier = sb("earlier", [P, P])
        ones = sb("ones", [P, P])
        zero = sb("zero", [P, P])
        regionI = sb("regionI", [P, E], I32)
        region = sb("region", [P, E])
        tileI = sb("tileI", [P, NT], I32)
        tileno = sb("tileno", [P, NT])
        count = sb("count", [P, E])
        tilesI = sb("tilesI", [P, E], I32)
        tiles = sb("tiles", [P, E])
        sumtri = sb("sumtri", [P, E, E])
        begin = sb("begin", [P, E])
        end = sb("end", [P, E])
        tailI = sb("tailI", [P, E], I32)
        past = sb("past", [P, NT, E])
        eT = sb("eT", [P, NT])
        sT = sb("sT", [P, NT])
        expertI = sb("expertI", [P, NT], I32)
        offsetI = sb("offsetI", [P, NT], I32)
        flatPr = Pr[:, :, :, :].rearrange("p s g q -> p (s g q)")
        xg = flatPr[:, 0:4 * P].rearrange("p (i n) -> p i n", i=4)
        yo = flatPr[:, 4 * P:8 * P].rearrange("p (i n) -> p i n", i=4)
        xgT = flatPr[:, 8 * P:10 * P].rearrange("p (i n) -> p i n", i=2)
        hid = flatPr[:, 10 * P:(10 + 2 * FC) * P].rearrange("p (i c n) -> p i c n", i=2, c=FC)
        flatW = wcur[:, :, :].rearrange("p i w -> p (i w)")
        y1 = flatW[:, 0:N].rearrange("p (t n) -> p t n", n=P)
        y2 = flatW[:, N:2 * N].rearrange("p (t n) -> p t n", n=P)
        cwT = sb("cwT", [P, B // 2, Q], F32R)
        w2flat = w12[:, :, :].rearrange("p e w -> p (e w)")
        part = lambda i, m, mem: mem[:, i * Q:(i + m) * Q].rearrange("p (a q) -> p a q", q=Q)
        x3T = part(0, B, w2flat)
        hT = part(B, 2 * (PAIRS + 1), w2flat)
        gpad = w2flat[:, 14 * Q:15 * Q].rearrange("p (t n) -> p t n", t=T)
        sg = part(0, 2, flatPr)

        ps = ctx.enter_context(nc.psum_tensor("ps", [P, 8, 512], F32))
        S0, O, D, F, RB = 0, 2, 3, 4, 7
        KB = (O, D, F + 2, RB)
        K1 = 3 * GW + H
        QB = (F, F + 2, F + 1, F)
        G3, U3, C3, Y3 = 0, F, F + 2, O
        TX, HB, YB = 0, 2, 4
        xs_dram = nc.dram_tensor("expert_rows", [(E + 1) * R, P], F32).ap()
        y_dram = nc.dram_tensor("expert_out", [NT * P, P], F32).ap()

        x_in = [sem(f"x_in{b}") for b in range(B)]
        ctx_in, rows_in, attw_in, attw1_in, small_in, w1_in, w2_in, b2_in, m1w_in = (sem(n) for n in (
            "ctx_in", "rows_in", "attw_in", "attw1_in", "small_in", "w1_in", "w2_in", "b2_in", "m1w_in"))
        zeroed = sem("zeroed")
        consts = sem("consts")
        cols_ps, ctx_ps, wt_ps, prep_sb, tg_sb, k_ps, kh_sb, k_sb, bv_ps, bpx_sb, wv_sb = (sem(n) for n in (
            "cols_ps", "ctx_ps", "wt_ps", "prep_sb", "tg_sb", "k_ps", "kh_sb", "k_sb", "bv_ps", "bpx_sb", "wv_sb"))
        xh_sb = sem("xh_sb")
        dstep, astep, pstep = sem("dstep"), sem("astep"), sem("pstep")
        xn_ready, xt_ps, xt_sb, v_ps, v_sb, q_ps, qh_sb, z_sb = (sem(n) for n in (
            "xn_ready", "xt_ps", "xt_sb", "v_ps", "v_sb", "q_ps", "qh_sb", "z_sb"))
        k4_ready, mx_ps, mx_done, mt_ps, mz_sb = (sem(n) for n in (
            "k4_ready", "mx_ps", "mx_done", "mt_ps", "mz_sb"))
        s_ps, p_sb, pv_done, ot_sb, proj_ps, res_done = (sem(n) for n in (
            "s_ps", "p_sb", "pv_done", "ot_sb", "proj_ps", "res_done"))
        b1_ps, b1_sb, w1_scaled, bias_sb = (sem(n) for n in ("b1_ps", "b1_sb", "w1_scaled", "bias_sb"))
        xa_ready, xa_ps, xa_sb, lg_ps, dif_sb, e2_sb, both_sb, place_ps, row_sb = (sem(n) for n in (
            "xa_ready", "xa_ps", "xa_sb", "lg_ps", "dif_sb", "e2_sb", "both_sb", "place_ps", "row_sb"))
        scattered = [sem(f"scattered{b}") for b in range(B)]
        idle_zero, tails_sp, tails_act = (sem(n) for n in ("idle_zero", "tails_sp", "tails_act"))
        count_ps, table_sb, get_sb = (sem(n) for n in ("count_ps", "table_sb", "get_sb"))
        xg_in = [sem(f"xg_in{i}") for i in range(4)]
        y_st = [sem(f"y_st{i}") for i in range(4)]
        t_ps, xg_sb, wc_sb, h_ps, a_sb, y_ps, yo_sb = (sem(n) for n in (
            "t_ps", "xg_sb", "wc_sb", "h_ps", "a_sb", "y_ps", "yo_sb"))
        gates_zero = sem("gates_zero")
        gathered = [sem(f"gathered{i}") for i in range(B)]
        combined = sem("combined")
        n3_ready, t3_ps, t3_sb, l3_ps, l3_sb, e3_sb, c3_sb, c3_ps, c3h_sb, c3l_sb = (sem(n) for n in (
            "n3_ready", "t3_ps", "t3_sb", "l3_ps", "l3_sb", "e3_sb", "c3_sb", "c3_ps", "c3h_sb", "c3l_sb"))
        g_ps, u_ps, c_ps, sg_sb, su_sb, h3_sb, y3_ps, x_out = (sem(n) for n in (
            "g_ps", "u_ps", "c_ps", "sg_sb", "su_sb", "h3_sb", "y3_ps", "x_out"))
        stored = sem("stored")

        LN = L * B
        block = ctx.enter_context(nc.Block())

        def tails(eng, experts, done):
            eng.wait_ge(table_sb, 1)
            for e in experts:
                row = eng.value_load(tailI[0:1, e:e + 1], min_val=0, max_val=E * R)
                eng.dma_start(xs_dram[bass.ds(row, P), :], zero[:, :]).then_inc(done, 16)

        @block.sync
        def _(sp):
            def load_x(b):
                sp.dma_start(X[:, T * b:T * (b + 1), :],
                             I["x"][b].rearrange("(t p) d -> p t d", p=P)).then_inc(x_in[b], 16)

            load_x(0)
            sp.dma_start(ctx_sb[:, :, :], I["ctx_1024"].rearrange("b k d -> k b d")).then_inc(ctx_in, 16)
            sp.dma_start(wkv0[:, :], I["L0_xattn_Wkv"]).then_inc(attw_in, 16)
            sp.dma_start(wq0[:, :], I["L0_xattn_Wq"]).then_inc(attw_in, 16)
            sp.dma_start(wp[:, 0, :], I["L0_xattn_Wp"]).then_inc(attw_in, 16)
            for b in range(1, B):
                load_x(b)
            for e in range(E):
                sp.dma_start(w12[:, e, W1_AT:W1_AT + FF], I["L0_ffn_W1"][e]).then_inc(w1_in, 16)
            for e in range(E):
                sp.dma_start(w12[:, e, W2_AT:W2_AT + FF].rearrange("p (c n) -> p c n", c=FC),
                             I["L0_ffn_W2"][e].rearrange("(c p) n -> p c n", p=P)).then_inc(w2_in, 16)
            sp.dma_start(w12[:, :, B2_AT:B2_AT + P],
                         I["L0_ffn_b2"].rearrange("(o e) n -> o e n", o=1).broadcast_to([P, E, P])).then_inc(b2_in, 16)
            sp.wait_ge(zeroed, 4)
            for w, name in ((wg1, "L1_ffn_Wg"), (wu1, "L1_ffn_Wu")):
                sp.dma_start(w[:, 0:PAIRS, :].rearrange("p a (e i) -> p (a e) i", e=2),
                             I[name].rearrange("e d i -> d e i")).then_inc(m1w_in, 16)
                sp.dma_start(w[:, PAIRS, 0:I1], I[name + "_s"]).then_inc(m1w_in, 16)
            for two in range(2):
                sp.dma_start(wd1[I1 * two:I1 * (two + 1), 0:PAIRS, :],
                             I["L1_ffn_Wd"].rearrange("(a e) i n -> e i a n", e=2)[two]).then_inc(m1w_in, 16)
            sp.dma_start(wd1[0:I1, PAIRS, :], I["L1_ffn_Wd_s"]).then_inc(m1w_in, 16)
            sp.wait_ge(consts, 1)
            sp.dma_start(xs_dram[E * R:E * R + P, :], zero[:, :]).then_inc(idle_zero, 16)
            tails(sp, range(0, E, 2), tails_sp)

            def load_tile(i, ring):
                row = sp.value_load(offsetI[0:1, bass.ds(i, 1)], min_val=0, max_val=E * R)
                sp.dma_start(xg[:, ring, :], xs_dram[bass.ds(row, P), :]).then_inc(xg_in[ring], 16)

            sp.wait_ge(table_sb, 1)
            for b in range(B):
                sp.wait_ge(scattered[b], 16 * 2 * T)
            sp.wait_ge(idle_zero, 16)
            sp.wait_ge(tails_sp, 16 * (E // 2))
            sp.wait_ge(tails_act, 16 * (E // 2))
            def store_tile(i, ring):
                sp.wait_ge(yo_sb, i + 1)
                sp.dma_start(y_dram[bass.ds(i * P, P), :], yo[:, ring, :]).then_inc(y_st[ring], 16)

            for i in range(4):
                load_tile(i, i)
            with sp.Fori(1, NT // 4) as k:
                for u in range(4):
                    sp.wait_ge(t_ps, k * 4 + (u - 3))
                    load_tile(k * 4 + u, u)
                    store_tile(k * 4 + (u - 4), u)
            for i in range(NT // 4 * 4, NT):
                sp.wait_ge(t_ps, i - 3)
                load_tile(i, i % 4)
                store_tile(i - 4, i % 4)
            for i in range(NT - 4, NT):
                store_tile(i, i % 4)
            for b in range(B):
                sp.wait_ge(x_out, b + 1)
                sp.dma_start(out[b].rearrange("(t p) d -> p t d", p=P),
                             X[:, T * b:T * (b + 1), :]).then_inc(stored, 16)
            sp.wait_ge(stored, 16 * B)

        M1W = 16 * 7

        @block.gpsimd
        def _(pool):
            n = [0]

            def link(ins):
                n[0] += 1
                ins.then_inc(pstep, 1)
                pool.wait_ge(pstep, n[0])

            pool.memset(rows[:, :], 0.0).then_inc(zeroed, 1)
            pool.wait_ge(zeroed, 1)
            pool.memset(rows[0:8, 3 * GW:P], -1.0).then_inc(zeroed, 1)
            link(pool.memset(ident[:, :], 0.0))
            link(pool.affine_select(out=ident[:, :], in_=ident[:, :], compare_op=ALU.not_equal, fill=1.0,
                                    base=0, pattern=[[-1, P]], channel_multiplier=1))
            link(pool.memset(wg1[:, PAIRS, I1:P], 0.0))
            link(pool.memset(wu1[:, PAIRS, I1:P], 0.0))
            pool.memset(wd1[I1:P, PAIRS, :], 0.0).then_inc(zeroed, 2)
            pool.wait_ge(zeroed, 4)
            link(pool.memset(maskK[:, :, :], 1.0))
            for r in range(3):
                m = maskK[GW * r:GW * (r + 1), :, :]
                link(pool.affine_select(out=m, in_=m, compare_op=ALU.is_ge, fill=0.0, base=0,
                                        pattern=[[0, G], [-HD, HG]], channel_multiplier=1))
                link(pool.affine_select(out=m, in_=m, compare_op=ALU.is_ge, fill=0.0, base=HD - 1,
                                        pattern=[[0, G], [HD, HG]], channel_multiplier=-1))
            m = maskK[3 * GW:P, :, :]
            link(pool.affine_select(out=m, in_=m, compare_op=ALU.is_equal, fill=0.0, base=0,
                                    pattern=[[-HG, G], [-1, HG]], channel_multiplier=1))
            link(pool.memset(maskV[:, :, :], 1.0))
            for c in range(C):
                m = maskV[:, c, :].rearrange("p (g h d) -> p g h d", g=G, h=HG)
                link(pool.affine_select(out=m, in_=m, compare_op=ALU.is_ge, fill=0.0, base=P * c,
                                        pattern=[[0, G], [-S, HG], [0, HD]], channel_multiplier=1))
                link(pool.affine_select(out=m, in_=m, compare_op=ALU.is_ge, fill=0.0, base=S - 1 - P * c,
                                        pattern=[[0, G], [S, HG], [0, HD]], channel_multiplier=-1))
            for m in (E, E // 2):
                link(pool.memset(tri[m][:, :, :, :], 1.0))
                link(pool.affine_select(out=tri[m][:, :, :, :], in_=tri[m][:, :, :, :], compare_op=ALU.is_gt, fill=0.0,
                                        base=0, pattern=[[0, T], [1, m], [-1, m]], channel_multiplier=0))
            link(pool.memset(ones[:, :], 1.0))
            link(pool.memset(zero[:, :], 0.0))
            link(pool.affine_select(out=earlier[:, :], in_=ones[:, :], compare_op=ALU.is_gt, fill=0.0, base=0,
                                    pattern=[[1, P]], channel_multiplier=-1))
            link(pool.iota(regionI[:, :], pattern=[[R, E]], base=0, channel_multiplier=0))
            link(pool.tensor_copy(region[:, :], regionI[:, :]))
            link(pool.iota(tileI[:, :], pattern=[[1, NT]], base=0, channel_multiplier=0))
            link(pool.tensor_copy(tileno[:, :], tileI[:, :]))
            link(pool.memset(before[:, 0, :], 0.0))
            link(pool.memset(pick[:, :, :], 0.0))
            for r in (0, 32, 64, 96):
                m = pick[r:r + E, :, :].rearrange("p a (e i) -> p a e i", e=2)
                link(pool.affine_select(out=m, in_=m, compare_op=ALU.not_equal, fill=1.0, base=0,
                                        pattern=[[-2, PAIRS], [-1, 2], [0, I1]], channel_multiplier=1))
            link(pool.memset(mpad[:, :, :], 0.0))
            pool.tensor_copy(pickr[:, :, :], pick[:, :, :]).then_inc(consts, 1)

            def keys(s):
                l, b = divmod(s, B)
                pool.wait_ge(k_sb, G * (l + 1))
                if s >= 2:
                    pool.wait_ge(s_ps, G * C * (s - 1))
                for g in range(G):
                    o = K4[:, s % 2, g, 0:KG].rearrange("p (h k) -> p h k", h=HG)
                    k = kst[:, l, g, S * b:S * (b + 1)]
                    pool.tensor_tensor(o, k.unsqueeze(1).broadcast_to([P, HG, S]),
                                       maskK[:, g, :].unsqueeze(2).broadcast_to([P, HG, S]),
                                       ALU.mult).then_inc(k4_ready, 1)
                pool.wait_ge(k4_ready, G * (s + 1))

            def add_bias(s):
                l, b = divmod(s, B)
                pool.wait_ge(bpx_sb, l + 1)
                pool.wait_ge(xn_ready, s + 1)
                xb = X[:, T * b:T * (b + 1), :]
                pool.tensor_tensor(xb, xb, bpx[:, l, :].unsqueeze(1).broadcast_to([P, T, P]), ALU.add).then_inc(bias_sb, 1)
                pool.wait_ge(bias_sb, s + 1)

            def q_lower(s, g):
                pool.wait_ge(qh_sb, G * s + g + 1)
                z = Z[GW:2 * GW, s % 2, g, :]
                pool.tensor_tensor(z, qf[GW:2 * GW, g, :], z.bitcast(F32), ALU.subtract).then_inc(z_sb, 1)
                pool.wait_ge(z_sb, G * s + g + 1)

            def scatter(b):
                for t in range(T):
                    if t == 0:
                        pool.wait_ge(row_sb, b + 1)
                    for k in range(2):
                        pool.indirect_dma_start(
                            out=xs_dram, in_=xh[:, b % 2, t, :], in_offset=None,
                            out_offset=bass.IndirectOffsetOnAxis(ap=rowI[:, k, b, t:t + 1], axis=0),
                        ).then_inc(scattered[b], 16)
                pool.wait_ge(scattered[b], 16 * 2 * T)

            keys(0)
            for g in range(G):
                q_lower(0, g)
            keys(1)
            add_bias(0)
            add_bias(1)
            for s in range(B):
                if s + 1 < B:
                    for g in range(G):
                        q_lower(s + 1, g)
                if s >= 2:
                    scatter(s - 2)
                if s + 2 < B:
                    add_bias(s + 2)
                    keys(s + 2)
            scatter(B - 2)
            scatter(B - 1)
            pool.memset(cwT[:, :, :].bitcast(F32), 0.0).then_inc(gates_zero, 1)
            pool.wait_ge(gates_zero, 1)
            keys(B)
            keys(B + 1)
            pool.wait_ge(get_sb, 1)
            for u in range(4):
                pool.wait_ge(y_st[u], 16 * len(range(u, NT, 4)))

            def gather(b):
                for t in range(T):
                    for k, dst in enumerate((y1, y2)):
                        pool.indirect_dma_start(
                            out=dst[:, T * b + t, :], in_=y_dram, out_offset=None,
                            in_offset=bass.IndirectOffsetOnAxis(ap=getI[:, k, T * b + t:T * b + t + 1], axis=0),
                        ).then_inc(gathered[b], 16)
                pool.wait_ge(gathered[b], 16 * 2 * T)

            gather(0)
            gather(1)
            for g in range(G):
                q_lower(B, g)
            add_bias(B)
            gather(2)
            add_bias(B + 1)
            for s in range(B, 2 * B - 1):
                for g in range(G):
                    q_lower(s + 1, g)
                if s == B:
                    gather(3)
                else:
                    add_bias(s + 1)
                if s + 2 < 2 * B:
                    keys(s + 2)

        @block.scalar
        def _(eng):
            eng.wait_ge(zeroed, 2)
            bkv = I["L0_xattn_bkv"].rearrange("(g h x) -> g h x", g=G, h=HG)
            for r in range(3):
                dst = slice(GW * r, GW * (r + 1))
                eng.dma_start(rows[R_BK:R_BK + G, dst].rearrange("g (h d) -> g h d", h=HG),
                              bkv[:, :, 0:HD]).then_inc(rows_in, 16)
            for at, n in ((R_BK + G, "L1_xattn_bk"), (R_BQ, "L0_xattn_bq"), (R_BQ + G, "L1_xattn_bq")):
                eng.dma_start(rows[at:at + G, 0:3 * GW].rearrange("g (r x) -> g r x", r=3),
                              I[n].rearrange("(g o x) -> g o x", g=G, o=1).broadcast_to([G, 3, GW])).then_inc(rows_in, 16)
            eng.dma_start(rows[R_BV:R_BV + 1, :].rearrange("o (h d) -> o h d", h=H),
                          I["L0_xattn_bkv"].rearrange("(o h x) -> o h x", o=1, h=H)[:, :, HD:2 * HD]).then_inc(rows_in, 16)
            eng.dma_start(rows[R_BV + 1:R_BV + 2, :], I["L1_xattn_bv"].rearrange("(o n) -> o n", o=1)).then_inc(rows_in, 16)
            eng.dma_start(rows[R_B1:R_B1 + E * FC, :], I["L0_ffn_b1"].rearrange("e (c p) -> (e c) p", p=P)).then_inc(rows_in, 16)
            eng.dma_start(rows[R_LNG:R_LNG + E, :], I["L0_ffn_ln_g"]).then_inc(rows_in, 16)
            eng.dma_start(rows[R_LNB:R_LNB + E, :], I["L0_ffn_ln_b"]).then_inc(rows_in, 16)
            eng.dma_start(rows[R_GW:R_GW + E, :], I["L1_ffn_gate_w"]).then_inc(rows_in, 16)
            for i, (n, j) in enumerate((("g_xattn", 0), ("g_ffn", 2))):
                eng.dma_start(gains[:, j:j + 2], I[n].rearrange("(o n) -> o n", o=1).broadcast_to([P, 2])).then_inc(small_in, 16)
            eng.dma_start(bpb[:, 0, :], I["L0_xattn_bp"].rearrange("(o n) -> o n", o=1).broadcast_to([P, P])).then_inc(small_in, 16)
            eng.dma_start(bpb[:, 1, :], I["L1_xattn_bo"].rearrange("(o n) -> o n", o=1).broadcast_to([P, P])).then_inc(small_in, 16)
            eng.dma_start(rb[:, :], I["L0_ffn_router_b"].rearrange("(o n) -> o n", o=1).broadcast_to([P, E])).then_inc(small_in, 16)
            eng.dma_start(cb[:, :], I["L1_ffn_correction_bias"].rearrange("(o n) -> o n", o=1).broadcast_to([P, E])).then_inc(small_in, 16)
            eng.dma_start(rw[:, :], I["L0_ffn_router_W"]).then_inc(small_in, 16)
            for i, n in enumerate(("wq", "wk", "wv", "wo")):
                eng.dma_start(wnat[:, i, :], I["L1_xattn_" + n]).then_inc(attw1_in, 16)
            eng.wait_ge(small_in, 16 * 7)
            eng.activation(tg[:, :], gains[:, :], ACT.Tanh).then_inc(tg_sb, 1)

            def key_rows(l):
                for g in range(G):
                    eng.wait_ge(k_ps, G * l + g + 1)
                    bias = cols[:, R_BK + G * l + g:R_BK + G * l + g + 1]
                    eng.activation(kst[:, l, g, :], ps[:, KB[g], 0:B * S], ACT.Identity, bias=bias)
                    third = slice(2 * GW, 3 * GW)
                    eng.activation(khi[third, g, :], ps[third, KB[g], 0:B * S], ACT.Identity,
                                   bias=bias[third]).then_inc(kh_sb, 1)

            key_rows(0)

            def x_copy(s):
                eng.wait_ge(xt_ps, s + 1)
                eng.activation(xT[:, :], ps[:, F, :], ACT.Copy).then_inc(xt_sb, 1)

            def q_upper(s, g):
                l = s // B
                eng.wait_ge(q_ps, G * s + g + 1)
                if s >= 2:
                    eng.wait_ge(s_ps, G * C * (s - 1))
                if s >= 1:
                    eng.wait_ge(z_sb, G * (s - 1) + g + 1)
                bias = cols[:, R_BQ + G * l + g:R_BQ + G * l + g + 1]
                eng.activation(Z[0:3 * GW, s % 2, g, :], ps[0:3 * GW, QB[g], :], ACT.Identity, bias=bias[0:3 * GW])
                eng.activation(qf[GW:2 * GW, g, :], ps[GW:2 * GW, QB[g], :], ACT.Identity,
                               bias=bias[GW:2 * GW]).then_inc(qh_sb, 1)

            def m_rows(s):
                eng.wait_ge(mt_ps, s + 1)
                if s >= 2:
                    eng.wait_ge(s_ps, G * C * (s - 1))
                eng.activation(Z[3 * GW:3 * GW + H, s % 2, :, :],
                               ps[3 * GW:3 * GW + H, F, :].unsqueeze(1).broadcast_to([H, G, Q]),
                               ACT.Copy).then_inc(mz_sb, 1)

            def exps(s, c, g):
                i = G * C * s + G * c + g
                n = C * s + c
                eng.wait_ge(s_ps, i + 1)
                if n >= 2 and g == 0:
                    eng.wait_ge(pv_done, n - 1)
                eng.activation(Pr[:, n % 2, g, :], ps[:, S0 + i % 2, :], ACT.Exp, scale=SCALE).then_inc(p_sb, 1)

            def route_copy(b):
                eng.wait_ge(xa_ps, b + 1)
                eng.activation(xaT[:, :], ps[:, RB, :], ACT.Copy).then_inc(xa_sb, 1)

            def route_exp(b):
                eng.wait_ge(dif_sb, b + 1)
                eng.activation(e2[:, :], t4[:, :], ACT.Exp).then_inc(e2_sb, 1)

            def scale_w1(s):
                eng.wait_ge(b1_ps, s + 1)
                for e in (2 * s, 2 * s + 1):
                    w = w12[:, e, W1_AT:W1_AT + FF]
                    eng.activation(w, w, ACT.Copy, scale=cols[:, R_LNG + e:R_LNG + e + 1]).then_inc(w1_scaled, 1)

            def mix_copy(b):
                eng.wait_ge(t3_ps, b + 1)
                eng.activation(x3T[:, b, :], ps[:, RB, :], ACT.Copy).then_inc(t3_sb, 1)

            def mix_exp(b):
                eng.wait_ge(l3_sb, b + 1)
                eng.activation(ex[:, :, :], lw[:, :, :], ACT.Exp).then_inc(e3_sb, 1)

            def mix_gates(b):
                eng.wait_ge(c3_ps, b + 1)
                at = b % 2 * HP
                eng.activation(cwT[at:at + E, b // 2, :], ps[at:at + E, RB, :], ACT.Copy).then_inc(c3h_sb, 1)

            def mix_silu(i):
                eng.wait_ge(g_ps, i + 1)
                if i >= 2:
                    eng.wait_ge(su_sb, i - 1)
                eng.activation(sg[:, i % 2, :], ps[:, G3 + i % 2, :], ACT.Silu).then_inc(sg_sb, 1)

            def attention(l):
                s0 = l * B
                x_copy(s0)
                for g in range(G):
                    q_upper(s0, g)
                m_rows(s0)
                for s in range(s0, s0 + B):
                    more, prev = s + 1 < s0 + B, s > s0
                    p = s - s0 - 1
                    for i in range(G * C):
                        exps(s, i // G, i % G)
                        if more and i == 1:
                            x_copy(s + 1)
                        if more and i == 3:
                            q_upper(s + 1, 0)
                            q_upper(s + 1, 1)
                        if more and i == 5:
                            q_upper(s + 1, 2)
                            q_upper(s + 1, 3)
                        if l == 1 and s >= s0 + 2 and i == 7:
                            mix_gates(s - s0 - 2)
                        if prev and i == 8:
                            (route_copy if l == 0 else mix_copy)(p)
                    if more:
                        m_rows(s + 1)
                    if l == 0:
                        if prev:
                            route_exp(p)
                        scale_w1(s)
                    elif prev:
                        mix_exp(p)

            attention(0)
            route_copy(B - 1)
            route_exp(B - 1)
            tails(eng, range(1, E, 2), tails_act)
            key_rows(1)

            def gelu(i, par, ring):
                eng.wait_ge(h_ps, i + 1)
                if not isinstance(i, int) or i >= 2:
                    eng.wait_ge(y_ps, i - 1)
                for c in range(FC):
                    ins = eng.activation(hid[:, par, c, :], ps[:, HB + par, P * c:P * (c + 1)], ACT.Gelu,
                                         bias=wcur[:, ring, B1_AT + c:B1_AT + c + 1])
                ins.then_inc(a_sb, 1)

            gelu(0, 0, 0)
            with eng.Fori(0, (NT - 3) // 4) as k:
                for u in range(1, 5):
                    gelu(k * 4 + u, u % 2, u % 4)
            gelu(NT - 2, (NT - 2) % 2, (NT - 2) % 4)
            gelu(NT - 1, (NT - 1) % 2, (NT - 1) % 4)
            attention(1)
            PA = PAIRS + 1
            for i in range(B * PA):
                mix_silu(i)
                if i == 3:
                    mix_gates(B - 2)
                if i == 4:
                    mix_copy(B - 1)
                if i == 5:
                    mix_exp(B - 1)
                if i == 7:
                    mix_gates(B - 1)

        @block.tensor
        def _(pe):
            def mm(o, w, x, start=True, stop=True):
                return nc.tensor.matmul(o, w, x, start=start, stop=stop)

            pe.wait_ge(pstep, 2)
            pe.wait_ge(rows_in, 16 * 12)
            nc.tensor.transpose(ps[:, F, 0:ROWS], rows[:, :], ident[0:ROWS, 0:ROWS]).then_inc(cols_ps, 1)
            pe.wait_ge(ctx_in, 16)
            for b in range(B):
                ins = nc.tensor.transpose(ps[:, F + 1, S * b:S * (b + 1)], ctx_sb[:, b, :], ident[0:S, 0:S])
            ins.then_inc(ctx_ps, 1)

            def key_products(l):
                pe.wait_ge(prep_sb, l + 1)
                for g in range(G):
                    mm(ps[:, KB[g], 0:B * S], wkS[:, l, g, :], ctxT[:, :, 0, :]).then_inc(k_ps, 1)
                mm(ps[:, S0, 0:P], bvb[:, l, :], wp[:, l, :]).then_inc(bv_ps, 1)
                pe.wait_ge(kh_sb, G * (l + 1))
                pe.wait_ge(bpx_sb, l + 1)

            key_products(0)

            def front_x(s):
                pe.wait_ge(xn_ready, s + 1)
                if s % B:
                    pe.wait_ge(mz_sb, s)
                for t in range(T):
                    ins = nc.tensor.transpose(ps[:, F, P * t:P * (t + 1)], xn[:, T * (s % B) + t, :], ident[:, :])
                ins.then_inc(xt_ps, 1)

            def front_v(s):
                l, b = divmod(s, B)
                pe.wait_ge(wv_sb, l + 1)
                rep = ctxT[:, b, :, :].rearrange("p r k -> p (r k)")
                for c in range(C):
                    ins = mm(ps[:, F + 1, P * c:P * (c + 1)], rep[:, CH[c]:CH[c] + P], wv[:, l, :])
                ins.then_inc(v_ps, 1)

            def front_q(s, g):
                l = s // B
                if g == 0:
                    pe.wait_ge(xt_sb, s + 1)
                if g == 1 and 2 <= s < B:
                    pe.wait_ge(b1_sb, s - 1)
                if g == 2:
                    pe.wait_ge(v_sb, s + 1)
                if g == 3:
                    pe.wait_ge(qh_sb, G * s + 1)
                mm(ps[:, QB[g], :], wqS[:, l, g, :], xT[:, :]).then_inc(q_ps, 1)

            def front_mx(s, t):
                for g in range(G):
                    j = G * t + g
                    if t == 0:
                        pe.wait_ge(k4_ready, G * s + g + 1)
                    if t == 0:
                        pe.wait_ge(z_sb, G * s + g + 1)
                    if j < 3:
                        pe.wait_ge(qh_sb, G * (s + 1))
                    else:
                        pe.wait_ge(mx_done, T * G * s + j - 2)
                    mm(ps[:, F + j % 3, 0:KG], Z[0:3 * GW, s % 2, g, P * t:P * (t + 1)],
                       K4[0:3 * GW, s % 2, g, 0:KG]).then_inc(mx_ps, 1)

            def front_m(s):
                pe.wait_ge(mx_done, T * G * (s + 1))
                for t in range(T):
                    ins = mm(ps[:, F, P * t:P * (t + 1)], mpad[:, t, :], ident[:, :])
                ins.then_inc(mt_ps, 1)

            def scores(s, c, g):
                i = G * C * s + G * c + g
                if c == 0 and g == 0:
                    pe.wait_ge(mz_sb, s + 1)
                if i >= 2:
                    pe.wait_ge(p_sb, i - 1)
                mm(ps[:, S0 + i % 2, :], K4[0:K1, s % 2, g, P * c:P * (c + 1)],
                   Z[0:K1, s % 2, g, :]).then_inc(s_ps, 1)

            def pv(s, c):
                n = C * s + c
                pe.wait_ge(p_sb, G * (n + 1))
                if c == 0:
                    pe.wait_ge(v_sb, s + 1)
                    if s:
                        pe.wait_ge(res_done, s)
                for bank, w in ((O, V4[:, s % 2, c, :]), (D, maskV[:, c, :])):
                    for g in range(G):
                        cols_g = slice(GW * g, GW * (g + 1))
                        ins = nc.tensor.matmul(ps[cols_g, bank, :], w[:, cols_g], Pr[:, n % 2, g, :],
                                               start=c == 0, stop=c == C - 1, tile_position=(0, GW * g))
                ins.then_inc(pv_done, 1)

            def w1_bias(s):
                pe.wait_ge(mx_done, T * G * min(s + 2, B))
                pe.wait_ge(w1_in, 16 * E)
                for e in (2 * s, 2 * s + 1):
                    for c in range(FC):
                        i = FC * (e % 2) + c
                        ins = mm(ps[:, F + 2, i:i + 1], w12[:, e, W1_AT + P * c:W1_AT + P * (c + 1)], cols[:, R_LNB + e:R_LNB + e + 1])
                ins.then_inc(b1_ps, 1)

            def project(s):
                pe.wait_ge(ot_sb, s + 1)
                for t in range(T):
                    ins = mm(ps[:, D, P * t:P * (t + 1)], oT[:, P * t:P * (t + 1)], wpx[:, s // B, :])
                ins.then_inc(proj_ps, 1)

            def transposed(bank, src, done):
                for t in range(T):
                    ins = nc.tensor.transpose(ps[:, bank, P * t:P * (t + 1)], src(t), ident[:, :])
                ins.then_inc(done, 1)

            def route_x(b):
                pe.wait_ge(xa_ready, b + 1)
                if b:
                    pe.wait_ge(row_sb, b)
                transposed(RB, lambda t: xa[:, t, :], xa_ps)

            def route_logits(b):
                pe.wait_ge(xa_sb, b + 1)
                for t in range(T):
                    ins = mm(ps[:, RB, E * t:E * (t + 1)], xaT[:, P * t:P * (t + 1)], rw[:, :])
                ins.then_inc(lg_ps, 1)

            def route_places(b):
                pe.wait_ge(both_sb, b + 1)
                mm(ps[:, RB, 0:T * E], earlier[:, :], both[:, :, :].rearrange("p t e -> p (t e)"), True, False)
                mm(ps[:, RB, 0:T * E], ones[:, :], before[:, 0:T, :].rearrange("p t e -> p (t e)"),
                   False, True).then_inc(place_ps, 1)

            def mix_x(b):
                pe.wait_ge(n3_ready, b + 1)
                if b:
                    pe.wait_ge(c3l_sb, b)
                else:
                    pe.wait_ge(get_sb, 1)
                transposed(RB, lambda t: xn[:, T * b + t, :], t3_ps)

            def mix_logits(b):
                pe.wait_ge(t3_sb, b + 1)
                for t in range(T):
                    ins = mm(ps[:, RB, E * t:E * (t + 1)], x3T[:, b, P * t:P * (t + 1)], cols[:, R_GW:R_GW + E])
                ins.then_inc(l3_ps, 1)

            def mix_gates(b):
                pe.wait_ge(c3_sb, b + 1)
                transposed(RB, lambda t: gpad[:, t, :], c3_ps)

            def mix_pair(i):
                b, a = divmod(i, PAIRS + 1)
                if i >= 2:
                    pe.wait_ge(sg_sb, i - 1)
                mm(ps[:, G3 + i % 2, :], wg1[:, a, :], x3T[:, b, :]).then_inc(g_ps, 1)
                if i >= 2:
                    pe.wait_ge(su_sb, i - 1)
                mm(ps[:, U3 + i % 2, :], wu1[:, a, :], x3T[:, b, :]).then_inc(u_ps, 1)
                if a < PAIRS:
                    if a == 0:
                        pe.wait_ge(c3l_sb, b + 1)
                    if i:
                        pe.wait_ge(h3_sb, i)
                    half = slice(b % 2 * HP, b % 2 * HP + HP)
                    mm(ps[:, C3, :], pickr[half, a, :], cwT[half, b // 2, :]).then_inc(c_ps, 1)

            def mix_out(b):
                pe.wait_ge(h3_sb, (b + 1) * (PAIRS + 1))
                if b >= 2:
                    pe.wait_ge(x_out, b - 1)
                for t in range(T):
                    for a in range(PAIRS + 1):
                        ins = mm(ps[:, Y3 + b % 2, P * t:P * (t + 1)], hT[:, b % 2 * (PAIRS + 1) + a, P * t:P * (t + 1)],
                                 wd1[:, a, :], a == 0, a == PAIRS)
                ins.then_inc(y3_ps, 1)

            def attention(l):
                s0 = l * B
                front_x(s0)
                front_v(s0)
                for g in range(G):
                    front_q(s0, g)
                for t in range(T):
                    front_mx(s0, t)
                front_m(s0)
                for s in range(s0, s0 + B):
                    n, more, prev = s + 1, s + 1 < s0 + B, s > s0
                    p = s - s0 - 1
                    scores(s, 0, 0)
                    scores(s, 0, 1)
                    if more:
                        front_x(n)
                    scores(s, 0, 2)
                    scores(s, 0, 3)
                    if more:
                        front_v(n)
                        front_q(n, 0)
                    if prev:
                        project(s - 1)
                    if more:
                        front_q(n, 1)
                    scores(s, 1, 0)
                    scores(s, 1, 1)
                    if more:
                        front_q(n, 2)
                        front_q(n, 3)
                    pv(s, 0)
                    if l == 1 and s >= s0 + 2:
                        mix_gates(s - s0 - 2)
                    scores(s, 1, 2)
                    scores(s, 1, 3)
                    if more:
                        front_mx(n, 0)
                    if prev:
                        (route_x if l == 0 else mix_x)(p)
                    scores(s, 2, 0)
                    if more:
                        front_mx(n, 1)
                    scores(s, 2, 1)
                    pv(s, 1)
                    if more:
                        front_mx(n, 2)
                    if prev:
                        (route_logits if l == 0 else mix_logits)(p)
                    scores(s, 2, 2)
                    if more:
                        front_mx(n, 3)
                    scores(s, 2, 3)
                    if more:
                        front_m(n)
                    pv(s, 2)
                    if l == 0 and prev:
                        route_places(p)
                    if l == 0:
                        w1_bias(s)

            attention(0)
            project(B - 1)
            route_x(B - 1)
            route_logits(B - 1)
            route_places(B - 1)
            pe.wait_ge(row_sb, B)
            mm(ps[:, RB, 0:E], ones[:, :], before[:, T, :]).then_inc(count_ps, 1)
            pe.wait_ge(attw1_in, 16 * 4)
            pe.wait_ge(res_done, B)
            for i in range(4):
                ins = nc.tensor.transpose(ps[:, F + 1, P * i:P * (i + 1)], wnat[:, i, :], ident[:, :])
            ins.then_inc(wt_ps, 1)
            key_products(1)

            def tile_x(i, par, ring, turn):
                pe.wait_ge(xg_in[ring], (turn + 1) * 16)
                if not isinstance(i, int) or i >= 2:
                    pe.wait_ge(xg_sb, i - 1)
                nc.tensor.transpose(ps[:, TX + par, 0:P], xg[:, ring, :], ident[:, :]).then_inc(t_ps, 1)

            def tile_hidden(i, par, ring):
                pe.wait_ge(xg_sb, i + 1)
                pe.wait_ge(wc_sb, i + 1)
                if not isinstance(i, int) or i >= 2:
                    pe.wait_ge(a_sb, i - 1)
                for c in range(FC):
                    ins = mm(ps[:, HB + par, P * c:P * (c + 1)], wcur[:, ring, W1_AT + P * c:W1_AT + P * (c + 1)],
                             xgT[:, par, :])
                ins.then_inc(h_ps, 1)

            def tile_out(i, par, ring):
                pe.wait_ge(a_sb, i + 1)
                if not isinstance(i, int) or i >= 2:
                    pe.wait_ge(yo_sb, i - 1)
                for c in range(FC):
                    ins = mm(ps[:, YB + par, 0:P], hid[:, par, c, :],
                             wcur[:, ring, W2_AT + P * c:W2_AT + P * (c + 1)], c == 0, c == FC - 1)
                ins.then_inc(y_ps, 1)

            tile_x(0, 0, 0, 0)
            tile_x(1, 1, 1, 0)
            tile_hidden(0, 0, 0)
            for u in range(1, 5):
                tile_x(u + 1, (u + 1) % 2, (u + 1) % 4, (u + 1) // 4)
                tile_hidden(u, u % 2, u % 4)
                tile_out(u - 1, (u - 1) % 2, (u - 1) % 4)
            with pe.Fori(1, (NT - 3) // 4) as k:
                for u in range(1, 5):
                    tile_x(k * 4 + (u + 1), (u + 1) % 2, (u + 1) % 4, k + (u + 1) // 4)
                    tile_hidden(k * 4 + u, u % 2, u % 4)
                    tile_out(k * 4 + (u - 1), (u - 1) % 2, (u - 1) % 4)
            i = NT - 2
            tile_x(i + 1, (i + 1) % 2, (i + 1) % 4, (i + 1) // 4)
            tile_hidden(i, i % 2, i % 4)
            tile_out(i - 1, (i - 1) % 2, (i - 1) % 4)
            i = NT - 1
            tile_hidden(i, i % 2, i % 4)
            tile_out(i - 1, (i - 1) % 2, (i - 1) % 4)
            tile_out(i, i % 2, i % 4)
            pe.wait_ge(yo_sb, NT)
            attention(1)
            PA = PAIRS + 1
            pe.wait_ge(m1w_in, M1W)
            pe.wait_ge(p_sb, G * C * LN)
            for i in range(B * PA):
                mix_pair(i)
                if i == 0:
                    project(LN - 1)
                if i == 3:
                    mix_gates(B - 2)
                if i == 4:
                    mix_x(B - 1)
                if i == 5:
                    mix_logits(B - 1)
                    pe.wait_ge(res_done, LN)
                if i == 7:
                    mix_gates(B - 1)
                if i and i % PA == 0:
                    mix_out(i // PA - 1)
            mix_out(B - 1)

        @block.vector
        def _(dve):
            n = [0]

            def link(ins):
                n[0] += 1
                ins.then_inc(dstep, 1)
                dve.wait_ge(dstep, n[0])

            def rsqrt(m):
                v, y, t = ve[:, 0:m], rs[:, 0:m], rt[:, 0:m]
                link(dve.tensor_scalar(y.bitcast(I32), v.bitcast(I32), -0.5, float(RSQRT_GUESS),
                                       ALU.mult, ALU.add))
                for _ in range(3):
                    link(dve.scalar_tensor_tensor(out=t, in0=y, scalar=-0.5, in1=y, op0=ALU.mult, op1=ALU.mult))
                    link(dve.tensor_tensor(t, t, v, ALU.mult))
                    link(dve.scalar_tensor_tensor(out=y, in0=t, scalar=1.5, in1=y, op0=ALU.add, op1=ALU.mult))

            def moments(m, src):
                for t in range(m):
                    ins = dve.bn_stats(st6w[:, t, :], src(t))
                link(ins)
                for t in range(m):
                    ins = dve.bn_aggr(mv[:, t, :], st6w[:, t, :])
                link(ins)
                link(dve.tensor_scalar(ve[:, 0:m], mv[:, 0:m, 1], EPS, None, ALU.add))

            def scaled(m, dst, src, at=0):
                for t in range(m):
                    ins = dve.tensor_scalar(dst(t), src(t), mv[:, t, 0:1], rs[:, at + t:at + t + 1], ALU.subtract, ALU.mult)
                return ins

            def norm(m, dst, src):
                moments(m, src)
                rsqrt(m)
                return scaled(m, dst, src)

            def ranks(x, m, into):
                k = [P, T, m, m]
                a, c = cmpa[:, 0:T * m * m], cmpb[:, 0:T * m * m]
                shaped = a.rearrange("p (t i j) -> p t i j", t=T, i=m)
                link(dve.tensor_tensor(shaped, x.unsqueeze(2).broadcast_to(k), x.unsqueeze(3).broadcast_to(k), ALU.subtract))
                link(dve.scalar_tensor_tensor(out=c, in0=a, scalar=0.0, in1=tri[m][:, :, :, :].rearrange("p t i j -> p (t i j)"),
                                              op0=ALU.is_ge, op1=ALU.mult))
                link(dve.scalar_tensor_tensor(out=a, in0=a, scalar=0.0, in1=c, op0=ALU.is_gt, op1=ALU.max))
                link(dve.tensor_reduce(into, shaped, AX.X, ALU.add))

            dve.memset(wkS[:, :, :, 3 * GW:P], 0.0)
            dve.memset(wqS[:, :, :, 3 * GW:P], 0.0)
            link(dve.memset(K4[:, :, :, KG:C * P].bitcast(F32), 0.0))
            dve.wait_ge(x_in[0], 16)
            norm(T, lambda t: xn[:, t, :], lambda t: X[:, t, :]).then_inc(xn_ready, 1)
            for b in range(1, B):
                dve.wait_ge(x_in[b], 16)
            norm(3 * T, lambda t: xn[:, T + t, :], lambda t: X[:, T + t, :]).then_inc(xn_ready, 3)
            dve.wait_ge(cols_ps, 1)
            link(dve.tensor_copy(cols[:, :], ps[:, F, 0:ROWS]))
            dve.wait_ge(ctx_ps, 1)
            dve.tensor_copy(ctxT[:, :, :, :], ps[:, F + 1, 0:B * S].rearrange("p (b k) -> p b k", b=B)
                            .unsqueeze(2).broadcast_to([P, B, 3, S]))
            dve.wait_ge(attw_in, 16 * 3)
            kv0 = wkv0[:, :].rearrange("p (g h x) -> p g h x", g=G, h=HG)

            def stack(l, wk, wq):
                for dst, src in ((wkS, wk), (wqS, wq)):
                    for g in range(G):
                        dve.tensor_copy(dst[:, l, g, 0:3 * GW].rearrange("p (r h d) -> p r h d", r=3, h=HG),
                                        src(g).unsqueeze(1).broadcast_to([P, 3, HG, HD]))
                return dve.tensor_copy(bvb[:, l, :], cols[:, R_BV + l:R_BV + l + 1].broadcast_to([P, P]))

            def lower_keys(l):
                for g in range(G):
                    dve.wait_ge(kh_sb, G * l + g + 1)
                    k = kst[2 * GW:3 * GW, l, g, :]
                    dve.tensor_tensor(k, k, khi[2 * GW:3 * GW, g, :].bitcast(F32), ALU.subtract).then_inc(k_sb, 1)
                dve.wait_ge(tg_sb, 1)
                dve.tensor_scalar(wpx[:, l, :], wp[:, l, :], tg[:, l:l + 1], None, ALU.mult)
                dve.wait_ge(bv_ps, l + 1)
                link(dve.tensor_tensor(bpb[:, l, :], ps[:, S0, 0:P], bpb[:, l, :], ALU.add))
                dve.tensor_scalar(bpx[:, l, :], bpb[:, l, :], tg[:, l:l + 1], None, ALU.mult).then_inc(bpx_sb, 1)

            stack(0, lambda g: kv0[:, g, :, 0:HD],
                  lambda g: wq0[:, GW * g:GW * (g + 1)].rearrange("p (h d) -> p h d", h=HG)).then_inc(prep_sb, 1)
            dve.tensor_copy(wv[:, 0, :].rearrange("p (g h d) -> p g h d", g=G, h=HG), kv0[:, :, :, HD:2 * HD]).then_inc(wv_sb, 1)
            lower_keys(0)
            dve.wait_ge(consts, 1)

            def v_mask(s):
                dve.wait_ge(v_ps, s + 1)
                if s >= 2:
                    dve.wait_ge(pv_done, C * (s - 1))
                dve.tensor_tensor(V4[:, s % 2, :, :], ps[:, F + 1, 0:C * P].rearrange("p (c n) -> p c n", c=C),
                                  maskV[:, :, :], ALU.mult).then_inc(v_sb, 1)

            def maxima(s, t):
                for g in range(G):
                    j = G * t + g
                    dve.wait_ge(mx_ps, T * G * s + j + 1)
                    at = 3 * GW + HG * g
                    dve.tensor_reduce(mpad[:, t, at:at + HG], ps[:, F + j % 3, 0:KG].rearrange("p (h k) -> p h k", h=HG),
                                      AX.X, ALU.max).then_inc(mx_done, 1)

            def normalise(s):
                dve.wait_ge(pv_done, C * (s + 1))
                link(dve.reciprocal(rden[:, :], ps[:, D, :]))
                if s:
                    dve.wait_ge(proj_ps, s)
                dve.tensor_tensor(oT[:, :], ps[:, O, :], rden[:, :], ALU.mult).then_inc(ot_sb, 1)

            def residual(s):
                l, b = divmod(s, B)
                xb = X[:, T * b:T * (b + 1), :]
                dve.wait_ge(proj_ps, s + 1)
                dve.wait_ge(bias_sb, s + 1)
                ins = dve.tensor_tensor(xb, xb, ps[:, D, :].rearrange("p (t n) -> p t n", t=T), ALU.add)
                ins.then_inc(res_done, 1)

            def b1_copy(s):
                dve.wait_ge(b1_ps, s + 1)
                j = R_B1 + 2 * FC * s
                dve.tensor_tensor(w12[:, 2 * s:2 * s + 2, B1_AT:B1_AT + FC],
                                  ps[:, F + 2, 0:2 * FC].rearrange("p (e c) -> p e c", e=2),
                                  cols[:, j:j + 2 * FC].rearrange("p (e c) -> p e c", e=2), ALU.add).then_inc(b1_sb, 1)

            def route_norms(b):
                dve.wait_ge(res_done, b + 1)
                if b >= 2:
                    dve.wait_ge(scattered[b - 2], 16 * 2 * T)
                moments(T, lambda t: X[:, T * b + t, :])
                link(dve.scalar_tensor_tensor(out=ve[:, T:2 * T], in0=ve[:, 0:T], scalar=EPS, in1=mv[:, 0:T, 1],
                                              op0=ALU.mult, op1=ALU.add))
                rsqrt(2 * T)
                scaled(T, lambda t: xa[:, t, :], lambda t: X[:, T * b + t, :]).then_inc(xa_ready, 1)
                link(scaled(T, lambda t: xh[:, b % 2, t, :], lambda t: X[:, T * b + t, :], T))
                xb = X[:, T * b:T * (b + 1), :]
                link(dve.scalar_tensor_tensor(out=xb, in0=xa[:, :, :], scalar=tg[:, 2:3], in1=xb,
                                              op0=ALU.mult, op1=ALU.add))

            def route_choice(b):
                dve.wait_ge(lg_ps, b + 1)
                link(dve.tensor_tensor(lg[:, :, :], ps[:, RB, 0:T * E].rearrange("p (t e) -> p t e", t=T),
                                       rb[:, :].unsqueeze(1).broadcast_to([P, T, E]), ALU.add))
                dve.tensor_reduce(l1[:, :], lg[:, :, :], AX.X, ALU.max)
                ranks(lg[:, :, :], E, rank[:, :, :])
                dve.tensor_scalar(both[:, :, :], rank[:, :, :], 2.0, None, ALU.is_lt)
                dve.tensor_scalar(first[:, b, :, :], rank[:, :, :], 0.0, None, ALU.is_equal)
                link(dve.tensor_scalar(second[:, b, :, :], rank[:, :, :], 1.0, None, ALU.is_equal))
                dve.wait_ge(e2_sb, b) if b else None
                link(dve.tensor_tensor(lw[:, :, :], second[:, b, :, :], lg[:, :, :], ALU.mult))
                link(dve.tensor_reduce(t4[:, :], lw[:, :, :], AX.X, ALU.add))
                dve.tensor_tensor(t4[:, :], t4[:, :], l1[:, :], ALU.subtract).then_inc(dif_sb, 1)
                if b:
                    link(dve.tensor_copy(before[:, 0, :], before[:, T, :]))
                for t in range(T):
                    ins = dve.tensor_tensor(before[:, t + 1, :], before[:, t, :], both[:, t, :], ALU.add)
                    if t + 1 < T:
                        link(ins)
                ins.then_inc(both_sb, 1)

            def route_rows(b):
                dve.wait_ge(place_ps, b + 1)
                link(dve.tensor_tensor(place[:, b, :, :], ps[:, RB, 0:T * E].rearrange("p (t e) -> p t e", t=T),
                                       region[:, :].unsqueeze(1).broadcast_to([P, T, E]), ALU.add))
                dve.tensor_tensor(lw[:, :, :], first[:, b, :, :], place[:, b, :, :], ALU.mult)
                link(dve.tensor_tensor(ex[:, :, :], second[:, b, :, :], place[:, b, :, :], ALU.mult))
                dve.tensor_reduce(rowF[:, 0, :], lw[:, :, :], AX.X, ALU.add)
                link(dve.tensor_reduce(rowF[:, 1, :], ex[:, :, :], AX.X, ALU.add))
                dve.tensor_copy(rowI[:, :, b, :], rowF[:, :, :]).then_inc(row_sb, 1)
                dve.wait_ge(e2_sb, b + 1)
                link(dve.tensor_scalar(l1[:, :], e2[:, :], 1.0, None, ALU.add))
                link(dve.reciprocal(l1[:, :], l1[:, :]))
                link(dve.tensor_scalar(w_first[:, b, :], l1[:, :], tg[:, 2:3], None, ALU.mult))
                link(dve.tensor_tensor(w_second[:, b, :], w_first[:, b, :], e2[:, :], ALU.mult))

            def mix_norm(b):
                dve.wait_ge(res_done, B + b + 1)
                norm(T, lambda t: xn[:, T * b + t, :], lambda t: X[:, T * b + t, :]).then_inc(n3_ready, 1)

            def mix_logits(b):
                dve.wait_ge(l3_ps, b + 1)
                dve.tensor_scalar(lw[:, :, :], ps[:, RB, 0:T * E].rearrange("p (t e) -> p t e", t=T),
                                  -1.0, 88.0, ALU.mult, ALU.min).then_inc(l3_sb, 1)

            def mix_choice(b):
                dve.wait_ge(e3_sb, b + 1)
                link(dve.tensor_scalar(ex[:, :, :], ex[:, :, :], 1.0, None, ALU.add))
                link(dve.reciprocal(ex[:, :, :], ex[:, :, :]))
                link(dve.tensor_tensor(lg[:, :, :], ex[:, :, :], cb[:, :].unsqueeze(1).broadcast_to([P, T, E]), ALU.add))
                two = lg[:, :, :].rearrange("p t (g e) -> p t g e", e=2)
                link(dve.tensor_tensor(gsc[:, :, :], two[:, :, :, 0], two[:, :, :, 1], ALU.add))
                ranks(gsc[:, :, :], E // 2, rank[:, :, 0:E // 2])
                link(dve.tensor_scalar(gsc[:, :, :], rank[:, :, 0:E // 2], 2.0, None, ALU.is_lt))
                link(dve.tensor_tensor(two, two, gsc[:, :, :].unsqueeze(3).broadcast_to([P, T, E // 2, 2]), ALU.mult))
                ranks(lg[:, :, :], E, rank[:, :, :])
                link(dve.tensor_scalar(rank[:, :, :], rank[:, :, :], 4.0, None, ALU.is_lt))
                link(dve.tensor_tensor(ex[:, :, :], ex[:, :, :], rank[:, :, :], ALU.mult))
                link(dve.tensor_reduce(t4[:, :], ex[:, :, :], AX.X, ALU.add))
                link(dve.tensor_scalar(t4[:, :], t4[:, :], 1e-20, None, ALU.add))
                link(dve.reciprocal(t4[:, :], t4[:, :]))
                link(dve.tensor_scalar(t4[:, :], t4[:, :], ROUTED_SCALE, None, ALU.mult))
                at = b % 2 * HP
                dve.tensor_tensor(gpad[:, :, at:at + E], ex[:, :, :], t4[:, :].unsqueeze(2).broadcast_to([P, T, E]),
                                  ALU.mult).then_inc(c3_sb, 1)

            def mix_gates(b):
                dve.wait_ge(c3h_sb, b + 1)
                at = b % 2 * HP
                dve.tensor_tensor(cwT[at + 32:at + 32 + E, b // 2, :], ps[at:at + E, RB, :],
                                  cwT[at:at + E, b // 2, :].bitcast(F32),
                                  ALU.subtract).then_inc(c3l_sb, 1)

            def mix_pair(i):
                b, a = divmod(i, PAIRS + 1)
                h = hT[:, b % 2 * (PAIRS + 1) + a, :]
                dve.wait_ge(sg_sb, i + 1)
                dve.wait_ge(u_ps, i + 1)
                if b >= 2:
                    dve.wait_ge(y3_ps, b - 1)
                dve.tensor_tensor(h, sg[:, i % 2, :], ps[:, U3 + i % 2, :], ALU.mult).then_inc(su_sb, 1)
                dve.wait_ge(su_sb, i + 1)
                if a < PAIRS:
                    dve.wait_ge(c_ps, b * PAIRS + a + 1)
                    dve.tensor_tensor(h, h, ps[:, C3, :], ALU.mult).then_inc(h3_sb, 1)
                else:
                    dve.tensor_copy(rt[:, 0:1], rs[:, 0:1]).then_inc(h3_sb, 1)

            def mix_residual(b):
                dve.wait_ge(y3_ps, b + 1)
                xb = X[:, T * b:T * (b + 1), :]
                dve.scalar_tensor_tensor(out=xb, in0=ps[:, Y3 + b % 2, :].rearrange("p (t n) -> p t n", t=T),
                                         scalar=tg[:, 3:4], in1=xb, op0=ALU.mult, op1=ALU.add).then_inc(x_out, 1)

            def combine(b):
                dve.wait_ge(gathered[b], 16 * 2 * T)
                for y, w in ((y1, w_first), (y2, w_second)):
                    for t in range(T):
                        x = X[:, T * b + t, :]
                        ins = dve.scalar_tensor_tensor(out=x, in0=y[:, T * b + t, :], scalar=w[:, b, t:t + 1], in1=x,
                                                       op0=ALU.mult, op1=ALU.add)
                    if y is y1:
                        link(ins)
                ins.then_inc(combined, 1)
                dve.wait_ge(combined, b + 1)
                norm(T, lambda t: xn[:, T * b + t, :], lambda t: X[:, T * b + t, :]).then_inc(xn_ready, 1)

            def attention(l):
                s0 = l * B
                v_mask(s0)
                for t in range(T):
                    maxima(s0, t)
                if l == 1:
                    combine(1)
                v_mask(s0 + 1)

                for s in range(s0, s0 + B):
                    n, more, prev = s + 1, s + 1 < s0 + B, s > s0
                    p = s - s0 - 1
                    if more:
                        maxima(n, 0)
                    if l == 1 and s >= s0 + 2:
                        mix_gates(s - s0 - 2)
                    if more:
                        for t in range(1, T):
                            maxima(n, t)
                    if l == 0:
                        if prev:
                            route_choice(p)
                        normalise(s)
                        if prev:
                            route_rows(p)
                        if s + 2 < s0 + B:
                            v_mask(s + 2)
                        b1_copy(s)
                        residual(s)
                        route_norms(s)
                    else:
                        if s + 2 < s0 + B:
                            combine(s + 2 - s0)
                        if prev:
                            mix_logits(p)
                        normalise(s)
                        if s + 2 < s0 + B:
                            v_mask(s + 2)
                        residual(s)
                        if more:
                            if prev:
                                mix_choice(p)
                            mix_norm(s - s0)

            attention(0)

            route_choice(B - 1)
            route_rows(B - 1)
            dve.wait_ge(count_ps, 1)
            link(dve.tensor_copy(count[:, :], ps[:, RB, 0:E]))
            dve.tensor_tensor(tailI[:, :], count[:, :], region[:, :], ALU.add)
            link(dve.tensor_scalar(tilesI[:, :], count[:, :], 1.0 / P, (P - 1) / P - 0.498, ALU.mult, ALU.add))
            link(dve.tensor_copy(tiles[:, :], tilesI[:, :]))
            link(dve.tensor_tensor(sumtri[:, :, :], tri[E][:, 0, :, :], tiles[:, :].unsqueeze(1).broadcast_to([P, E, E]), ALU.mult))
            link(dve.tensor_reduce(begin[:, :], sumtri[:, :, :], AX.X, ALU.add))
            link(dve.tensor_tensor(end[:, :], begin[:, :], tiles[:, :], ALU.add))
            k = [P, NT, E]
            link(dve.tensor_tensor(past[:, :, :], end[:, :].unsqueeze(1).broadcast_to(k),
                                   tileno[:, :].unsqueeze(2).broadcast_to(k), ALU.is_le))
            link(dve.tensor_reduce(eT[:, :], past[:, :, :], AX.X, ALU.add))
            link(dve.tensor_tensor(past[:, :, :], past[:, :, :], tiles[:, :].unsqueeze(1).broadcast_to(k), ALU.mult))
            link(dve.tensor_reduce(sT[:, :], past[:, :, :], AX.X, ALU.add))
            link(dve.tensor_tensor(sT[:, :], tileno[:, :], sT[:, :], ALU.subtract))
            link(dve.tensor_scalar(sT[:, :], sT[:, :], float(P), None, ALU.mult))
            link(dve.scalar_tensor_tensor(out=sT[:, :], in0=eT[:, :], scalar=float(R), in1=sT[:, :], op0=ALU.mult, op1=ALU.add))
            dve.tensor_scalar(expertI[:, :], eT[:, :], float(E - 1), None, ALU.min)
            dve.tensor_scalar(offsetI[:, :], sT[:, :], float(E * R), None, ALU.min).then_inc(table_sb, 1)
            dve.wait_ge(table_sb, 1)

            def weights(i, ring):
                if not isinstance(i, int) or i >= 4:
                    dve.wait_ge(yo_sb, i - 3)
                e = dve.value_load(expertI[0:1, bass.ds(i, 1)], min_val=0, max_val=E - 1)
                dve.tensor_copy(wcur[:, ring, :], w12[:, bass.ds(e, 1), :].rearrange("p o w -> p (o w)")).then_inc(wc_sb, 1)

            def tile_x(i, par):
                dve.wait_ge(t_ps, i + 1)
                if not isinstance(i, int) or i >= 2:
                    dve.wait_ge(h_ps, i - 1)
                dve.tensor_copy(xgT[:, par, :], ps[:, TX + par, 0:P]).then_inc(xg_sb, 1)

            def tile_out(i, par, ring, turn):
                dve.wait_ge(y_ps, i + 1)
                if not isinstance(turn, int) or turn > 0:
                    dve.wait_ge(y_st[ring], turn * 16)
                dve.tensor_tensor(yo[:, ring, :], ps[:, YB + par, 0:P], wcur[:, ring, B2_AT:B2_AT + P],
                                  ALU.add).then_inc(yo_sb, 1)

            dve.wait_ge(w1_scaled, E)
            dve.wait_ge(b1_sb, B)
            dve.wait_ge(w2_in, 16 * E)
            dve.wait_ge(b2_in, 16)
            for i in range(3):
                weights(i, i)
            dve.wait_ge(wt_ps, 1)
            link(dve.tensor_copy(wT[:, :, :], ps[:, F + 1, :].rearrange("p (i n) -> p i n", i=4)))
            dve.tensor_copy(wp[:, 1, :], wT[:, 3, :])
            cols_of = lambda i: lambda g: wT[:, i, GW * g:GW * (g + 1)].rearrange("p (h d) -> p h d", h=HG)
            stack(1, cols_of(1), cols_of(0)).then_inc(prep_sb, 1)
            dve.tensor_copy(wv[:, 1, :], wT[:, 2, :]).then_inc(wv_sb, 1)
            lower_keys(1)
            tile_x(0, 0)
            tile_x(1, 1)
            link(dve.scalar_tensor_tensor(out=begin[:, :], in0=begin[:, :], scalar=float(P), in1=region[:, :],
                                          op0=ALU.mult, op1=ALU.subtract))
            k = [P, B * T, E]
            flat = lambda a: a[:, :, :, :].rearrange("p b t e -> p (b t) e")
            link(dve.tensor_tensor(flat(place), flat(place), begin[:, :].unsqueeze(1).broadcast_to(k), ALU.add))
            link(dve.tensor_tensor(flat(wide), flat(first), flat(place), ALU.mult))
            link(dve.tensor_reduce(getF[:, 0, :], flat(wide), AX.X, ALU.add))
            link(dve.tensor_tensor(flat(wide), flat(second), flat(place), ALU.mult))
            link(dve.tensor_reduce(getF[:, 1, :], flat(wide), AX.X, ALU.add))
            dve.tensor_copy(getI[:, :, :], getF[:, :, :]).then_inc(get_sb, 1)
            with dve.Fori(0, (NT - 3) // 4) as k:
                for u in range(1, 5):
                    weights(k * 4 + (u + 2), (u + 2) % 4)
                    tile_x(k * 4 + (u + 1), (u + 1) % 2)
                    tile_out(k * 4 + (u - 1), (u - 1) % 2, (u - 1) % 4, k + (u - 1) // 4)
            i = NT - 2
            tile_x(i + 1, (i + 1) % 2)
            for i in range(NT - 3, NT):
                tile_out(i, i % 2, i % 4, i // 4)
            dve.wait_ge(yo_sb, NT)
            combine(0)
            attention(1)
            PA = PAIRS + 1
            for i in range(B * PA):
                mix_pair(i)
                if i == 0:
                    mix_norm(B - 1)
                if i == 1:
                    mix_choice(B - 2)
                if i == 3:
                    mix_gates(B - 2)
                if i == 4:
                    mix_logits(B - 1)
                if i == 5:
                    mix_choice(B - 1)
                if i == 7:
                    mix_gates(B - 1)
                if i > PA and i % PA == 1:
                    mix_residual(i // PA - 1)
            mix_residual(B - 1)


_INS = ["x", "ctx_1024", "g_xattn", "g_ffn", "L0_xattn_Wq", "L0_xattn_bq", "L0_xattn_Wkv", "L0_xattn_bkv",
        "L0_xattn_Wp", "L0_xattn_bp", "L0_ffn_router_W", "L0_ffn_router_b", "L0_ffn_ln_g", "L0_ffn_ln_b",
        "L0_ffn_W1", "L0_ffn_b1", "L0_ffn_W2", "L0_ffn_b2", "L1_xattn_wq", "L1_xattn_bq", "L1_xattn_wk",
        "L1_xattn_bk", "L1_xattn_wv", "L1_xattn_bv", "L1_xattn_wo", "L1_xattn_bo", "L1_ffn_gate_w",
        "L1_ffn_correction_bias", "L1_ffn_Wg", "L1_ffn_Wu", "L1_ffn_Wd", "L1_ffn_Wg_s", "L1_ffn_Wu_s",
        "L1_ffn_Wd_s"]


def kernel(**inputs):
    import numpy as np
    import concourse.bacc as bacc
    from concourse.bass_utils import run_bass_kernel_spmd

    nc = bacc.Bacc("TRN2", target_bir_lowering=False, num_devices=1)
    arrays, aps = {}, {}
    for name in _INS:
        a = np.ascontiguousarray(inputs[name])
        arrays[f"in_{name}"] = a
        aps[name] = nc.dram_tensor(f"in_{name}", a.shape, mybir.dt.from_np(a.dtype), kind="ExternalInput").ap()
    out = nc.dram_tensor("out", inputs["x"].shape, F32, kind="ExternalOutput").ap()
    build(nc, aps, out)
    r = run_bass_kernel_spmd(nc, [arrays], core_ids=[0])
    return r.results[0]["out"]
```

```python
import concourse.bass as bass
from concourse import mybir
from contextlib import ExitStack

F32 = mybir.dt.float32
F32R = mybir.dt.float32r
I32 = mybir.dt.int32
ALU = mybir.AluOpType
ACT = mybir.ActivationFunctionType
AX = mybir.AxisListType

P = 128
HP = P // 2
B = 4
T = 4
Q = T * P
L = 2
S = 77
HD = 8
G = 4
HG = 4
H = G * HG
GW = HG * HD
KG = HG * S
C = -(-KG // P)
E = 8
FF = 512
FC = FF // P
I1 = 64
PAIRS = E // 2
PA = PAIRS + 1
EPS = 1e-5
SCALE = 1.0 / float(HD) ** 0.5
ROUTED_SCALE = 2.5
RSQRT_GUESS = 0x5F3759DF
N = B * Q
R = N + P
NT = (2 * N + E * (P - 1)) // P
W1_AT, W2_AT, B1_AT, B2_AT = 0, FF, 2 * FF, 2 * FF + FC
WW = B2_AT + P

R_BK, R_BQ, R_BV, R_B1, R_LNG, R_LNB, R_GW = 0, 8, 16, 18, 50, 58, 66
ROWS = 74
CH = [(c * P) % S for c in range(C)]


def build(nc, I, out):
    ctx = ExitStack()
    with ctx:
        def sb(name, shape, dt=F32):
            return ctx.enter_context(nc.sbuf_tensor(name, shape, dt))

        def sem(name):
            return ctx.enter_context(nc.semaphore(name))

        X = sb("X", [P, B * T, P])
        xn = sb("xn", [P, B * T, P])
        ctx_sb = sb("ctx_sb", [S, B, P])
        rows = sb("rows", [ROWS, P])
        cols = sb("cols", [P, ROWS])
        wq0 = sb("wq0", [P, P])
        wkv0 = sb("wkv0", [P, 2 * P])
        wnat = sb("wnat", [P, 4, P])
        wT = sb("wT", [P, 4, P])
        wv = sb("wv", [P, L, P])
        wp = sb("wp", [P, L, P])
        wpx = sb("wpx", [P, L, P])
        wkS = sb("wkS", [P, L, G, P])
        wqS = sb("wqS", [P, L, G, P])
        gains = sb("gains", [P, 4])
        tg = sb("tg", [P, 4])
        bpb = sb("bpb", [P, L, P])
        bpx = sb("bpx", [P, L, P])
        bvb = sb("bvb", [P, L, P])
        rb = sb("rb", [P, E])
        cb = sb("cb", [P, E])
        rw = sb("rw", [P, E])
        w12 = sb("w12", [P, E, WW])
        wcur = sb("wcur", [P, 4, WW])
        wg1 = sb("wg1", [P, PA, P])
        wu1 = sb("wu1", [P, PA, P])
        wd1 = sb("wd1", [P, PA, P])
        ident = sb("ident", [P, P])
        maskK = sb("maskK", [P, G, HG])
        maskV = sb("maskV", [P, C, P])
        tri = {m: sb(f"tri{m}", [P, T, m, m]) for m in (E, E // 2)}
        pickr = sb("pickr", [P, PAIRS, P], F32R)
        last_const = sb("last_const", [P, 1])
        ctxT = sb("ctxT", [P, B, 3, S])
        kst = sb("kst", [P, L, G, B * S])
        K4 = sb("K4", [P, 2, G, C * P], F32R)
        V4 = sb("V4", [P, 2, C, P])
        Z = sb("Z", [P, 2, G, Q], F32R)
        khi = Z[:, 1, :, 0:B * S]
        qf = sb("qf", [P, G, Q])
        xT = sb("xT", [P, Q])
        mpad = sb("mpad", [P, T, P])
        Pr = sb("Pr", [P, 2, G, Q])
        maskH = sb("maskH", [P, C, G, 2, H])
        rden = sb("rden", [P, P])
        spread = sb("spread", [P, T, P])
        oT = sb("oT", [P, Q])
        st6w = sb("st6w", [P, 3 * T, 6])
        mv = sb("mv", [P, 3 * T, 2])
        ve = sb("ve", [P, 3 * T])
        rs = sb("rs", [P, 3 * T])
        rt = sb("rt", [P, 3 * T])
        xa = sb("xa", [P, T, P])
        xh = sb("xh", [P, 2, T, P])
        xaT = sb("xaT", [P, Q])
        lg = sb("lg", [P, T, E])
        lw = sb("lw", [P, T, E])
        cmpa = sb("cmpa", [P, T * E * E])
        cmpb = sb("cmpb", [P, T * E * E])
        rank = sb("rank", [P, T, E])
        gsc = sb("gsc", [P, T, E // 2])
        l1 = sb("l1", [P, T])
        t4 = sb("t4", [P, T])
        e2 = sb("e2", [P, T])
        ex = sb("ex", [P, T, E])
        first = sb("first", [P, B, T, E])
        second = sb("second", [P, B, T, E])
        both = sb("both", [P, T, E])
        before = sb("before", [P, T + 1, E])
        place = sb("place", [P, B, T, E])
        w_first = sb("w_first", [P, B, T])
        w_second = sb("w_second", [P, B, T])
        rowF = sb("rowF", [P, 2, T])
        rowI = sb("rowI", [P, 2, B, T], I32)
        getF = sb("getF", [P, 2, B * T])
        getI = sb("getI", [P, 2, B * T], I32)
        wide = sb("wide", [P, B, T, E])
        earlier = sb("earlier", [P, P])
        ones = sb("ones", [P, P])
        zero = sb("zero", [P, P])
        regionI = sb("regionI", [P, E], I32)
        region = sb("region", [P, E])
        tileI = sb("tileI", [P, NT], I32)
        tileno = sb("tileno", [P, NT])
        count = sb("count", [P, E])
        tilesI = sb("tilesI", [P, E], I32)
        tiles = sb("tiles", [P, E])
        sumtri = sb("sumtri", [P, E, E])
        begin = sb("begin", [P, E])
        end = sb("end", [P, E])
        tailI = sb("tailI", [P, E], I32)
        past = sb("past", [P, NT, E])
        eT = sb("eT", [P, NT])
        sT = sb("sT", [P, NT])
        expertI = sb("expertI", [P, NT], I32)
        offsetI = sb("offsetI", [P, NT], I32)
        flatPr = Pr[:, :, :, :].rearrange("p s g q -> p (s g q)")
        xg = flatPr[:, 0:4 * P].rearrange("p (i n) -> p i n", i=4)
        yo = flatPr[:, 4 * P:8 * P].rearrange("p (i n) -> p i n", i=4)
        xgT = flatPr[:, 8 * P:10 * P].rearrange("p (i n) -> p i n", i=2)
        hid = flatPr[:, 10 * P:(10 + 2 * FC) * P].rearrange("p (i c n) -> p i c n", i=2, c=FC)
        flatW = wcur[:, :, :].rearrange("p i w -> p (i w)")
        y1 = flatW[:, 0:N].rearrange("p (t n) -> p t n", n=P)
        y2 = flatW[:, N:2 * N].rearrange("p (t n) -> p t n", n=P)
        cwT = sb("cwT", [P, B // 2, Q], F32R)
        w2flat = w12[:, :, :].rearrange("p e w -> p (e w)")
        part = lambda i, m, mem: mem[:, i * Q:(i + m) * Q].rearrange("p (a q) -> p a q", q=Q)
        x3T = part(0, B, w2flat)
        hT = part(B, 2 * PA, w2flat)
        GPAD = B + 2 * PA
        gpad = w2flat[:, GPAD * Q:(GPAD + 1) * Q].rearrange("p (t n) -> p t n", t=T)
        sg = part(0, 2, flatPr)
        gates = part(2, 2, flatPr)
        halves = lambda a, n: a.rearrange("p (h n) -> p h n", n=n)
        PW = PA * P
        wr = [halves(K4[:, i, :, :].rearrange("p g n -> p (g n)")[:, 0:2 * PW], PW) for i in range(2)]
        xr = [halves(Z[:, b // 2, :, :].rearrange("p g n -> p (g n)")[:, b % 2 * 2 * Q:(b % 2 + 1) * 2 * Q], Q)
              for b in range(B)]

        ps = ctx.enter_context(nc.psum_tensor("ps", [P, 8, 512], F32))
        S0, O, D, F, RB = 0, 2, 3, 4, 7
        KB = ((O, D, F + 2, RB), (F, F + 1, F, F + 1))
        K1 = 3 * GW + H
        QB = (F, F + 2, F + 1, F)
        G3, U3, C3, Y3 = 0, F, F + 2, O
        TX, HB, YB = 0, 2, 4
        xs_dram = nc.dram_tensor("expert_rows", [(E + 1) * R, P], F32).ap()
        y_dram = nc.dram_tensor("expert_out", [NT * P, P], F32).ap()

        x_in = [sem(f"x_in{b}") for b in range(B)]
        ctx_in, rows_in, attw_in, attw1_in, small_in, router_in, w1_in, w2_in, b2_in, m1w_in = (sem(n) for n in (
            "ctx_in", "rows_in", "attw_in", "attw1_in", "small_in", "router_in", "w1_in", "w2_in", "b2_in", "m1w_in"))
        zeroed = sem("zeroed")
        consts = sem("consts")
        cols_ps, ctx_ps, wt_ps, prep_sb, tg_sb, k_ps, kh_sb, k_sb, bv_ps, bpx_sb, wv_sb, rden_sb, spread_ps, o_sb = (sem(n) for n in (
            "cols_ps", "ctx_ps", "wt_ps", "prep_sb", "tg_sb", "k_ps", "kh_sb", "k_sb", "bv_ps", "bpx_sb", "wv_sb", "rden_sb", "spread_ps", "o_sb"))
        dstep, pstep = sem("dstep"), sem("pstep")
        xn_ready, xt_ps, xt_sb, v_ps, v_sb, q_ps, qh_sb, z_sb = (sem(n) for n in (
            "xn_ready", "xt_ps", "xt_sb", "v_ps", "v_sb", "q_ps", "qh_sb", "z_sb"))
        k4_ready, mx_ps, mx_done, mt_ps, mz_sb = (sem(n) for n in (
            "k4_ready", "mx_ps", "mx_done", "mt_ps", "mz_sb"))
        s_ps, p_sb, pv_done, ot_sb, proj_ps, res_done = (sem(n) for n in (
            "s_ps", "p_sb", "pv_done", "ot_sb", "proj_ps", "res_done"))
        b1_ps, b1_sb, w1_scaled, bias_sb = (sem(n) for n in ("b1_ps", "b1_sb", "w1_scaled", "bias_sb"))
        xa_ready, xa_ps, xa_sb, lg_ps, dif_sb, e2_sb, both_sb, place_ps, row_sb = (sem(n) for n in (
            "xa_ready", "xa_ps", "xa_sb", "lg_ps", "dif_sb", "e2_sb", "both_sb", "place_ps", "row_sb"))
        scattered = [sem(f"scattered{b}") for b in range(B)]
        idle_zero, tails_sp, tails_act = (sem(n) for n in ("idle_zero", "tails_sp", "tails_act"))
        count_ps, table_sb, get_sb = (sem(n) for n in ("count_ps", "table_sb", "get_sb"))
        xg_in = [sem(f"xg_in{i}") for i in range(4)]
        y_st = [sem(f"y_st{i}") for i in range(4)]
        t_ps, xg_sb, wc_sb, h_ps, a_sb, y_ps, yo_sb = (sem(n) for n in (
            "t_ps", "xg_sb", "wc_sb", "h_ps", "a_sb", "y_ps", "yo_sb"))
        gates_zero = sem("gates_zero")
        first_gathered = [sem(f"first_gathered{t}") for t in range(T)]
        gathered = [sem(f"gathered{i}") for i in range(B)]
        weighted, combined = sem("weighted"), sem("combined")
        n3_ready, t3_ps, t3_sb, l3_ps, l3_sb, e3_sb, c3_sb, c3_ps, c3h_sb, c3l_sb, gates_sb, wr_sb, xr_sb = (sem(n) for n in (
            "n3_ready", "t3_ps", "t3_sb", "l3_ps", "l3_sb", "e3_sb", "c3_sb", "c3_ps", "c3h_sb", "c3l_sb", "gates_sb", "wr_sb", "xr_sb"))
        g_ps, u_ps, c_ps, sg_sb, su_sb, h3_sb, y3_ps, x_out = (sem(n) for n in (
            "g_ps", "u_ps", "c_ps", "sg_sb", "su_sb", "h3_sb", "y3_ps", "x_out"))
        stored = sem("stored")

        LN = L * B
        M1W = 16 * (2 * 2 + 2 + 1)
        block = ctx.enter_context(nc.Block())

        def tails(eng, experts, done):
            eng.wait_ge(table_sb, 1)
            for e in experts:
                row = eng.value_load(tailI[0:1, e:e + 1], min_val=0, max_val=E * R)
                eng.dma_start(xs_dram[bass.ds(row, P), :], zero[:, :]).then_inc(done, 16)

        @block.sync
        def _(sp):
            def load_x(b):
                sp.dma_start(X[:, T * b:T * (b + 1), :],
                             I["x"][b].rearrange("(t p) d -> p t d", p=P)).then_inc(x_in[b], 16)

            load_x(0)
            sp.dma_start(ctx_sb[:, :, :], I["ctx_1024"].rearrange("b k d -> k b d")).then_inc(ctx_in, 16)
            sp.dma_start(wkv0[:, :], I["L0_xattn_Wkv"]).then_inc(attw_in, 16)
            sp.dma_start(wq0[:, :], I["L0_xattn_Wq"]).then_inc(attw_in, 16)
            sp.dma_start(wp[:, 0, :], I["L0_xattn_Wp"]).then_inc(attw_in, 16)
            for b in range(1, B):
                load_x(b)
            sp.dma_start(rb[:, :], I["L0_ffn_router_b"].rearrange("(o n) -> o n", o=1).broadcast_to([P, E])).then_inc(router_in, 16)
            sp.dma_start(cb[:, :], I["L1_ffn_correction_bias"].rearrange("(o n) -> o n", o=1).broadcast_to([P, E])).then_inc(router_in, 16)
            sp.dma_start(rw[:, :], I["L0_ffn_router_W"]).then_inc(router_in, 16)
            for i, n in enumerate(("wq", "wk", "wv", "wo")):
                sp.dma_start(wnat[:, i, :], I["L1_xattn_" + n]).then_inc(attw1_in, 16)
            for e in range(E):
                sp.dma_start(w12[:, e, W1_AT:W1_AT + FF], I["L0_ffn_W1"][e]).then_inc(w1_in, 16)
            for e in range(E):
                sp.dma_start(w12[:, e, W2_AT:W2_AT + FF].rearrange("p (c n) -> p c n", c=FC),
                             I["L0_ffn_W2"][e].rearrange("(c p) n -> p c n", p=P)).then_inc(w2_in, 16)
            sp.dma_start(w12[:, :, B2_AT:B2_AT + P],
                         I["L0_ffn_b2"].rearrange("(o e) n -> o e n", o=1).broadcast_to([P, E, P])).then_inc(b2_in, 16)
            sp.wait_ge(zeroed, 4)
            for w, name in ((wg1, "L1_ffn_Wg"), (wu1, "L1_ffn_Wu")):
                sp.dma_start(w[:, 0:PAIRS, :].rearrange("p a (e i) -> p (a e) i", e=2),
                             I[name].rearrange("e d i -> d e i")).then_inc(m1w_in, 16)
                sp.dma_start(w[:, PAIRS, 0:I1], I[name + "_s"]).then_inc(m1w_in, 16)
            for two in range(2):
                sp.dma_start(wd1[I1 * two:I1 * (two + 1), 0:PAIRS, :],
                             I["L1_ffn_Wd"].rearrange("(a e) i n -> e i a n", e=2)[two]).then_inc(m1w_in, 16)
            sp.dma_start(wd1[0:I1, PAIRS, :], I["L1_ffn_Wd_s"]).then_inc(m1w_in, 16)
            sp.wait_ge(consts, 1)
            sp.dma_start(xs_dram[E * R:E * R + P, :], zero[:, :]).then_inc(idle_zero, 16)
            tails(sp, range(0, E, 2), tails_sp)

            def load_tile(i, ring):
                row = sp.value_load(offsetI[0:1, bass.ds(i, 1)], min_val=0, max_val=E * R)
                sp.dma_start(xg[:, ring, :], xs_dram[bass.ds(row, P), :]).then_inc(xg_in[ring], 16)

            def store_tile(i, ring):
                sp.wait_ge(yo_sb, i + 1)
                sp.dma_start(y_dram[bass.ds(i * P, P), :], yo[:, ring, :]).then_inc(y_st[ring], 16)

            sp.wait_ge(table_sb, 1)
            for b in range(B):
                sp.wait_ge(scattered[b], 16 * 2 * T)
            sp.wait_ge(idle_zero, 16)
            sp.wait_ge(tails_sp, 16 * (E // 2))
            sp.wait_ge(tails_act, 16 * (E // 2))
            for i in range(4):
                load_tile(i, i)
            with sp.Fori(1, NT // 4) as k:
                for u in range(4):
                    sp.wait_ge(t_ps, k * 4 + (u - 3))
                    load_tile(k * 4 + u, u)
                    store_tile(k * 4 + (u - 4), u)
            for i in range(NT // 4 * 4, NT):
                sp.wait_ge(t_ps, i - 3)
                load_tile(i, i % 4)
                store_tile(i - 4, i % 4)
            for i in range(NT - 4, NT):
                store_tile(i, i % 4)
            for b in range(B - 1):
                sp.wait_ge(x_out, b + 1)
                sp.dma_start(out[b].rearrange("(t p) d -> p t d", p=P),
                             X[:, T * b:T * (b + 1), :]).then_inc(stored, 16)
            for half in range(2):
                span = slice(half * T // 2, (half + 1) * T // 2)
                sp.wait_ge(x_out, B + half)
                sp.dma_start(out[B - 1].rearrange("(t p) d -> p t d", p=P)[:, span, :],
                             X[:, T * (B - 1) + span.start:T * (B - 1) + span.stop, :]).then_inc(stored, 16)
            sp.wait_ge(stored, 16 * (B + 1))

        @block.gpsimd
        def _(pool):
            n = [0]

            def link(ins):
                n[0] += 1
                ins.then_inc(pstep, 1)
                pool.wait_ge(pstep, n[0])

            pool.memset(rows[:, :], 0.0).then_inc(zeroed, 1)
            pool.wait_ge(zeroed, 1)
            pool.memset(rows[0:8, 3 * GW:P], -1.0).then_inc(zeroed, 1)
            link(pool.memset(ident[:, :], 0.0))
            link(pool.affine_select(out=ident[:, :], in_=ident[:, :], compare_op=ALU.not_equal, fill=1.0,
                                    base=0, pattern=[[-1, P]], channel_multiplier=1))
            link(pool.memset(wg1[:, PAIRS, I1:P], 0.0))
            link(pool.memset(wu1[:, PAIRS, I1:P], 0.0))
            pool.memset(wd1[I1:P, PAIRS, :], 0.0).then_inc(zeroed, 2)
            pool.wait_ge(zeroed, 4)
            link(pool.memset(maskK[:, :, :], 1.0))
            for r in range(3):
                m = maskK[GW * r:GW * (r + 1), :, :]
                link(pool.affine_select(out=m, in_=m, compare_op=ALU.is_ge, fill=0.0, base=0,
                                        pattern=[[0, G], [-HD, HG]], channel_multiplier=1))
                link(pool.affine_select(out=m, in_=m, compare_op=ALU.is_ge, fill=0.0, base=HD - 1,
                                        pattern=[[0, G], [HD, HG]], channel_multiplier=-1))
            m = maskK[3 * GW:P, :, :]
            link(pool.affine_select(out=m, in_=m, compare_op=ALU.is_equal, fill=0.0, base=0,
                                    pattern=[[-HG, G], [-1, HG]], channel_multiplier=1))
            link(pool.memset(maskV[:, :, :], 1.0))
            for c in range(C):
                m = maskV[:, c, :].rearrange("p (g h d) -> p g h d", g=G, h=HG)
                link(pool.affine_select(out=m, in_=m, compare_op=ALU.is_ge, fill=0.0, base=P * c,
                                        pattern=[[0, G], [-S, HG], [0, HD]], channel_multiplier=1))
                link(pool.affine_select(out=m, in_=m, compare_op=ALU.is_ge, fill=0.0, base=S - 1 - P * c,
                                        pattern=[[0, G], [S, HG], [0, HD]], channel_multiplier=-1))
            link(pool.memset(maskH[:, :, :, :, :], 1.0))
            for c in range(C):
                m = maskH[:, c, :, :, :]
                link(pool.affine_select(out=m, in_=m, compare_op=ALU.is_ge, fill=0.0, base=P * c,
                                        pattern=[[KG, G], [0, 2], [-S, H]], channel_multiplier=1))
                link(pool.affine_select(out=m, in_=m, compare_op=ALU.is_ge, fill=0.0, base=S - 1 - P * c,
                                        pattern=[[-KG, G], [0, 2], [S, H]], channel_multiplier=-1))
            m = maskH[:, C - 1, :, :, :]
            link(pool.affine_select(out=m, in_=m, compare_op=ALU.is_ge, fill=0.0, base=KG - 1 - P * (C - 1),
                                    pattern=[[0, G], [0, 2], [0, H]], channel_multiplier=-1))
            link(pool.memset(spread[:, :, :], 1.0))
            m = spread[:, :, :].rearrange("p t (h d) -> p t h d", d=HD)
            link(pool.affine_select(out=m, in_=m, compare_op=ALU.is_equal, fill=0.0, base=0,
                                    pattern=[[-GW, T], [-1, H], [0, HD]], channel_multiplier=1))
            for m in (E, E // 2):
                link(pool.memset(tri[m][:, :, :, :], 1.0))
                link(pool.affine_select(out=tri[m][:, :, :, :], in_=tri[m][:, :, :, :], compare_op=ALU.is_gt, fill=0.0,
                                        base=0, pattern=[[0, T], [1, m], [-1, m]], channel_multiplier=0))
            link(pool.memset(ones[:, :], 1.0))
            link(pool.memset(zero[:, :], 0.0))
            link(pool.affine_select(out=earlier[:, :], in_=ones[:, :], compare_op=ALU.is_gt, fill=0.0, base=0,
                                    pattern=[[1, P]], channel_multiplier=-1))
            link(pool.iota(regionI[:, :], pattern=[[R, E]], base=0, channel_multiplier=0))
            link(pool.tensor_copy(region[:, :], regionI[:, :]))
            link(pool.iota(tileI[:, :], pattern=[[1, NT]], base=0, channel_multiplier=0))
            link(pool.tensor_copy(tileno[:, :], tileI[:, :]))
            link(pool.memset(before[:, 0, :], 0.0))
            link(pool.memset(pickr[:, :, :].bitcast(F32), 0.0))
            for r in (0, 32, 64, 96):
                m = pickr[r:r + E, :, :].rearrange("p a (e i) -> p a e i", e=2)
                link(pool.affine_select(out=m, in_=m, compare_op=ALU.not_equal, fill=1.0, base=0,
                                        pattern=[[-2, PAIRS], [-1, 2], [0, I1]], channel_multiplier=1))
            link(pool.memset(mpad[:, :, :], 0.0))
            pool.memset(last_const[:, :], 0.0).then_inc(consts, 1)

            def keys(s):
                l, b = divmod(s, B)
                pool.wait_ge(k_sb, G * (l + 1))
                if s >= 2:
                    pool.wait_ge(s_ps, G * C * (s - 1))
                for g in range(G):
                    o = K4[:, s % 2, g, 0:KG].rearrange("p (h k) -> p h k", h=HG)
                    k = kst[:, l, g, S * b:S * (b + 1)]
                    pool.tensor_tensor(o, k.unsqueeze(1).broadcast_to([P, HG, S]),
                                       maskK[:, g, :].unsqueeze(2).broadcast_to([P, HG, S]),
                                       ALU.mult).then_inc(k4_ready, 1)
                pool.wait_ge(k4_ready, G * (s + 1))

            def add_bias(s):
                l, b = divmod(s, B)
                pool.wait_ge(bpx_sb, l + 1)
                pool.wait_ge(xn_ready, s + 1)
                xb = X[:, T * b:T * (b + 1), :]
                pool.tensor_tensor(xb, xb, bpx[:, l, :].unsqueeze(1).broadcast_to([P, T, P]), ALU.add).then_inc(bias_sb, 1)
                pool.wait_ge(bias_sb, s + 1)

            def q_lower(s, g):
                pool.wait_ge(qh_sb, G * s + g + 1)
                z = Z[GW:2 * GW, s % 2, g, :]
                pool.tensor_tensor(z, qf[GW:2 * GW, g, :], z.bitcast(F32), ALU.subtract).then_inc(z_sb, 1)
                pool.wait_ge(z_sb, G * s + g + 1)

            def scatter(b):
                pool.wait_ge(row_sb, b + 1)
                for t in range(T):
                    for k in range(2):
                        pool.indirect_dma_start(
                            out=xs_dram, in_=xh[:, b % 2, t, :], in_offset=None,
                            out_offset=bass.IndirectOffsetOnAxis(ap=rowI[:, k, b, t:t + 1], axis=0),
                        ).then_inc(scattered[b], 16)
                pool.wait_ge(scattered[b], 16 * 2 * T)

            keys(0)
            for g in range(G):
                q_lower(0, g)
            keys(1)
            add_bias(0)
            add_bias(1)
            for s in range(B):
                if s + 1 < B:
                    for g in range(G):
                        q_lower(s + 1, g)
                if s >= 2:
                    scatter(s - 2)
                if s + 2 < B:
                    add_bias(s + 2)
                    keys(s + 2)
            scatter(B - 2)
            scatter(B - 1)
            pool.memset(cwT[:, :, :].bitcast(F32), 0.0).then_inc(gates_zero, 1)
            pool.wait_ge(gates_zero, 1)
            keys(B)
            keys(B + 1)
            pool.wait_ge(get_sb, 1)
            for u in range(4):
                pool.wait_ge(y_st[u], 16 * len(range(u, NT, 4)))

            def gather(b):
                for t in range(T):
                    for k, dst in enumerate((y1, y2)):
                        pool.indirect_dma_start(
                            out=dst[:, T * b + t, :], in_=y_dram, out_offset=None,
                            in_offset=bass.IndirectOffsetOnAxis(ap=getI[:, k, T * b + t:T * b + t + 1], axis=0),
                        ).then_inc(gathered[b] if b else first_gathered[t], 16)
                for done in [gathered[b]] if b else first_gathered:
                    pool.wait_ge(done, 16 * 2 * (T if b else 1))

            def combine(b):
                pool.wait_ge(weighted, b)
                xb = X[:, T * b:T * (b + 1), :]
                link(pool.tensor_tensor(xb, xb, y1[:, T * b:T * (b + 1), :], ALU.add))
                pool.tensor_tensor(xb, xb, y2[:, T * b:T * (b + 1), :], ALU.add).then_inc(combined, 1)
                pool.wait_ge(combined, b)

            gather(0)
            gather(1)
            for g in range(G):
                q_lower(B, g)
            combine(1)
            add_bias(B)
            gather(2)
            add_bias(B + 1)
            for s in range(B, 2 * B - 1):
                for g in range(G):
                    q_lower(s + 1, g)
                if s < 2 * B - 2:
                    combine(s + 2 - B)
                if s == B:
                    gather(3)
                else:
                    add_bias(s + 1)
                if s + 2 < 2 * B:
                    keys(s + 2)

            def split(x, into):
                link(pool.tensor_scalar(into[:, 0, :], x, 1.0, None, ALU.mult))
                return pool.tensor_tensor(into[:, 1, :], x, into[:, 0, :].bitcast(F32), ALU.subtract)

            def split_x(b):
                pool.wait_ge(t3_sb, b + 1)
                split(x3T[:, b, :], xr[b]).then_inc(xr_sb, 1)

            pool.wait_ge(m1w_in, M1W)
            pool.wait_ge(s_ps, G * C * (LN - 1))
            split(wg1[:, :, :].rearrange("p a n -> p (a n)"), wr[0]).then_inc(wr_sb, 1)
            split_x(0)
            split_x(1)
            pool.wait_ge(s_ps, G * C * LN)
            split(wu1[:, :, :].rearrange("p a n -> p (a n)"), wr[1]).then_inc(wr_sb, 1)
            for j in range(B * PAIRS):
                b, a = divmod(j, PAIRS)
                if a == 0 and 2 <= b + 1 < B:
                    split_x(b + 1)
                h = hT[:, b % 2 * PA + a, :]
                pool.wait_ge(su_sb, b * PA + a + 1)
                pool.wait_ge(gates_sb, j + 1)
                pool.tensor_tensor(h, h, gates[:, j % 2, :], ALU.mult).then_inc(h3_sb, 1)

        @block.scalar
        def _(eng):
            eng.wait_ge(zeroed, 2)
            bkv = I["L0_xattn_bkv"].rearrange("(g h x) -> g h x", g=G, h=HG)
            for r in range(3):
                dst = slice(GW * r, GW * (r + 1))
                eng.dma_start(rows[R_BK:R_BK + G, dst].rearrange("g (h d) -> g h d", h=HG),
                              bkv[:, :, 0:HD]).then_inc(rows_in, 16)
            for at, n in ((R_BK + G, "L1_xattn_bk"), (R_BQ, "L0_xattn_bq"), (R_BQ + G, "L1_xattn_bq")):
                eng.dma_start(rows[at:at + G, 0:3 * GW].rearrange("g (r x) -> g r x", r=3),
                              I[n].rearrange("(g o x) -> g o x", g=G, o=1).broadcast_to([G, 3, GW])).then_inc(rows_in, 16)
            eng.dma_start(rows[R_BV:R_BV + 1, :].rearrange("o (h d) -> o h d", h=H),
                          I["L0_xattn_bkv"].rearrange("(o h x) -> o h x", o=1, h=H)[:, :, HD:2 * HD]).then_inc(rows_in, 16)
            eng.dma_start(rows[R_BV + 1:R_BV + 2, :], I["L1_xattn_bv"].rearrange("(o n) -> o n", o=1)).then_inc(rows_in, 16)
            eng.dma_start(rows[R_B1:R_B1 + E * FC, :], I["L0_ffn_b1"].rearrange("e (c p) -> (e c) p", p=P)).then_inc(rows_in, 16)
            eng.dma_start(rows[R_LNG:R_LNG + E, :], I["L0_ffn_ln_g"]).then_inc(rows_in, 16)
            eng.dma_start(rows[R_LNB:R_LNB + E, :], I["L0_ffn_ln_b"]).then_inc(rows_in, 16)
            eng.dma_start(rows[R_GW:R_GW + E, :], I["L1_ffn_gate_w"]).then_inc(rows_in, 16)
            for i, (n, j) in enumerate((("g_xattn", 0), ("g_ffn", 2))):
                eng.dma_start(gains[:, j:j + 2], I[n].rearrange("(o n) -> o n", o=1).broadcast_to([P, 2])).then_inc(small_in, 16)
            eng.dma_start(bpb[:, 0, :], I["L0_xattn_bp"].rearrange("(o n) -> o n", o=1).broadcast_to([P, P])).then_inc(small_in, 16)
            eng.dma_start(bpb[:, 1, :], I["L1_xattn_bo"].rearrange("(o n) -> o n", o=1).broadcast_to([P, P])).then_inc(small_in, 16)
            eng.wait_ge(small_in, 16 * 4)
            eng.activation(tg[:, :], gains[:, :], ACT.Tanh).then_inc(tg_sb, 1)

            def key_rows(l):
                for g in range(G):
                    eng.wait_ge(k_ps, G * l + g + 1)
                    bias = cols[:, R_BK + G * l + g:R_BK + G * l + g + 1]
                    eng.activation(kst[:, l, g, :], ps[:, KB[l][g], 0:B * S], ACT.Identity, bias=bias)
                    third = slice(2 * GW, 3 * GW)
                    eng.activation(khi[third, g, :], ps[third, KB[l][g], 0:B * S], ACT.Identity,
                                   bias=bias[third]).then_inc(kh_sb, 1)

            key_rows(0)

            def x_copy(s):
                eng.wait_ge(xt_ps, s + 1)
                eng.activation(xT[:, :], ps[:, F, :], ACT.Copy).then_inc(xt_sb, 1)

            def q_upper(s, g):
                l = s // B
                eng.wait_ge(q_ps, G * s + g + 1)
                if s >= 2:
                    eng.wait_ge(s_ps, G * C * (s - 1))
                if s >= 1:
                    eng.wait_ge(z_sb, G * (s - 1) + g + 1)
                bias = cols[:, R_BQ + G * l + g:R_BQ + G * l + g + 1]
                eng.activation(Z[0:3 * GW, s % 2, g, :], ps[0:3 * GW, QB[g], :], ACT.Identity, bias=bias[0:3 * GW])
                eng.activation(qf[GW:2 * GW, g, :], ps[GW:2 * GW, QB[g], :], ACT.Identity,
                               bias=bias[GW:2 * GW]).then_inc(qh_sb, 1)

            def m_rows(s):
                eng.wait_ge(mt_ps, s + 1)
                if s >= 2:
                    eng.wait_ge(s_ps, G * C * (s - 1))
                for g in range(G):
                    eng.activation(Z[3 * GW:3 * GW + H, s % 2, g, :], ps[3 * GW:3 * GW + H, F, :],
                                   ACT.Copy).then_inc(mz_sb, 1)

            def exps(s, c, g):
                i = G * C * s + G * c + g
                n = C * s + c
                eng.wait_ge(s_ps, i + 1)
                if n >= 2 and g == 0:
                    eng.wait_ge(pv_done, n - 1)
                eng.activation(Pr[:, n % 2, g, :], ps[:, S0 + i % 2, :], ACT.Exp, scale=SCALE).then_inc(p_sb, 1)

            def o_copy(s):
                eng.wait_ge(pv_done, C * (s + 1))
                if s:
                    eng.wait_ge(proj_ps, s)
                eng.activation(oT[:, :], ps[:, O, :], ACT.Copy).then_inc(o_sb, 1)

            def route_copy(b):
                eng.wait_ge(xa_ps, b + 1)
                eng.activation(xaT[:, :], ps[:, RB, :], ACT.Copy).then_inc(xa_sb, 1)

            def route_exp(b):
                eng.wait_ge(dif_sb, b + 1)
                eng.activation(e2[:, :], t4[:, :], ACT.Exp).then_inc(e2_sb, 1)

            def scale_w1(s):
                eng.wait_ge(b1_ps, s // 2 + 1)
                for e in (2 * s, 2 * s + 1):
                    w = w12[:, e, W1_AT:W1_AT + FF]
                    eng.activation(w, w, ACT.Copy, scale=cols[:, R_LNG + e:R_LNG + e + 1]).then_inc(w1_scaled, 1)

            def weigh(b):
                eng.wait_ge(gathered[b], 16 * 2 * T)
                for y, w in ((y1, w_first), (y2, w_second)):
                    for t in range(T):
                        row = y[:, T * b + t, :]
                        ins = eng.activation(row, row, ACT.Copy, scale=w[:, b, t:t + 1])
                ins.then_inc(weighted, 1)

            def mix_copy(b):
                eng.wait_ge(t3_ps, b + 1)
                eng.activation(x3T[:, b, :], ps[:, RB, :], ACT.Copy).then_inc(t3_sb, 1)

            def mix_exp(b):
                eng.wait_ge(l3_sb, b + 1)
                eng.activation(ex[:, :, :], lw[:, :, :], ACT.Exp).then_inc(e3_sb, 1)

            def mix_gates(b):
                eng.wait_ge(gates_zero, 1)
                eng.wait_ge(c3_ps, b + 1)
                at = b % 2 * HP
                eng.activation(cwT[at:at + E, b // 2, :], ps[at:at + E, RB, :], ACT.Copy).then_inc(c3h_sb, 1)

            def mix_silu(i):
                eng.wait_ge(g_ps, i + 1)
                if i >= 2:
                    eng.wait_ge(su_sb, i - 1)
                eng.activation(sg[:, i % 2, :], ps[:, G3 + i % 2, :], ACT.Silu).then_inc(sg_sb, 1)
                b, a = divmod(i, PA)
                if a < PAIRS:
                    j = b * PAIRS + a
                    eng.wait_ge(c_ps, j + 1)
                    if j >= 2:
                        eng.wait_ge(h3_sb, j - 1)
                    eng.activation(gates[:, j % 2, :], ps[:, C3, :], ACT.Copy).then_inc(gates_sb, 1)

            def attention(l):
                s0 = l * B
                x_copy(s0)
                for g in range(G):
                    q_upper(s0, g)
                if l == 1:
                    weigh(1)
                m_rows(s0)
                for s in range(s0, s0 + B):
                    more, prev = s + 1 < s0 + B, s > s0
                    p = s - s0 - 1
                    for i in range(G * C):
                        exps(s, i // G, i % G)
                        if more and i == 1:
                            x_copy(s + 1)
                        if more and i == 3:
                            q_upper(s + 1, 0)
                            q_upper(s + 1, 1)
                        if more and i == 5:
                            q_upper(s + 1, 2)
                            q_upper(s + 1, 3)
                        if l == 1 and s + 2 < s0 + B and i == 8:
                            weigh(s + 2 - s0)
                        if l == 1 and s >= s0 + 2 and i == 8:
                            mix_gates(s - s0 - 2)
                        if l == 0 and prev and i == 8:
                            route_copy(p)
                    if more:
                        m_rows(s + 1)
                    if l == 1 and prev:
                        mix_copy(p)
                    o_copy(s)
                    if l == 0:
                        if not more:
                            key_rows(1)
                        if prev:
                            route_exp(p)
                        if s < 2:
                            scale_w1(s)
                    elif prev:
                        mix_exp(p)

            attention(0)
            route_copy(B - 1)
            scale_w1(2)
            scale_w1(3)
            route_exp(B - 1)
            tails(eng, range(1, E, 2), tails_act)

            def gelu(i, par, ring):
                eng.wait_ge(h_ps, i + 1)
                if not isinstance(i, int) or i >= 2:
                    eng.wait_ge(y_ps, i - 1)
                for c in range(FC):
                    ins = eng.activation(hid[:, par, c, :], ps[:, HB + par, P * c:P * (c + 1)], ACT.Gelu,
                                         bias=wcur[:, ring, B1_AT + c:B1_AT + c + 1])
                ins.then_inc(a_sb, 1)

            gelu(0, 0, 0)
            with eng.Fori(0, (NT - 3) // 4) as k:
                for u in range(1, 5):
                    gelu(k * 4 + u, u % 2, u % 4)
            gelu(NT - 2, (NT - 2) % 2, (NT - 2) % 4)
            gelu(NT - 1, (NT - 1) % 2, (NT - 1) % 4)
            attention(1)
            for i in range(B * PA):
                mix_silu(i)
                if i == 5:
                    mix_gates(B - 2)
                if i == 7:
                    mix_copy(B - 1)
                if i == 8:
                    mix_exp(B - 1)
                if i == 12:
                    mix_gates(B - 1)

        @block.tensor
        def _(pe):
            def mm(o, w, x, start=True, stop=True):
                return nc.tensor.matmul(o, w, x, start=start, stop=stop)

            pe.wait_ge(pstep, 2)
            pe.wait_ge(rows_in, 16 * 12)
            nc.tensor.transpose(ps[:, F, 0:ROWS], rows[:, :], ident[0:ROWS, 0:ROWS]).then_inc(cols_ps, 1)
            pe.wait_ge(ctx_in, 16)
            for b in range(B):
                ins = nc.tensor.transpose(ps[:, F + 1, S * b:S * (b + 1)], ctx_sb[:, b, :], ident[0:S, 0:S])
            ins.then_inc(ctx_ps, 1)

            def key_product(l, g):
                pe.wait_ge(prep_sb, l + 1)
                if l == 1 and g >= 2:
                    pe.wait_ge(kh_sb, G + g - 1)
                mm(ps[:, KB[l][g], 0:B * S], wkS[:, l, g, :], ctxT[:, :, 0, :]).then_inc(k_ps, 1)

            def bias_product(l):
                mm(ps[:, S0, 0:P], bvb[:, l, :], wp[:, l, :]).then_inc(bv_ps, 1)

            for g in range(G):
                key_product(0, g)
            bias_product(0)
            pe.wait_ge(kh_sb, G)
            pe.wait_ge(bpx_sb, 1)

            def front_x(s):
                pe.wait_ge(xn_ready, s + 1)
                if s % B:
                    pe.wait_ge(mz_sb, G * s)
                for t in range(T):
                    ins = nc.tensor.transpose(ps[:, F, P * t:P * (t + 1)], xn[:, T * (s % B) + t, :], ident[:, :])
                ins.then_inc(xt_ps, 1)

            def front_v(s):
                l, b = divmod(s, B)
                pe.wait_ge(wv_sb, l + 1)
                rep = ctxT[:, b, :, :].rearrange("p r k -> p (r k)")
                for c in range(C):
                    ins = mm(ps[:, F + 1, P * c:P * (c + 1)], rep[:, CH[c]:CH[c] + P], wv[:, l, :])
                ins.then_inc(v_ps, 1)

            def front_q(s, g):
                l = s // B
                if g == 0:
                    pe.wait_ge(xt_sb, s + 1)
                if g == 2:
                    pe.wait_ge(v_sb, s + 1)
                if g == 3:
                    pe.wait_ge(qh_sb, G * s + 1)
                mm(ps[:, QB[g], :], wqS[:, l, g, :], xT[:, :]).then_inc(q_ps, 1)

            def front_mx(s, g):
                for t in range(T):
                    j = T * g + t
                    if t == 0:
                        pe.wait_ge(k4_ready, G * s + g + 1)
                        pe.wait_ge(z_sb, G * s + g + 1)
                    if j < 3:
                        pe.wait_ge(qh_sb, G * (s + 1))
                    else:
                        pe.wait_ge(mx_done, T * G * s + j - 2)
                    mm(ps[:, F + j % 3, 0:KG], Z[0:3 * GW, s % 2, g, P * t:P * (t + 1)],
                       K4[0:3 * GW, s % 2, g, 0:KG]).then_inc(mx_ps, 1)

            def front_m(s):
                pe.wait_ge(mx_done, T * G * (s + 1))
                for t in range(T):
                    ins = mm(ps[:, F, P * t:P * (t + 1)], mpad[:, t, :], ident[:, :])
                ins.then_inc(mt_ps, 1)

            def scores(s, c, g):
                i = G * C * s + G * c + g
                if c == 0:
                    pe.wait_ge(mz_sb, G * s + g + 1)
                if i >= 2:
                    pe.wait_ge(p_sb, i - 1)
                mm(ps[:, S0 + i % 2, :], K4[0:K1, s % 2, g, P * c:P * (c + 1)],
                   Z[0:K1, s % 2, g, :]).then_inc(s_ps, 1)

            def pv(s, c):
                n = C * s + c
                pe.wait_ge(p_sb, G * (n + 1))
                if c == 0:
                    pe.wait_ge(v_sb, s + 1)
                    if s:
                        pe.wait_ge(res_done, s)
                for g in range(G):
                    at = slice(GW * g, GW * (g + 1))
                    nc.tensor.matmul(ps[at, O, :], V4[:, s % 2, c, at], Pr[:, n % 2, g, :],
                                     start=c == 0, stop=c == C - 1, tile_position=(0, GW * g))
                for g in range(G):
                    for t in range(T):
                        ins = nc.tensor.matmul(ps[GW * t:GW * (t + 1), D, 0:P], maskH[:, c, g, :, :].rearrange("p a h -> p (a h)"),
                                               Pr[:, n % 2, g, P * t:P * (t + 1)], start=c == 0 and g == 0,
                                               stop=c == C - 1 and g == G - 1, tile_position=(0, GW * t))
                ins.then_inc(pv_done, 1)

            def spread_out(s):
                pe.wait_ge(rden_sb, s + 1)
                for t in range(T):
                    ins = mm(ps[:, D, P * t:P * (t + 1)], spread[:, t, :], rden[:, :])
                ins.then_inc(spread_ps, 1)

            def w1_bias(half):
                pe.wait_ge(w1_in, 16 * E)
                bank = (RB, F + 2)[half]
                for e in range(half * E // 2, (half + 1) * E // 2):
                    for c in range(FC):
                        i = FC * e + c
                        ins = mm(ps[:, bank, i:i + 1], w12[:, e, W1_AT + P * c:W1_AT + P * (c + 1)], cols[:, R_LNB + e:R_LNB + e + 1])
                ins.then_inc(b1_ps, 1)

            def project(s):
                pe.wait_ge(ot_sb, s + 1)
                for t in range(T):
                    ins = mm(ps[:, D, P * t:P * (t + 1)], oT[:, P * t:P * (t + 1)], wpx[:, s // B, :])
                ins.then_inc(proj_ps, 1)

            def transposed(bank, src, done):
                for t in range(T):
                    ins = nc.tensor.transpose(ps[:, bank, P * t:P * (t + 1)], src(t), ident[:, :])
                ins.then_inc(done, 1)

            def route_x(b):
                pe.wait_ge(xa_ready, b + 1)
                if b:
                    pe.wait_ge(row_sb, b)
                else:
                    pe.wait_ge(b1_sb, 1)
                transposed(RB, lambda t: xa[:, t, :], xa_ps)

            def route_logits(b):
                if b == 0:
                    pe.wait_ge(router_in, 16 * 3)
                pe.wait_ge(xa_sb, b + 1)
                for t in range(T):
                    ins = mm(ps[:, RB, E * t:E * (t + 1)], xaT[:, P * t:P * (t + 1)], rw[:, :])
                ins.then_inc(lg_ps, 1)

            def route_places(b):
                pe.wait_ge(both_sb, b + 1)
                mm(ps[:, RB, 0:T * E], earlier[:, :], both[:, :, :].rearrange("p t e -> p (t e)"), True, False)
                mm(ps[:, RB, 0:T * E], ones[:, :], before[:, 0:T, :].rearrange("p t e -> p (t e)"),
                   False, True).then_inc(place_ps, 1)

            def mix_x(b):
                pe.wait_ge(n3_ready, b + 1)
                if b:
                    pe.wait_ge(c3l_sb, b)
                else:
                    pe.wait_ge(get_sb, 1)
                transposed(RB, lambda t: xn[:, T * b + t, :], t3_ps)

            def mix_logits(b):
                pe.wait_ge(t3_sb, b + 1)
                for t in range(T):
                    ins = mm(ps[:, RB, E * t:E * (t + 1)], x3T[:, b, P * t:P * (t + 1)], cols[:, R_GW:R_GW + E])
                ins.then_inc(l3_ps, 1)

            def mix_gates(b):
                pe.wait_ge(c3_sb, b + 1)
                transposed(RB, lambda t: gpad[:, t, :], c3_ps)

            def halves_product(bank, w, x):
                mm(ps[:, bank, :], w[:, 0, :], x[:, 0, :], True, False)
                mm(ps[:, bank, :], w[:, 0, :], x[:, 1, :], False, False)
                return mm(ps[:, bank, :], w[:, 1, :], x[:, 0, :], False, True)

            def mix_pair(i):
                b, a = divmod(i, PA)
                if i >= 2:
                    pe.wait_ge(sg_sb, i - 1)
                if i == 0:
                    pe.wait_ge(wr_sb, 1)
                if a == 0:
                    pe.wait_ge(xr_sb, b + 1)
                halves_product(G3 + i % 2, wr[0][:, :, P * a:P * (a + 1)], xr[b]).then_inc(g_ps, 1)
                if i >= 2:
                    pe.wait_ge(su_sb, i - 1)
                if i == 0:
                    pe.wait_ge(wr_sb, 2)
                halves_product(U3 + i % 2, wr[1][:, :, P * a:P * (a + 1)], xr[b]).then_inc(u_ps, 1)
                if a < PAIRS:
                    if a == 0:
                        pe.wait_ge(c3l_sb, b + 1)
                    if b or a:
                        pe.wait_ge(gates_sb, b * PAIRS + a)
                    half = slice(b % 2 * HP, b % 2 * HP + HP)
                    mm(ps[:, C3, :], pickr[half, a, :], cwT[half, b // 2, :]).then_inc(c_ps, 1)

            def mix_out(b):
                pe.wait_ge(su_sb, (b + 1) * PA)
                pe.wait_ge(h3_sb, (b + 1) * PAIRS)
                if b >= 2:
                    pe.wait_ge(x_out, b - 1)
                for t in range(T):
                    for a in range(PA):
                        ins = mm(ps[:, Y3 + b % 2, P * t:P * (t + 1)], hT[:, b % 2 * PA + a, P * t:P * (t + 1)],
                                 wd1[:, a, :], a == 0, a == PAIRS)
                ins.then_inc(y3_ps, 1)

            def attention(l):
                s0 = l * B
                front_x(s0)
                front_v(s0)
                for g in range(G):
                    front_q(s0, g)
                if l == 0:
                    w1_bias(0)
                for g in range(G):
                    front_mx(s0, g)
                front_m(s0)
                for s in range(s0, s0 + B):
                    n, more, prev = s + 1, s + 1 < s0 + B, s > s0
                    p = s - s0 - 1
                    scores(s, 0, 0)
                    scores(s, 0, 1)
                    if prev:
                        spread_out(s - 1)
                    if more:
                        front_x(n)
                    scores(s, 0, 2)
                    scores(s, 0, 3)
                    if more:
                        front_v(n)
                    if prev:
                        project(s - 1)
                    if more:
                        front_q(n, 0)
                        front_q(n, 1)
                    if l == 0 and not more:
                        pe.wait_ge(attw1_in, 16 * 4)
                        for i in range(4):
                            ins = nc.tensor.transpose(ps[:, F + 2, P * i:P * (i + 1)], wnat[:, i, :], ident[:, :])
                        ins.then_inc(wt_ps, 1)
                    scores(s, 1, 0)
                    scores(s, 1, 1)
                    if more:
                        front_q(n, 2)
                        front_q(n, 3)
                    pv(s, 0)
                    scores(s, 1, 2)
                    scores(s, 1, 3)
                    if more:
                        front_mx(n, 0)
                    if l == 0 and prev:
                        route_x(p)
                    scores(s, 2, 0)
                    if more:
                        front_mx(n, 1)
                    if l == 1 and s >= s0 + 2:
                        mix_gates(s - s0 - 2)
                    scores(s, 2, 1)
                    pv(s, 1)
                    if l == 0 and not more:
                        key_product(1, 0)
                        key_product(1, 1)
                    if more:
                        front_mx(n, 2)
                    if l == 0 and prev:
                        route_logits(p)
                    scores(s, 2, 2)
                    if more:
                        front_mx(n, 3)
                    scores(s, 2, 3)
                    if more:
                        front_m(n)
                    if l == 1 and prev:
                        mix_x(p)
                    pv(s, 2)
                    if prev:
                        (route_places if l == 0 else mix_logits)(p)
                    if l == 0 and not more:
                        key_product(1, 2)
                        key_product(1, 3)
                        bias_product(1)

            attention(0)
            spread_out(B - 1)
            project(B - 1)
            w1_bias(1)
            route_x(B - 1)
            route_logits(B - 1)
            route_places(B - 1)
            pe.wait_ge(row_sb, B)
            mm(ps[:, RB, 0:E], ones[:, :], before[:, T, :]).then_inc(count_ps, 1)

            def tile_x(i, par, ring, turn):
                pe.wait_ge(xg_in[ring], (turn + 1) * 16)
                if not isinstance(i, int) or i >= 2:
                    pe.wait_ge(xg_sb, i - 1)
                nc.tensor.transpose(ps[:, TX + par, 0:P], xg[:, ring, :], ident[:, :]).then_inc(t_ps, 1)

            def tile_hidden(i, par, ring):
                pe.wait_ge(xg_sb, i + 1)
                pe.wait_ge(wc_sb, i + 1)
                if not isinstance(i, int) or i >= 2:
                    pe.wait_ge(a_sb, i - 1)
                for c in range(FC):
                    ins = mm(ps[:, HB + par, P * c:P * (c + 1)], wcur[:, ring, W1_AT + P * c:W1_AT + P * (c + 1)],
                             xgT[:, par, :])
                ins.then_inc(h_ps, 1)

            def tile_out(i, par, ring):
                pe.wait_ge(a_sb, i + 1)
                if not isinstance(i, int) or i >= 2:
                    pe.wait_ge(yo_sb, i - 1)
                for c in range(FC):
                    ins = mm(ps[:, YB + par, 0:P], hid[:, par, c, :],
                             wcur[:, ring, W2_AT + P * c:W2_AT + P * (c + 1)], c == 0, c == FC - 1)
                ins.then_inc(y_ps, 1)

            pe.wait_ge(kh_sb, G * L)
            pe.wait_ge(bpx_sb, L)
            tile_x(0, 0, 0, 0)
            tile_x(1, 1, 1, 0)
            tile_hidden(0, 0, 0)
            for u in range(1, 5):
                tile_x(u + 1, (u + 1) % 2, (u + 1) % 4, (u + 1) // 4)
                tile_hidden(u, u % 2, u % 4)
                tile_out(u - 1, (u - 1) % 2, (u - 1) % 4)
            with pe.Fori(1, (NT - 3) // 4) as k:
                for u in range(1, 5):
                    tile_x(k * 4 + (u + 1), (u + 1) % 2, (u + 1) % 4, k + (u + 1) // 4)
                    tile_hidden(k * 4 + u, u % 2, u % 4)
                    tile_out(k * 4 + (u - 1), (u - 1) % 2, (u - 1) % 4)
            i = NT - 2
            tile_x(i + 1, (i + 1) % 2, (i + 1) % 4, (i + 1) // 4)
            tile_hidden(i, i % 2, i % 4)
            tile_out(i - 1, (i - 1) % 2, (i - 1) % 4)
            i = NT - 1
            tile_hidden(i, i % 2, i % 4)
            tile_out(i - 1, (i - 1) % 2, (i - 1) % 4)
            tile_out(i, i % 2, i % 4)
            pe.wait_ge(yo_sb, NT)
            attention(1)
            pe.wait_ge(m1w_in, M1W)
            pe.wait_ge(p_sb, G * C * LN)
            for i in range(B * PA):
                mix_pair(i)
                if i == 0:
                    spread_out(LN - 1)
                    project(LN - 1)
                if i == 5:
                    mix_gates(B - 2)
                    pe.wait_ge(res_done, LN)
                if i == 7:
                    mix_x(B - 1)
                if i == 8:
                    mix_logits(B - 1)
                if i == 12:
                    mix_gates(B - 1)
                if i and i % PA == 0:
                    mix_out(i // PA - 1)
            pe.wait_ge(x_out, B - 1)
            for a in range(PA):
                if a < PAIRS:
                    pe.wait_ge(h3_sb, (B - 1) * PAIRS + a + 1)
                else:
                    pe.wait_ge(su_sb, B * PA)
                for t in range(T):
                    bank = Y3 + (B - 1 + t // (T // 2)) % 2
                    ins = mm(ps[:, bank, P * t:P * (t + 1)], hT[:, (B - 1) % 2 * PA + a, P * t:P * (t + 1)],
                             wd1[:, a, :], a == 0 and t % (T // 2) == 0, a == PAIRS and not (t + 1) % (T // 2))
                    if a == PAIRS and (t + 1) % (T // 2) == 0:
                        ins.then_inc(y3_ps, 1)

        @block.vector
        def _(dve):
            n = [0]

            def link(ins):
                n[0] += 1
                ins.then_inc(dstep, 1)
                dve.wait_ge(dstep, n[0])

            def rsqrt(m):
                v, y, t = ve[:, 0:m], rs[:, 0:m], rt[:, 0:m]
                link(dve.tensor_scalar(y.bitcast(I32), v.bitcast(I32), -0.5, float(RSQRT_GUESS),
                                       ALU.mult, ALU.add))
                for _ in range(3):
                    link(dve.scalar_tensor_tensor(out=t, in0=y, scalar=-0.5, in1=y, op0=ALU.mult, op1=ALU.mult))
                    link(dve.tensor_tensor(t, t, v, ALU.mult))
                    link(dve.scalar_tensor_tensor(out=y, in0=t, scalar=1.5, in1=y, op0=ALU.add, op1=ALU.mult))

            def from_stats(m):
                for t in range(m):
                    ins = dve.bn_aggr(mv[:, t, :], st6w[:, t, :])
                link(ins)
                link(dve.tensor_scalar(ve[:, 0:m], mv[:, 0:m, 1], EPS, None, ALU.add))

            def moments(m, src):
                for t in range(m):
                    ins = dve.bn_stats(st6w[:, t, :], src(t))
                link(ins)
                from_stats(m)

            def scaled(m, dst, src, at=0):
                for t in range(m):
                    ins = dve.tensor_scalar(dst(t), src(t), mv[:, t, 0:1], rs[:, at + t:at + t + 1], ALU.subtract, ALU.mult)
                return ins

            def norm(m, dst, src):
                moments(m, src)
                rsqrt(m)
                return scaled(m, dst, src)

            def ranks(x, m, into):
                k = [P, T, m, m]
                a, c = cmpa[:, 0:T * m * m], cmpb[:, 0:T * m * m]
                shaped = a.rearrange("p (t i j) -> p t i j", t=T, i=m)
                link(dve.tensor_tensor(shaped, x.unsqueeze(2).broadcast_to(k), x.unsqueeze(3).broadcast_to(k), ALU.subtract))
                link(dve.scalar_tensor_tensor(out=c, in0=a, scalar=0.0, in1=tri[m][:, :, :, :].rearrange("p t i j -> p (t i j)"),
                                              op0=ALU.is_ge, op1=ALU.mult))
                link(dve.scalar_tensor_tensor(out=a, in0=a, scalar=0.0, in1=c, op0=ALU.is_gt, op1=ALU.max))
                link(dve.tensor_reduce(into, shaped, AX.X, ALU.add))

            dve.memset(wkS[:, :, :, 3 * GW:P], 0.0)
            dve.memset(wqS[:, :, :, 3 * GW:P], 0.0)
            link(dve.memset(K4[:, :, :, KG:C * P].bitcast(F32), 0.0))

            def input_norms(b, count):
                for i in range(b, b + count):
                    dve.wait_ge(x_in[i], 16)
                norm(count * T, lambda t: xn[:, T * b + t, :], lambda t: X[:, T * b + t, :]).then_inc(xn_ready, count)

            input_norms(0, 1)
            dve.wait_ge(cols_ps, 1)
            link(dve.tensor_copy(cols[:, :], ps[:, F, 0:ROWS]))
            dve.wait_ge(ctx_ps, 1)
            dve.tensor_copy(ctxT[:, :, :, :], ps[:, F + 1, 0:B * S].rearrange("p (b k) -> p b k", b=B)
                            .unsqueeze(2).broadcast_to([P, B, 3, S]))
            dve.wait_ge(attw_in, 16 * 3)
            kv0 = wkv0[:, :].rearrange("p (g h x) -> p g h x", g=G, h=HG)

            def stack(l, wk, wq):
                for dst, src in ((wkS, wk), (wqS, wq)):
                    for g in range(G):
                        dve.tensor_copy(dst[:, l, g, 0:3 * GW].rearrange("p (r h d) -> p r h d", r=3, h=HG),
                                        src(g).unsqueeze(1).broadcast_to([P, 3, HG, HD]))
                return dve.tensor_copy(bvb[:, l, :], cols[:, R_BV + l:R_BV + l + 1].broadcast_to([P, P]))

            def lower_keys(l):
                for g in range(G):
                    dve.wait_ge(kh_sb, G * l + g + 1)
                    k = kst[2 * GW:3 * GW, l, g, :]
                    dve.tensor_tensor(k, k, khi[2 * GW:3 * GW, g, :].bitcast(F32), ALU.subtract).then_inc(k_sb, 1)
                dve.wait_ge(tg_sb, 1)
                dve.tensor_scalar(wpx[:, l, :], wp[:, l, :], tg[:, l:l + 1], None, ALU.mult)
                dve.wait_ge(bv_ps, l + 1)
                link(dve.tensor_tensor(bpb[:, l, :], ps[:, S0, 0:P], bpb[:, l, :], ALU.add))
                dve.tensor_scalar(bpx[:, l, :], bpb[:, l, :], tg[:, l:l + 1], None, ALU.mult).then_inc(bpx_sb, 1)

            stack(0, lambda g: kv0[:, g, :, 0:HD],
                  lambda g: wq0[:, GW * g:GW * (g + 1)].rearrange("p (h d) -> p h d", h=HG)).then_inc(prep_sb, 1)
            dve.tensor_copy(wv[:, 0, :].rearrange("p (g h d) -> p g h d", g=G, h=HG), kv0[:, :, :, HD:2 * HD]).then_inc(wv_sb, 1)
            lower_keys(0)
            dve.wait_ge(consts, 1)

            def v_mask(s):
                dve.wait_ge(v_ps, s + 1)
                if s >= 2:
                    dve.wait_ge(pv_done, C * (s - 1))
                dve.tensor_tensor(V4[:, s % 2, :, :], ps[:, F + 1, 0:C * P].rearrange("p (c n) -> p c n", c=C),
                                  maskV[:, :, :], ALU.mult).then_inc(v_sb, 1)

            def maxima(s, g):
                for t in range(T):
                    j = T * g + t
                    dve.wait_ge(mx_ps, T * G * s + j + 1)
                    at = 3 * GW + HG * g
                    dve.tensor_reduce(mpad[:, t, at:at + HG], ps[:, F + j % 3, 0:KG].rearrange("p (h k) -> p h k", h=HG),
                                      AX.X, ALU.max).then_inc(mx_done, 1)

            def reciprocals(s):
                dve.wait_ge(pv_done, C * (s + 1))
                if s:
                    dve.wait_ge(spread_ps, s)
                dve.reciprocal(rden[:, :], ps[:, D, 0:P]).then_inc(rden_sb, 1)

            def normalise(s):
                dve.wait_ge(spread_ps, s + 1)
                dve.wait_ge(o_sb, s + 1)
                dve.tensor_tensor(oT[:, :], oT[:, :], ps[:, D, :], ALU.mult).then_inc(ot_sb, 1)

            def residual(s):
                l, b = divmod(s, B)
                xb = X[:, T * b:T * (b + 1), :]
                dve.wait_ge(proj_ps, s + 1)
                dve.wait_ge(bias_sb, s + 1)
                ins = dve.tensor_tensor(xb, xb, ps[:, D, :].rearrange("p (t n) -> p t n", t=T), ALU.add)
                ins.then_inc(res_done, 1)

            def b1_copy(half):
                dve.wait_ge(b1_ps, half + 1)
                experts = slice(half * E // 2, (half + 1) * E // 2)
                at = slice(FC * experts.start, FC * experts.stop)
                b1 = cols[:, R_B1 + at.start:R_B1 + at.stop]
                dve.tensor_tensor(w12[:, experts, B1_AT:B1_AT + FC],
                                  ps[:, (RB, F + 2)[half], at].rearrange("p (e c) -> p e c", c=FC),
                                  b1.rearrange("p (e c) -> p e c", c=FC), ALU.add).then_inc(b1_sb, 1)

            def route_norms(b):
                dve.wait_ge(res_done, b + 1)
                if b >= 2:
                    dve.wait_ge(scattered[b - 2], 16 * 2 * T)
                moments(T, lambda t: X[:, T * b + t, :])
                link(dve.scalar_tensor_tensor(out=ve[:, T:2 * T], in0=ve[:, 0:T], scalar=EPS, in1=mv[:, 0:T, 1],
                                              op0=ALU.mult, op1=ALU.add))
                rsqrt(2 * T)
                scaled(T, lambda t: xa[:, t, :], lambda t: X[:, T * b + t, :]).then_inc(xa_ready, 1)
                link(scaled(T, lambda t: xh[:, b % 2, t, :], lambda t: X[:, T * b + t, :], T))
                xb = X[:, T * b:T * (b + 1), :]
                link(dve.scalar_tensor_tensor(out=xb, in0=xa[:, :, :], scalar=tg[:, 2:3], in1=xb,
                                              op0=ALU.mult, op1=ALU.add))

            def route_choice(b):
                dve.wait_ge(lg_ps, b + 1)
                link(dve.tensor_tensor(lg[:, :, :], ps[:, RB, 0:T * E].rearrange("p (t e) -> p t e", t=T),
                                       rb[:, :].unsqueeze(1).broadcast_to([P, T, E]), ALU.add))
                dve.tensor_reduce(l1[:, :], lg[:, :, :], AX.X, ALU.max)
                ranks(lg[:, :, :], E, rank[:, :, :])
                dve.tensor_scalar(both[:, :, :], rank[:, :, :], 2.0, None, ALU.is_lt)
                dve.tensor_scalar(first[:, b, :, :], rank[:, :, :], 0.0, None, ALU.is_equal)
                link(dve.tensor_scalar(second[:, b, :, :], rank[:, :, :], 1.0, None, ALU.is_equal))
                if b:
                    dve.wait_ge(e2_sb, b)
                link(dve.tensor_tensor(lw[:, :, :], second[:, b, :, :], lg[:, :, :], ALU.mult))
                link(dve.tensor_reduce(t4[:, :], lw[:, :, :], AX.X, ALU.add))
                dve.tensor_tensor(t4[:, :], t4[:, :], l1[:, :], ALU.subtract).then_inc(dif_sb, 1)
                if b:
                    link(dve.tensor_copy(before[:, 0, :], before[:, T, :]))
                for t in range(T):
                    ins = dve.tensor_tensor(before[:, t + 1, :], before[:, t, :], both[:, t, :], ALU.add)
                    if t + 1 < T:
                        link(ins)
                ins.then_inc(both_sb, 1)

            def route_rows(b):
                dve.wait_ge(place_ps, b + 1)
                link(dve.tensor_tensor(place[:, b, :, :], ps[:, RB, 0:T * E].rearrange("p (t e) -> p t e", t=T),
                                       region[:, :].unsqueeze(1).broadcast_to([P, T, E]), ALU.add))
                dve.tensor_tensor(lw[:, :, :], first[:, b, :, :], place[:, b, :, :], ALU.mult)
                link(dve.tensor_tensor(ex[:, :, :], second[:, b, :, :], place[:, b, :, :], ALU.mult))
                dve.tensor_reduce(rowF[:, 0, :], lw[:, :, :], AX.X, ALU.add)
                link(dve.tensor_reduce(rowF[:, 1, :], ex[:, :, :], AX.X, ALU.add))
                dve.tensor_copy(rowI[:, :, b, :], rowF[:, :, :]).then_inc(row_sb, 1)
                dve.wait_ge(e2_sb, b + 1)
                link(dve.tensor_scalar(l1[:, :], e2[:, :], 1.0, None, ALU.add))
                link(dve.reciprocal(l1[:, :], l1[:, :]))
                link(dve.tensor_scalar(w_first[:, b, :], l1[:, :], tg[:, 2:3], None, ALU.mult))
                link(dve.tensor_tensor(w_second[:, b, :], w_first[:, b, :], e2[:, :], ALU.mult))

            def mix_norm(b):
                dve.wait_ge(res_done, B + b + 1)
                norm(T, lambda t: xn[:, T * b + t, :], lambda t: X[:, T * b + t, :]).then_inc(n3_ready, 1)

            def mix_logits(b):
                dve.wait_ge(l3_ps, b + 1)
                dve.tensor_scalar(lw[:, :, :], ps[:, RB, 0:T * E].rearrange("p (t e) -> p t e", t=T),
                                  -1.0, 88.0, ALU.mult, ALU.min).then_inc(l3_sb, 1)

            def mix_choice(b):
                dve.wait_ge(e3_sb, b + 1)
                link(dve.tensor_scalar(ex[:, :, :], ex[:, :, :], 1.0, None, ALU.add))
                link(dve.reciprocal(ex[:, :, :], ex[:, :, :]))
                link(dve.tensor_tensor(lg[:, :, :], ex[:, :, :], cb[:, :].unsqueeze(1).broadcast_to([P, T, E]), ALU.add))
                two = lg[:, :, :].rearrange("p t (g e) -> p t g e", e=2)
                link(dve.tensor_tensor(gsc[:, :, :], two[:, :, :, 0], two[:, :, :, 1], ALU.add))
                ranks(gsc[:, :, :], E // 2, rank[:, :, 0:E // 2])
                link(dve.tensor_scalar(gsc[:, :, :], rank[:, :, 0:E // 2], 2.0, None, ALU.is_lt))
                link(dve.tensor_tensor(two, two, gsc[:, :, :].unsqueeze(3).broadcast_to([P, T, E // 2, 2]), ALU.mult))

            def mix_experts(b):
                ranks(lg[:, :, :], E, rank[:, :, :])
                link(dve.scalar_tensor_tensor(out=ex[:, :, :], in0=rank[:, :, :], scalar=4.0, in1=ex[:, :, :],
                                              op0=ALU.is_lt, op1=ALU.mult))
                link(dve.tensor_reduce(t4[:, :], ex[:, :, :], AX.X, ALU.add))
                link(dve.tensor_scalar(t4[:, :], t4[:, :], 1e-20, None, ALU.add))
                link(dve.reciprocal(t4[:, :], t4[:, :]))
                at = b % 2 * HP
                dve.scalar_tensor_tensor(out=gpad[:, :, at:at + E], in0=ex[:, :, :], scalar=ROUTED_SCALE,
                                         in1=t4[:, :].unsqueeze(2).broadcast_to([P, T, E]),
                                         op0=ALU.mult, op1=ALU.mult).then_inc(c3_sb, 1)

            def mix_gates(b):
                dve.wait_ge(c3h_sb, b + 1)
                at = b % 2 * HP
                dve.tensor_tensor(cwT[at + 32:at + 32 + E, b // 2, :], ps[at:at + E, RB, :],
                                  cwT[at:at + E, b // 2, :].bitcast(F32),
                                  ALU.subtract).then_inc(c3l_sb, 1)

            def mix_pair(i):
                b, a = divmod(i, PA)
                h = hT[:, b % 2 * PA + a, :]
                dve.wait_ge(sg_sb, i + 1)
                dve.wait_ge(u_ps, i + 1)
                if b >= 2:
                    dve.wait_ge(y3_ps, b - 1)
                dve.tensor_tensor(h, sg[:, i % 2, :], ps[:, U3 + i % 2, :], ALU.mult).then_inc(su_sb, 1)

            def mix_residual(b):
                dve.wait_ge(y3_ps, b + 1)
                xb = X[:, T * b:T * (b + 1), :]
                dve.scalar_tensor_tensor(out=xb, in0=ps[:, Y3 + b % 2, :].rearrange("p (t n) -> p t n", t=T),
                                         scalar=tg[:, 3:4], in1=xb, op0=ALU.mult, op1=ALU.add).then_inc(x_out, 1)

            def combined_norm(b):
                dve.wait_ge(combined, b)
                norm(T, lambda t: xn[:, T * b + t, :], lambda t: X[:, T * b + t, :]).then_inc(xn_ready, 1)

            def combine_first():
                x = lambda t: X[:, t, :]
                for t in range(T):
                    dve.wait_ge(first_gathered[t], 16 * 2)
                    for y, w in ((y1, w_first), (y2, w_second)):
                        link(dve.scalar_tensor_tensor(out=x(t), in0=y[:, t, :], scalar=w[:, 0, t:t + 1], in1=x(t),
                                                      op0=ALU.mult, op1=ALU.add))
                    ins = dve.bn_stats(st6w[:, t, :], x(t))
                link(ins)
                from_stats(T)
                rsqrt(T)
                scaled(T, lambda t: xn[:, t, :], x).then_inc(xn_ready, 1)

            def prepare_layer_1():
                dve.wait_ge(wt_ps, 1)
                link(dve.tensor_copy(wT[:, :, :], ps[:, F + 2, :].rearrange("p (i n) -> p i n", i=4)))
                dve.tensor_copy(wp[:, 1, :], wT[:, 3, :])
                cols_of = lambda i: lambda g: wT[:, i, GW * g:GW * (g + 1)].rearrange("p (h d) -> p h d", h=HG)
                stack(1, cols_of(1), cols_of(0)).then_inc(prep_sb, 1)
                dve.tensor_copy(wv[:, 1, :], wT[:, 2, :]).then_inc(wv_sb, 1)

            def attention(l):
                s0 = l * B
                v_mask(s0)
                if l == 0:
                    input_norms(1, 1)
                for g in range(G):
                    maxima(s0, g)
                if l == 0:
                    input_norms(2, 2)
                else:
                    combined_norm(1)
                v_mask(s0 + 1)

                for s in range(s0, s0 + B):
                    n, more, prev = s + 1, s + 1 < s0 + B, s > s0
                    p = s - s0 - 1
                    if more:
                        maxima(n, 0)
                        maxima(n, 1)
                    if l == 1 and s >= s0 + 2:
                        mix_gates(s - s0 - 2)
                    if more:
                        maxima(n, 2)
                        maxima(n, 3)
                    if l == 0:
                        if prev:
                            route_choice(p)
                        reciprocals(s)
                        if prev:
                            route_rows(p)
                        normalise(s)
                        if s + 2 < s0 + B:
                            v_mask(s + 2)
                        if not prev:
                            b1_copy(0)
                        residual(s)
                        route_norms(s)
                        if s == B - 2:
                            prepare_layer_1()
                    else:
                        if s + 2 < s0 + B:
                            combined_norm(s + 2 - s0)
                        reciprocals(s)
                        if prev:
                            mix_logits(p)
                        normalise(s)
                        if s + 2 < s0 + B:
                            v_mask(s + 2)
                        residual(s)
                        if more:
                            if prev:
                                mix_choice(p)
                                mix_experts(p)
                            mix_norm(s - s0)

            attention(0)

            lower_keys(1)
            route_choice(B - 1)
            route_rows(B - 1)
            b1_copy(1)
            dve.wait_ge(count_ps, 1)
            link(dve.tensor_copy(count[:, :], ps[:, RB, 0:E]))
            dve.tensor_tensor(tailI[:, :], count[:, :], region[:, :], ALU.add)
            link(dve.tensor_scalar(tilesI[:, :], count[:, :], 1.0 / P, (P - 1) / P - 0.498, ALU.mult, ALU.add))
            link(dve.tensor_copy(tiles[:, :], tilesI[:, :]))
            link(dve.tensor_tensor(sumtri[:, :, :], tri[E][:, 0, :, :], tiles[:, :].unsqueeze(1).broadcast_to([P, E, E]), ALU.mult))
            link(dve.tensor_reduce(begin[:, :], sumtri[:, :, :], AX.X, ALU.add))
            link(dve.tensor_tensor(end[:, :], begin[:, :], tiles[:, :], ALU.add))
            k = [P, NT, E]
            link(dve.tensor_tensor(past[:, :, :], end[:, :].unsqueeze(1).broadcast_to(k),
                                   tileno[:, :].unsqueeze(2).broadcast_to(k), ALU.is_le))
            link(dve.tensor_reduce(eT[:, :], past[:, :, :], AX.X, ALU.add))
            link(dve.tensor_tensor(past[:, :, :], past[:, :, :], tiles[:, :].unsqueeze(1).broadcast_to(k), ALU.mult))
            link(dve.tensor_reduce(sT[:, :], past[:, :, :], AX.X, ALU.add))
            link(dve.tensor_tensor(sT[:, :], tileno[:, :], sT[:, :], ALU.subtract))
            link(dve.tensor_scalar(sT[:, :], sT[:, :], float(P), None, ALU.mult))
            link(dve.scalar_tensor_tensor(out=sT[:, :], in0=eT[:, :], scalar=float(R), in1=sT[:, :], op0=ALU.mult, op1=ALU.add))
            dve.tensor_scalar(expertI[:, :], eT[:, :], float(E - 1), None, ALU.min)
            dve.tensor_scalar(offsetI[:, :], sT[:, :], float(E * R), None, ALU.min).then_inc(table_sb, 1)
            dve.wait_ge(table_sb, 1)

            def weights(i, ring):
                if not isinstance(i, int) or i >= 4:
                    dve.wait_ge(yo_sb, i - 3)
                e = dve.value_load(expertI[0:1, bass.ds(i, 1)], min_val=0, max_val=E - 1)
                dve.tensor_copy(wcur[:, ring, :], w12[:, bass.ds(e, 1), :].rearrange("p o w -> p (o w)")).then_inc(wc_sb, 1)

            def tile_x(i, par):
                dve.wait_ge(t_ps, i + 1)
                if not isinstance(i, int) or i >= 2:
                    dve.wait_ge(h_ps, i - 1)
                dve.tensor_copy(xgT[:, par, :], ps[:, TX + par, 0:P]).then_inc(xg_sb, 1)

            def tile_out(i, par, ring, turn):
                dve.wait_ge(y_ps, i + 1)
                if not isinstance(turn, int) or turn > 0:
                    dve.wait_ge(y_st[ring], turn * 16)
                dve.tensor_tensor(yo[:, ring, :], ps[:, YB + par, 0:P], wcur[:, ring, B2_AT:B2_AT + P],
                                  ALU.add).then_inc(yo_sb, 1)

            dve.wait_ge(w1_scaled, E)
            dve.wait_ge(b1_sb, 2)
            dve.wait_ge(w2_in, 16 * E)
            dve.wait_ge(b2_in, 16)
            for i in range(3):
                weights(i, i)
            tile_x(0, 0)
            tile_x(1, 1)
            link(dve.scalar_tensor_tensor(out=begin[:, :], in0=begin[:, :], scalar=float(P), in1=region[:, :],
                                          op0=ALU.mult, op1=ALU.subtract))
            k = [P, B * T, E]
            flat = lambda a: a[:, :, :, :].rearrange("p b t e -> p (b t) e")
            link(dve.tensor_tensor(flat(place), flat(place), begin[:, :].unsqueeze(1).broadcast_to(k), ALU.add))
            link(dve.tensor_tensor(flat(wide), flat(first), flat(place), ALU.mult))
            link(dve.tensor_reduce(getF[:, 0, :], flat(wide), AX.X, ALU.add))
            link(dve.tensor_tensor(flat(wide), flat(second), flat(place), ALU.mult))
            link(dve.tensor_reduce(getF[:, 1, :], flat(wide), AX.X, ALU.add))
            dve.tensor_copy(getI[:, :, :], getF[:, :, :]).then_inc(get_sb, 1)
            with dve.Fori(0, (NT - 3) // 4) as k:
                for u in range(1, 5):
                    tile_x(k * 4 + (u + 1), (u + 1) % 2)
                    weights(k * 4 + (u + 2), (u + 2) % 4)
                    tile_out(k * 4 + (u - 1), (u - 1) % 2, (u - 1) % 4, k + (u - 1) // 4)
            i = NT - 2
            tile_x(i + 1, (i + 1) % 2)
            for i in range(NT - 3, NT):
                tile_out(i, i % 2, i % 4, i // 4)
            dve.wait_ge(yo_sb, NT)
            combine_first()
            attention(1)
            for i in range(B * PA):
                mix_pair(i)
                if i == 1:
                    mix_norm(B - 1)
                if i == 2:
                    mix_choice(B - 2)
                if i == 3:
                    mix_experts(B - 2)
                if i == 5:
                    mix_gates(B - 2)
                if i == 7:
                    mix_logits(B - 1)
                if i == 8:
                    mix_choice(B - 1)
                if i == 10:
                    mix_experts(B - 1)
                if i == 12:
                    mix_gates(B - 1)
                if i > PA and i % PA == 1:
                    mix_residual(i // PA - 1)
            for half in range(2):
                span = slice(half * T // 2, (half + 1) * T // 2)
                bank = Y3 + (B - 1 + half) % 2
                xb = X[:, T * (B - 1) + span.start:T * (B - 1) + span.stop, :]
                dve.wait_ge(y3_ps, B + half)
                dve.scalar_tensor_tensor(out=xb, in0=ps[:, bank, P * span.start:P * span.stop].rearrange("p (t n) -> p t n", n=P),
                                         scalar=tg[:, 3:4], in1=xb, op0=ALU.mult, op1=ALU.add).then_inc(x_out, 1)


_INS = ["x", "ctx_1024", "g_xattn", "g_ffn", "L0_xattn_Wq", "L0_xattn_bq", "L0_xattn_Wkv", "L0_xattn_bkv",
        "L0_xattn_Wp", "L0_xattn_bp", "L0_ffn_router_W", "L0_ffn_router_b", "L0_ffn_ln_g", "L0_ffn_ln_b",
        "L0_ffn_W1", "L0_ffn_b1", "L0_ffn_W2", "L0_ffn_b2", "L1_xattn_wq", "L1_xattn_bq", "L1_xattn_wk",
        "L1_xattn_bk", "L1_xattn_wv", "L1_xattn_bv", "L1_xattn_wo", "L1_xattn_bo", "L1_ffn_gate_w",
        "L1_ffn_correction_bias", "L1_ffn_Wg", "L1_ffn_Wu", "L1_ffn_Wd", "L1_ffn_Wg_s", "L1_ffn_Wu_s",
        "L1_ffn_Wd_s"]


def kernel(**inputs):
    import numpy as np
    import concourse.bacc as bacc
    from concourse.bass_utils import run_bass_kernel_spmd

    nc = bacc.Bacc("TRN2", target_bir_lowering=False, num_devices=1)
    arrays, aps = {}, {}
    for name in _INS:
        a = np.ascontiguousarray(inputs[name])
        arrays[f"in_{name}"] = a
        aps[name] = nc.dram_tensor(f"in_{name}", a.shape, mybir.dt.from_np(a.dtype), kind="ExternalInput").ap()
    out = nc.dram_tensor("out", inputs["x"].shape, F32, kind="ExternalOutput").ap()
    build(nc, aps, out)
    r = run_bass_kernel_spmd(nc, [arrays], core_ids=[0])
    return r.results[0]["out"]
```
